# Optimizing a Trainium2 kernel written in Bass

```python
import numpy as np
import jax
import jax.numpy as jnp

def _softmax(x, axis=-1):
    return jax.nn.softmax(x, axis=axis)

def _gelu(x):
    return jax.nn.gelu(x, approximate=True)

def _silu(x):
    return jax.nn.silu(x)

def _sigmoid(x):
    return jax.nn.sigmoid(x)

def _layernorm(x, axis=-1, eps=1e-05):
    m = jnp.mean(x, axis=axis, keepdims=True)
    v = jnp.var(x, axis=axis, keepdims=True)
    return (x - m) / jnp.sqrt(v + eps)

def _scatter_add(tgt, idx, src, axis=0):
    return tgt.at[idx].add(src)

def _segment_sum(src, seg, n):
    return jax.ops.segment_sum(src, seg, n)
kernel_name = 'mk_adj_ffn_d4_adj_r2_1646d9'

def setup_inputs(seed: int=0):
    np.random.seed(seed)
    _w = jnp.asarray

    def _rec_inputs():
        import jax
        import jax.numpy as jnp
        _gk = jax.random.key(seed)
        x = -0.0005207 + 1.001 * jax.random.normal(jax.random.fold_in(_gk, 1), (16, 512, 128), jnp.float32)
        _w = (1.0 + jnp.arange(512, dtype=jnp.float32)) ** (-0.5)
        _w = _w / _w.mean()
        _pij = jnp.clip(0.03125 * _w[:, None] * _w[None, :], 0.0, 1.0)
        _a = jax.random.uniform(jax.random.fold_in(_gk, 2), (16, 512, 512)) < _pij
        _a = jnp.logical_or(_a, jnp.eye(512, dtype=bool))
        adj = _a.astype(jnp.int32)
        return (x, adj)
    x, adj = _rec_inputs()

    def _L0_gnn_setup():
        import jax, jax.numpy as jnp
        import numpy as np
        B, N, D, H = (4, 1024, 128, 8)
        HD = D // H
        DFF = 4 * D
        EPS = 1e-05

        def layer_norm(x, gamma, beta):
            mu = jnp.mean(x, axis=-1, keepdims=True)
            var = jnp.mean(jnp.square(x - mu), axis=-1, keepdims=True)
            return (x - mu) * jax.lax.rsqrt(var + EPS) * gamma + beta
        key = jax.random.key(seed)
        ks = jax.random.split(key, 10)
        x = jax.random.normal(ks[0], (B, N, D), dtype=jnp.float32)
        adj = jax.random.randint(ks[1], (B, N, N), 0, 2).astype(jnp.int32)
        idx = jnp.arange(N)
        adj = adj.at[:, idx, idx].set(1)
        gamma1 = 1.0 + 0.02 * jax.random.normal(ks[2], (D,), dtype=jnp.float32)
        beta1 = 0.02 * jax.random.normal(ks[3], (D,), dtype=jnp.float32)
        gamma2 = 1.0 + 0.02 * jax.random.normal(ks[4], (D,), dtype=jnp.float32)
        beta2 = 0.02 * jax.random.normal(ks[5], (D,), dtype=jnp.float32)
        W1 = 0.02 * jax.random.normal(ks[6], (D, DFF), dtype=jnp.float32)
        b1 = 0.01 * jax.random.normal(ks[7], (DFF,), dtype=jnp.float32)
        W2 = 0.02 * jax.random.normal(ks[8], (DFF, D), dtype=jnp.float32)
        b2 = 0.01 * jax.random.normal(ks[9], (D,), dtype=jnp.float32)
        return {'x': x, 'adj_matrix': adj, 'gamma1': gamma1, 'beta1': beta1, 'gamma2': gamma2, 'beta2': beta2, 'W1': W1, 'b1': b1, 'W2': W2, 'b2': b2}
    _L0_gnn_all = _L0_gnn_setup()
    _L0_gnn_in = {k: v for k, v in _L0_gnn_all.items() if k in ('gamma1', 'beta1', 'gamma2', 'beta2', 'W1', 'b1', 'W2', 'b2')}
    del _L0_gnn_all

    def _L0_ffn_setup():
        import jax, jax.numpy as jnp
        import numpy as np
        B, N, D = (16, 2048, 128)
        NUM_EXPERTS, TOP_K, HEADS = (4, 2, 4)
        N_EDGES = 524288
        LN_EPS = 1e-05

        def _layernorm(x, g, b):
            mu = x.mean(-1, keepdims=True)
            var = ((x - mu) ** 2).mean(-1, keepdims=True)
            return (x - mu) * jax.lax.rsqrt(var + LN_EPS) * g + b

        def _forward(x, edge_index, W_gat, att_src, att_dst, b_gat, ln_gamma, ln_beta, W1, b1, W2, b2):
            Bc, Nc, Dc = x.shape
            M = Bc * Nc
            x_flat = x.reshape(M, Dc)
            h = (x_flat @ W_gat).reshape(M, HEADS, NUM_EXPERTS)
            loops = jnp.arange(M, dtype=edge_index.dtype)
            src = jnp.concatenate([edge_index[0], loops])
            dst = jnp.concatenate([edge_index[1], loops])
            a_src = (h * att_src).sum(-1)
            a_dst = (h * att_dst).sum(-1)
            e = jax.nn.leaky_relu(a_src[src] + a_dst[dst], negative_slope=0.2)
            e_max = jax.ops.segment_max(e, dst, num_segments=M)
            ee = jnp.exp(e - e_max[dst])
            denom = jax.ops.segment_sum(ee, dst, num_segments=M)
            alpha = ee / (denom[dst] + 1e-16)
            msg = h[src] * alpha[:, :, None]
            agg = jax.ops.segment_sum(msg, dst, num_segments=M).reshape(M, HEADS * NUM_EXPERTS) + b_gat
            scores = _layernorm(agg, ln_gamma, ln_beta).reshape(M, HEADS, NUM_EXPERTS).mean(1)
            scores = scores.reshape(Bc, Nc, NUM_EXPERTS)
            topk_s, topk_i = jax.lax.top_k(scores, TOP_K)
            w = jax.nn.softmax(topk_s, axis=-1)
            out = jnp.zeros_like(x)
            for ei in range(NUM_EXPERTS):
                g = jnp.where(topk_i == ei, w, 0.0).sum(-1)
                hh = jax.nn.gelu(x @ W1[ei] + b1[ei], approximate=False)
                out = out + g[..., None] * (hh @ W2[ei] + b2[ei])
            return out
        key = jax.random.key(seed)
        ks = jax.random.split(key, 8)
        s = 0.05
        return {'x': jax.random.normal(ks[0], (B, N, D), jnp.float32), 'W_gat': jax.random.normal(ks[1], (D, HEADS * NUM_EXPERTS), jnp.float32) * s, 'att_src': jax.random.normal(ks[2], (HEADS, NUM_EXPERTS), jnp.float32) * s, 'att_dst': jax.random.normal(ks[3], (HEADS, NUM_EXPERTS), jnp.float32) * s, 'b_gat': jnp.zeros((HEADS * NUM_EXPERTS,), jnp.float32), 'ln_gamma': jnp.ones((HEADS * NUM_EXPERTS,), jnp.float32), 'ln_beta': jnp.zeros((HEADS * NUM_EXPERTS,), jnp.float32), 'W1': jax.random.normal(ks[4], (NUM_EXPERTS, D, 2 * D), jnp.float32) * s, 'b1': jnp.zeros((NUM_EXPERTS, 2 * D), jnp.float32), 'W2': jax.random.normal(ks[5], (NUM_EXPERTS, 2 * D, D), jnp.float32) * s, 'b2': jnp.zeros((NUM_EXPERTS, D), jnp.float32), 'edge_index': jax.random.randint(ks[6], (2, N_EDGES), 0, B * N, jnp.int32)}
    _L0_ffn_all = _L0_ffn_setup()
    _L0_ffn_in = {k: v for k, v in _L0_ffn_all.items() if k in ('W_gat', 'att_src', 'att_dst', 'b_gat', 'ln_gamma', 'ln_beta', 'W1', 'b1', 'W2', 'b2', 'edge_index')}
    del _L0_ffn_all

    def _L1_gnn_setup():
        import jax, jax.numpy as jnp
        import numpy as np
        B, N, F_IN, F_OUT = (8, 1024, 128, 128)
        ALPHA = 0.2
        NEG_BIG = -9000000000000000.0
        key = jax.random.key(seed)
        k1, k2, k3, k4 = jax.random.split(key, 4)
        x = jax.random.normal(k1, (B, N, F_IN), dtype=jnp.float32)
        adj = jax.random.randint(k2, (B, N, N), 0, 2, dtype=jnp.int32)
        gain = 1.414
        lim_W = gain * np.sqrt(6.0 / (F_IN + F_OUT))
        W = jax.random.uniform(k3, (F_IN, F_OUT), dtype=jnp.float32, minval=-lim_W, maxval=lim_W)
        lim_a = gain * np.sqrt(6.0 / (2 * F_OUT + 1))
        a = jax.random.uniform(k4, (2 * F_OUT, 1), dtype=jnp.float32, minval=-lim_a, maxval=lim_a)
        return {'x': x, 'adj': adj, 'W': W, 'a': a}
    _L1_gnn_all = _L1_gnn_setup()
    _L1_gnn_in = {k: v for k, v in _L1_gnn_all.items() if k in ('W', 'a')}
    del _L1_gnn_all

    def _L1_ffn_setup():
        import jax, jax.numpy as jnp
        import numpy as np
        B, S, D_MODEL, FFN, P = (8, 2048, 128, 512, 8)
        BLK = 128
        key = jax.random.key(seed)
        ks = jax.random.split(key, 12)
        x = jax.random.normal(ks[0], (B, S, D_MODEL), jnp.float32)
        Wt = 0.05 * jax.random.normal(ks[1], (FFN, D_MODEL), jnp.float32)
        bt = 0.05 * jax.random.normal(ks[2], (FFN,), jnp.float32)
        sl_cvx = 1.0 + 0.1 * jax.random.normal(ks[3], (FFN, P), jnp.float32)
        of_cvx = 0.1 * jax.random.normal(ks[4], (FFN, P), jnp.float32)
        sl_ccv = 1.0 + 0.1 * jax.random.normal(ks[5], (FFN, P), jnp.float32)
        of_ccv = 0.1 * jax.random.normal(ks[6], (FFN, P), jnp.float32)
        alpha = jnp.zeros((FFN,), jnp.float32)
        Wc = jax.random.normal(ks[7], (D_MODEL, FFN), jnp.float32) / np.sqrt(D_MODEL)
        bc = jnp.zeros((FFN,), jnp.float32)
        Wg = 0.01 * jax.random.normal(ks[8], (D_MODEL, FFN), jnp.float32)
        bg = 2.0 * jnp.ones((FFN,), jnp.float32)
        Wd = jax.random.normal(ks[9], (FFN, D_MODEL), jnp.float32) / np.sqrt(FFN)
        bd = jnp.zeros((D_MODEL,), jnp.float32)
        return {'x': x, 'Wt': Wt, 'bt': bt, 'sl_cvx': sl_cvx, 'of_cvx': of_cvx, 'sl_ccv': sl_ccv, 'of_ccv': of_ccv, 'alpha': alpha, 'Wc': Wc, 'bc': bc, 'Wg': Wg, 'bg': bg, 'Wd': Wd, 'bd': bd}
    _L1_ffn_all = _L1_ffn_setup()
    _L1_ffn_in = {k: v for k, v in _L1_ffn_all.items() if k in ('Wt', 'bt', 'sl_cvx', 'of_cvx', 'sl_ccv', 'of_ccv', 'alpha', 'Wc', 'bc', 'Wg', 'bg', 'Wd', 'bd')}
    del _L1_ffn_all

    def _L2_gnn_setup():
        import jax, jax.numpy as jnp
        import numpy as np
        B, N, F = (4, 1024, 128)
        NEG = -9000000000000000.0
        key = jax.random.key(seed)
        k1, k2, k3, k4 = jax.random.split(key, 4)
        x = jax.random.normal(k1, (B, N, F), dtype=jnp.float32)
        adj = jax.random.randint(k2, (B, N, N), 0, 2, dtype=jnp.int32)
        W = jax.random.normal(k3, (F, F), dtype=jnp.float32) * 0.07
        a = jax.random.normal(k4, (2 * F, 1), dtype=jnp.float32) * 0.07
        return {'x': x, 'adj': adj, 'W': W, 'a': a}
    _L2_gnn_all = _L2_gnn_setup()
    _L2_gnn_in = {k: v for k, v in _L2_gnn_all.items() if k in ('W', 'a')}
    del _L2_gnn_all

    def _L2_ffn_setup():
        import jax, jax.numpy as jnp
        import numpy as np
        E, D, H, TOP_K = (6, 128, 128, 2)
        ROUTER_H = D // 2
        key = jax.random.key(seed)
        ks = jax.random.split(key, 12)
        s = 1.0 / np.sqrt(D)
        sh = 1.0 / np.sqrt(H)
        sr = 1.0 / np.sqrt(ROUTER_H)
        return {'features': jax.random.normal(ks[0], (8, 2048, D), dtype=jnp.float32), 'router_w1': jax.random.uniform(ks[1], (D, ROUTER_H), jnp.float32, -s, s), 'router_b1': jnp.zeros((ROUTER_H,), jnp.float32), 'router_w2': jax.random.uniform(ks[2], (ROUTER_H, E), jnp.float32, -sr, sr), 'router_b2': jnp.zeros((E,), jnp.float32), 'expert_w1': jax.random.uniform(ks[3], (E, D, H), jnp.float32, -s, s), 'expert_b1': jnp.zeros((E, H), jnp.float32), 'expert_w2': jax.random.uniform(ks[4], (E, H, H), jnp.float32, -sh, sh), 'expert_b2': jnp.zeros((E, H), jnp.float32), 'expert_w3': jax.random.uniform(ks[5], (E, H, D), jnp.float32, -sh, sh), 'expert_b3': jnp.zeros((E, D), jnp.float32)}
    _L2_ffn_all = _L2_ffn_setup()
    _L2_ffn_in = {k: v for k, v in _L2_ffn_all.items() if k in ('router_w1', 'router_b1', 'router_w2', 'router_b2', 'expert_w1', 'expert_b1', 'expert_w2', 'expert_b2', 'expert_w3', 'expert_b3')}
    del _L2_ffn_all

    def _L3_gnn_setup():
        import jax, jax.numpy as jnp
        import numpy as np
        IN_F = 128
        OUT_F = 128
        B, N = (8, 1024)
        key = jax.random.key(seed)
        k1, k2, k3, k4, k5 = jax.random.split(key, 5)
        x = jax.random.normal(k1, (B, N, IN_F), dtype=jnp.float32)
        adj = jax.random.randint(k2, (B, N, N), 0, 2, dtype=jnp.int32)
        diag = jnp.arange(N)
        adj = adj.at[:, diag, diag].set(1)
        W = jax.random.normal(k3, (IN_F, OUT_F), dtype=jnp.float32) / np.sqrt(IN_F)
        a_src = jax.random.normal(k4, (OUT_F,), dtype=jnp.float32) / np.sqrt(OUT_F)
        a_dst = jax.random.normal(k5, (OUT_F,), dtype=jnp.float32) / np.sqrt(OUT_F)
        return {'x': x, 'adj': adj, 'W': W, 'a_src': a_src, 'a_dst': a_dst}
    _L3_gnn_all = _L3_gnn_setup()
    _L3_gnn_in = {k: v for k, v in _L3_gnn_all.items() if k in ('W', 'a_src', 'a_dst')}
    del _L3_gnn_all

    def _L3_ffn_setup():
        import jax, jax.numpy as jnp
        import numpy as np
        DIM = 128
        HEADS = 8
        NUM_KEYS = 128
        NUM_KV = NUM_KEYS ** 2
        PK_TOPK = 16
        FINAL_TOPK = 16
        DIM_KEY = DIM // 2
        P = 2

        def _pk(x, Wq_pk, pk_keys):
            b, n, _ = x.shape
            q = (x @ Wq_pk).reshape(b, n, P, HEADS, DIM_KEY).transpose(2, 0, 1, 3, 4)
            sim = jnp.einsum('pbnhd,pkhd->pbnhk', q, pk_keys)
            scores, idx = jax.lax.top_k(sim, PK_TOPK)
            idx0 = idx[0]
            idx1 = idx[1] * NUM_KEYS
            index = (idx0[..., :, None] + idx1[..., None, :]).reshape(b, n, HEADS, PK_TOPK * PK_TOPK)
            score = (scores[0][..., :, None] + scores[1][..., None, :]).reshape(b, n, HEADS, PK_TOPK * PK_TOPK)
            final_scores, pk_idx = jax.lax.top_k(score, FINAL_TOPK)
            final_indices = jnp.take_along_axis(index, pk_idx, axis=-1)
            final_scores = jax.nn.softmax(final_scores, axis=-1)
            return (final_scores, final_indices)
        key = jax.random.key(seed)
        ks = jax.random.split(key, 7)
        b, n = (2, 512)
        std = 0.02
        x = jax.random.normal(ks[0], (b, n, DIM), dtype=jnp.float32)
        Wq_pk = jax.random.normal(ks[1], (DIM, P * HEADS * DIM_KEY), dtype=jnp.float32) * std
        pk_keys = jax.random.normal(ks[2], (P, NUM_KEYS, HEADS, DIM_KEY), dtype=jnp.float32) * std
        Wq = jax.random.normal(ks[3], (DIM, HEADS * DIM), dtype=jnp.float32) * std
        keys_table = jax.random.normal(ks[4], (NUM_KV * HEADS, DIM), dtype=jnp.float32) * std
        values_table = jax.random.normal(ks[5], (NUM_KV * HEADS, DIM), dtype=jnp.float32) * std
        Wo = jax.random.normal(ks[6], (DIM * HEADS, DIM), dtype=jnp.float32) * std
        return {'x': x, 'Wq_pk': Wq_pk, 'pk_keys': pk_keys, 'Wq': Wq, 'keys_table': keys_table, 'values_table': values_table, 'Wo': Wo}
    _L3_ffn_all = _L3_ffn_setup()
    _L3_ffn_in = {k: v for k, v in _L3_ffn_all.items() if k in ('Wq_pk', 'pk_keys', 'Wq', 'keys_table', 'values_table', 'Wo')}
    del _L3_ffn_all
    return {'x': x, 'adj': adj, 'L0_gnn_gamma1': _L0_gnn_in['gamma1'], 'L0_gnn_beta1': _L0_gnn_in['beta1'], 'L0_gnn_gamma2': _L0_gnn_in['gamma2'], 'L0_gnn_beta2': _L0_gnn_in['beta2'], 'L0_gnn_W1': _L0_gnn_in['W1'], 'L0_gnn_b1': _L0_gnn_in['b1'], 'L0_gnn_W2': _L0_gnn_in['W2'], 'L0_gnn_b2': _L0_gnn_in['b2'], 'L0_ffn_W_gat': _L0_ffn_in['W_gat'], 'L0_ffn_att_src': _L0_ffn_in['att_src'], 'L0_ffn_att_dst': _L0_ffn_in['att_dst'], 'L0_ffn_b_gat': _L0_ffn_in['b_gat'], 'L0_ffn_ln_gamma': _L0_ffn_in['ln_gamma'], 'L0_ffn_ln_beta': _L0_ffn_in['ln_beta'], 'L0_ffn_W1': _L0_ffn_in['W1'], 'L0_ffn_b1': _L0_ffn_in['b1'], 'L0_ffn_W2': _L0_ffn_in['W2'], 'L0_ffn_b2': _L0_ffn_in['b2'], 'L0_ffn_edge_index': _L0_ffn_in['edge_index'], 'L1_gnn_W': _L1_gnn_in['W'], 'L1_gnn_a': _L1_gnn_in['a'], 'L1_ffn_Wt': _L1_ffn_in['Wt'], 'L1_ffn_bt': _L1_ffn_in['bt'], 'L1_ffn_sl_cvx': _L1_ffn_in['sl_cvx'], 'L1_ffn_of_cvx': _L1_ffn_in['of_cvx'], 'L1_ffn_sl_ccv': _L1_ffn_in['sl_ccv'], 'L1_ffn_of_ccv': _L1_ffn_in['of_ccv'], 'L1_ffn_alpha': _L1_ffn_in['alpha'], 'L1_ffn_Wc': _L1_ffn_in['Wc'], 'L1_ffn_bc': _L1_ffn_in['bc'], 'L1_ffn_Wg': _L1_ffn_in['Wg'], 'L1_ffn_bg': _L1_ffn_in['bg'], 'L1_ffn_Wd': _L1_ffn_in['Wd'], 'L1_ffn_bd': _L1_ffn_in['bd'], 'L2_gnn_W': _L2_gnn_in['W'], 'L2_gnn_a': _L2_gnn_in['a'], 'L2_ffn_router_w1': _L2_ffn_in['router_w1'], 'L2_ffn_router_b1': _L2_ffn_in['router_b1'], 'L2_ffn_router_w2': _L2_ffn_in['router_w2'], 'L2_ffn_router_b2': _L2_ffn_in['router_b2'], 'L2_ffn_expert_w1': _L2_ffn_in['expert_w1'], 'L2_ffn_expert_b1': _L2_ffn_in['expert_b1'], 'L2_ffn_expert_w2': _L2_ffn_in['expert_w2'], 'L2_ffn_expert_b2': _L2_ffn_in['expert_b2'], 'L2_ffn_expert_w3': _L2_ffn_in['expert_w3'], 'L2_ffn_expert_b3': _L2_ffn_in['expert_b3'], 'L3_gnn_W': _L3_gnn_in['W'], 'L3_gnn_a_src': _L3_gnn_in['a_src'], 'L3_gnn_a_dst': _L3_gnn_in['a_dst'], 'L3_ffn_Wq_pk': _L3_ffn_in['Wq_pk'], 'L3_ffn_pk_keys': _L3_ffn_in['pk_keys'], 'L3_ffn_Wq': _L3_ffn_in['Wq'], 'L3_ffn_keys_table': _L3_ffn_in['keys_table'], 'L3_ffn_values_table': _L3_ffn_in['values_table'], 'L3_ffn_Wo': _L3_ffn_in['Wo']}

def reference(x, adj, L0_gnn_gamma1, L0_gnn_beta1, L0_gnn_gamma2, L0_gnn_beta2, L0_gnn_W1, L0_gnn_b1, L0_gnn_W2, L0_gnn_b2, L0_ffn_W_gat, L0_ffn_att_src, L0_ffn_att_dst, L0_ffn_b_gat, L0_ffn_ln_gamma, L0_ffn_ln_beta, L0_ffn_W1, L0_ffn_b1, L0_ffn_W2, L0_ffn_b2, L0_ffn_edge_index, L1_gnn_W, L1_gnn_a, L1_ffn_Wt, L1_ffn_bt, L1_ffn_sl_cvx, L1_ffn_of_cvx, L1_ffn_sl_ccv, L1_ffn_of_ccv, L1_ffn_alpha, L1_ffn_Wc, L1_ffn_bc, L1_ffn_Wg, L1_ffn_bg, L1_ffn_Wd, L1_ffn_bd, L2_gnn_W, L2_gnn_a, L2_ffn_router_w1, L2_ffn_router_b1, L2_ffn_router_w2, L2_ffn_router_b2, L2_ffn_expert_w1, L2_ffn_expert_b1, L2_ffn_expert_w2, L2_ffn_expert_b2, L2_ffn_expert_w3, L2_ffn_expert_b3, L3_gnn_W, L3_gnn_a_src, L3_gnn_a_dst, L3_ffn_Wq_pk, L3_ffn_pk_keys, L3_ffn_Wq, L3_ffn_keys_table, L3_ffn_values_table, L3_ffn_Wo):
    import jax
    import jax.numpy as jnp

    def _L0_gnn_ref(x, adj_matrix, gamma1, beta1, gamma2, beta2, W1, b1, W2, b2):
        import jax, jax.numpy as jnp
        import numpy as np
        B, N, D, H = (4, 1024, 128, 8)
        HD = D // H
        DFF = 4 * D
        EPS = 1e-05

        def layer_norm(x, gamma, beta):
            mu = jnp.mean(x, axis=-1, keepdims=True)
            var = jnp.mean(jnp.square(x - mu), axis=-1, keepdims=True)
            return (x - mu) * jax.lax.rsqrt(var + EPS) * gamma + beta
        b_, n_, d_ = x.shape
        normed = layer_norm(x, gamma1, beta1)
        qkv = normed.reshape(b_, n_, H, HD).transpose(0, 2, 1, 3)
        scale = 1.0 / jnp.sqrt(jnp.asarray(HD, dtype=x.dtype))
        scores = jnp.einsum('bhqd,bhkd->bhqk', qkv, qkv) * scale
        mask = adj_matrix[:, None, :, :] > 0
        masked = jnp.where(mask, scores, -jnp.inf)
        attn = jax.nn.softmax(masked, axis=-1)
        out = jnp.einsum('bhqk,bhkd->bhqd', attn, qkv)
        out = out.transpose(0, 2, 1, 3).reshape(b_, n_, d_)
        x = x + out
        y = layer_norm(x, gamma2, beta2)
        mlp = jax.nn.gelu(y @ W1 + b1, approximate=False) @ W2 + b2
        return x + mlp

    def _L0_ffn_ref(x, W_gat, att_src, att_dst, b_gat, ln_gamma, ln_beta, W1, b1, W2, b2, edge_index):
        import jax, jax.numpy as jnp
        import numpy as np
        B, N, D = (16, 2048, 128)
        NUM_EXPERTS, TOP_K, HEADS = (4, 2, 4)
        N_EDGES = 524288
        LN_EPS = 1e-05

        def _layernorm(x, g, b):
            mu = x.mean(-1, keepdims=True)
            var = ((x - mu) ** 2).mean(-1, keepdims=True)
            return (x - mu) * jax.lax.rsqrt(var + LN_EPS) * g + b

        def _forward(x, edge_index, W_gat, att_src, att_dst, b_gat, ln_gamma, ln_beta, W1, b1, W2, b2):
            Bc, Nc, Dc = x.shape
            M = Bc * Nc
            x_flat = x.reshape(M, Dc)
            h = (x_flat @ W_gat).reshape(M, HEADS, NUM_EXPERTS)
            loops = jnp.arange(M, dtype=edge_index.dtype)
            src = jnp.concatenate([edge_index[0], loops])
            dst = jnp.concatenate([edge_index[1], loops])
            a_src = (h * att_src).sum(-1)
            a_dst = (h * att_dst).sum(-1)
            e = jax.nn.leaky_relu(a_src[src] + a_dst[dst], negative_slope=0.2)
            e_max = jax.ops.segment_max(e, dst, num_segments=M)
            ee = jnp.exp(e - e_max[dst])
            denom = jax.ops.segment_sum(ee, dst, num_segments=M)
            alpha = ee / (denom[dst] + 1e-16)
            msg = h[src] * alpha[:, :, None]
            agg = jax.ops.segment_sum(msg, dst, num_segments=M).reshape(M, HEADS * NUM_EXPERTS) + b_gat
            scores = _layernorm(agg, ln_gamma, ln_beta).reshape(M, HEADS, NUM_EXPERTS).mean(1)
            scores = scores.reshape(Bc, Nc, NUM_EXPERTS)
            topk_s, topk_i = jax.lax.top_k(scores, TOP_K)
            w = jax.nn.softmax(topk_s, axis=-1)
            out = jnp.zeros_like(x)
            for ei in range(NUM_EXPERTS):
                g = jnp.where(topk_i == ei, w, 0.0).sum(-1)
                hh = jax.nn.gelu(x @ W1[ei] + b1[ei], approximate=False)
                out = out + g[..., None] * (hh @ W2[ei] + b2[ei])
            return out
        return _forward(x, edge_index, W_gat, att_src, att_dst, b_gat, ln_gamma, ln_beta, W1, b1, W2, b2)

    def _L1_gnn_ref(x, adj, W, a):
        import jax, jax.numpy as jnp
        import numpy as np
        B, N, F_IN, F_OUT = (8, 1024, 128, 128)
        ALPHA = 0.2
        NEG_BIG = -9000000000000000.0
        h = jnp.einsum('bnf,fo->bno', x, W)
        a1 = a[:F_OUT, 0]
        a2 = a[F_OUT:, 0]
        s1 = h @ a1
        s2 = h @ a2
        e = jax.nn.leaky_relu(s1[:, :, None] + s2[:, None, :], negative_slope=ALPHA)
        att = jnp.where(adj > 0, e, jnp.float32(NEG_BIG))
        att = jax.nn.softmax(att, axis=1)
        h_prime = jnp.einsum('bij,bjo->bio', att, h)
        return jax.nn.elu(h_prime)

    def _L1_ffn_ref(x, Wt, bt, sl_cvx, of_cvx, sl_ccv, of_ccv, alpha, Wc, bc, Wg, bg, Wd, bd):
        import jax, jax.numpy as jnp
        import numpy as np
        B, S, D_MODEL, FFN, P = (8, 2048, 128, 512, 8)
        BLK = 128
        Bx, Sx, D = x.shape
        T = Bx * Sx
        xf = x.reshape(T, D)
        xb = xf.reshape(T // BLK, BLK, D)
        s = jax.nn.sigmoid(alpha)

        def blk_fn(xx):
            t = jnp.max(xx[:, None, :] + Wt[None, :, :], axis=-1) + bt
            z = t[:, :, None]
            cvx = jnp.max(z * sl_cvx[None] + of_cvx[None], axis=-1)
            ccv = jnp.min(z * sl_ccv[None] + of_ccv[None], axis=-1)
            return s * cvx + (1.0 - s) * ccv
        trop = jax.lax.map(blk_fn, xb).reshape(T, FFN)
        classical = jax.nn.gelu(xf @ Wc + bc, approximate=False)
        g = jax.nn.sigmoid(xf @ Wg + bg)
        fused = g * trop + (1.0 - g) * classical
        out = fused @ Wd + bd
        return out.reshape(Bx, Sx, D)

    def _L2_gnn_ref(x, adj, W, a):
        import jax, jax.numpy as jnp
        import numpy as np
        B, N, F = (4, 1024, 128)
        NEG = -9000000000000000.0
        h = jnp.einsum('bnf,fg->bng', x, W)
        f_src = h @ a[:F, 0]
        f_dst = h @ a[F:, 0]
        e = jax.nn.relu(f_src[:, :, None] + f_dst[:, None, :])
        att = jnp.where(adj > 0, e, NEG)
        att = jax.nn.softmax(att, axis=2)
        h_prime = jnp.einsum('bnm,bmf->bnf', att, h)
        return jax.nn.elu(h_prime)

    def _L2_ffn_ref(features, router_w1, router_b1, router_w2, router_b2, expert_w1, expert_b1, expert_w2, expert_b2, expert_w3, expert_b3):
        import jax, jax.numpy as jnp
        import numpy as np
        E, D, H, TOP_K = (6, 128, 128, 2)
        ROUTER_H = D // 2
        rh = jax.nn.relu(features @ router_w1 + router_b1)
        expert_logits = jax.nn.softmax(rh @ router_w2 + router_b2, axis=-1)
        top_w, top_i = jax.lax.top_k(expert_logits, TOP_K)
        routing_weights = jax.nn.softmax(top_w, axis=-1)
        h1 = jax.nn.relu(jnp.einsum('bsd,edh->bseh', features, expert_w1) + expert_b1)
        h2 = jax.nn.relu(jnp.einsum('bseh,ehf->bsef', h1, expert_w2) + expert_b2)
        expert_out = jnp.einsum('bsef,efo->bseo', h2, expert_w3) + expert_b3
        sel = jnp.take_along_axis(expert_out, top_i[:, :, :, None], axis=2)
        combined = jnp.sum(sel * routing_weights[..., None], axis=2)
        return combined

    def _L3_gnn_ref(x, adj, W, a_src, a_dst):
        import jax, jax.numpy as jnp
        import numpy as np
        IN_F = 128
        OUT_F = 128
        B, N = (8, 1024)
        h = jnp.einsum('bnf,fo->bno', x, W)
        s = jnp.einsum('bno,o->bn', h, a_src)
        d = jnp.einsum('bno,o->bn', h, a_dst)
        attn = s[:, :, None] + d[:, None, :]
        attn = jnp.where(attn > 0, attn, 0.2 * attn)
        attn = jnp.where(adj == 0, -jnp.inf, attn)
        attn = jax.nn.softmax(attn, axis=-1)
        attn = jnp.nan_to_num(attn, nan=0.0)
        out = jnp.einsum('bij,bjo->bio', attn, h)
        return out

    def _L3_ffn_ref(x, Wq_pk, pk_keys, Wq, keys_table, values_table, Wo):
        import jax, jax.numpy as jnp
        import numpy as np
        DIM = 128
        HEADS = 8
        NUM_KEYS = 128
        NUM_KV = NUM_KEYS ** 2
        PK_TOPK = 16
        FINAL_TOPK = 16
        DIM_KEY = DIM // 2
        P = 2

        def _pk(x, Wq_pk, pk_keys):
            b, n, _ = x.shape
            q = (x @ Wq_pk).reshape(b, n, P, HEADS, DIM_KEY).transpose(2, 0, 1, 3, 4)
            sim = jnp.einsum('pbnhd,pkhd->pbnhk', q, pk_keys)
            scores, idx = jax.lax.top_k(sim, PK_TOPK)
            idx0 = idx[0]
            idx1 = idx[1] * NUM_KEYS
            index = (idx0[..., :, None] + idx1[..., None, :]).reshape(b, n, HEADS, PK_TOPK * PK_TOPK)
            score = (scores[0][..., :, None] + scores[1][..., None, :]).reshape(b, n, HEADS, PK_TOPK * PK_TOPK)
            final_scores, pk_idx = jax.lax.top_k(score, FINAL_TOPK)
            final_indices = jnp.take_along_axis(index, pk_idx, axis=-1)
            final_scores = jax.nn.softmax(final_scores, axis=-1)
            return (final_scores, final_indices)
        b, n, d = x.shape
        q = (x @ Wq).reshape(b, n, HEADS, DIM) * DIM ** (-0.5)
        kv_scores, indices = _pk(x, Wq_pk, pk_keys)
        offsets = jnp.arange(HEADS, dtype=indices.dtype) * NUM_KV
        ind = indices + offsets[None, None, :, None]
        k = jnp.einsum('bnhk,bnhkd->bnhd', kv_scores, keys_table[ind])
        v = jnp.einsum('bnhk,bnhkd->bnhd', kv_scores, values_table[ind])
        sim = jnp.einsum('bihd,bjhd->bhij', q, k)
        neg = -jnp.finfo(sim.dtype).max
        causal = jnp.tril(jnp.ones((n, n), dtype=bool))
        sim = jnp.where(causal, sim, neg)
        attn = jax.nn.softmax(sim, axis=-1)
        out = jnp.einsum('bhij,bjhd->bhid', attn, v)
        out = out.transpose(0, 2, 1, 3).reshape(b, n, HEADS * DIM)
        return out @ Wo
    x = x + _L0_gnn_ref(_layernorm(x, axis=-1), adj, L0_gnn_gamma1, L0_gnn_beta1, L0_gnn_gamma2, L0_gnn_beta2, L0_gnn_W1, L0_gnn_b1, L0_gnn_W2, L0_gnn_b2)
    x = x + _L0_ffn_ref(_layernorm(x, axis=-1), L0_ffn_W_gat, L0_ffn_att_src, L0_ffn_att_dst, L0_ffn_b_gat, L0_ffn_ln_gamma, L0_ffn_ln_beta, L0_ffn_W1, L0_ffn_b1, L0_ffn_W2, L0_ffn_b2, L0_ffn_edge_index)
    x = x + _L1_gnn_ref(_layernorm(x, axis=-1), adj, L1_gnn_W, L1_gnn_a)
    x = x + _L1_ffn_ref(_layernorm(x, axis=-1), L1_ffn_Wt, L1_ffn_bt, L1_ffn_sl_cvx, L1_ffn_of_cvx, L1_ffn_sl_ccv, L1_ffn_of_ccv, L1_ffn_alpha, L1_ffn_Wc, L1_ffn_bc, L1_ffn_Wg, L1_ffn_bg, L1_ffn_Wd, L1_ffn_bd)
    x = x + _L2_gnn_ref(_layernorm(x, axis=-1), adj, L2_gnn_W, L2_gnn_a)
    x = x + _L2_ffn_ref(_layernorm(x, axis=-1), L2_ffn_router_w1, L2_ffn_router_b1, L2_ffn_router_w2, L2_ffn_router_b2, L2_ffn_expert_w1, L2_ffn_expert_b1, L2_ffn_expert_w2, L2_ffn_expert_b2, L2_ffn_expert_w3, L2_ffn_expert_b3)
    x = x + _L3_gnn_ref(_layernorm(x, axis=-1), adj, L3_gnn_W, L3_gnn_a_src, L3_gnn_a_dst)
    x = x + _L3_ffn_ref(_layernorm(x, axis=-1), L3_ffn_Wq_pk, L3_ffn_pk_keys, L3_ffn_Wq, L3_ffn_keys_table, L3_ffn_values_table, L3_ffn_Wo)
    return x

_drawn_inputs = setup_inputs


def setup_inputs(seed=0):
    import zlib

    import numpy as np

    out = dict(_drawn_inputs(seed))
    spreads = {'L0_ffn_b_gat': (0.0, 0.8),
     'L0_ffn_ln_gamma': (1.0, 0.6),
     'L0_ffn_ln_beta': (0.0, 0.8),
     'L0_ffn_b1': (0.0, 0.575),
     'L0_ffn_b2': (0.0, 0.296),
     'L1_ffn_alpha': (0.0, 0.8),
     'L1_ffn_bc': (0.0, 2.0),
     'L1_ffn_bg': (2.0, 0.2),
     'L1_ffn_bd': (0.0, 0.289),
     'L2_ffn_router_b1': (0.0, 0.596),
     'L2_ffn_router_b2': (0.0, 0.465),
     'L2_ffn_expert_b1': (0.0, 0.8),
     'L2_ffn_expert_b2': (0.0, 0.8),
     'L2_ffn_expert_b3': (0.0, 1.519)}
    factors = {'L0_gnn_gamma1': 7.386,
     'L0_gnn_beta1': 5.928,
     'L0_gnn_gamma2': 8.0,
     'L0_gnn_beta2': 8.0,
     'L0_gnn_W1': 3.698,
     'L0_gnn_b1': 24.542,
     'L0_gnn_W2': 3.543,
     'L0_gnn_b2': 28.141,
     'L0_ffn_att_src': 42.162,
     'L0_ffn_att_dst': 55.318,
     'L1_ffn_Wt': 4.951,
     'L1_ffn_bt': 4.477,
     'L1_ffn_sl_cvx': 2.681,
     'L1_ffn_of_cvx': 4.967,
     'L1_ffn_of_ccv': 5.517,
     'L1_ffn_Wc': 2.763,
     'L1_ffn_Wg': 6.543,
     'L2_gnn_a': 3.885,
     'L2_ffn_router_w1': 2.797,
     'L2_ffn_expert_w1': 4.376,
     'L2_ffn_expert_w2': 3.658,
     'L2_ffn_expert_w3': 2.856,
     'L3_gnn_a_src': 33.144,
     'L3_ffn_Wq_pk': 64.0,
     'L3_ffn_pk_keys': 64.0,
     'L3_ffn_Wq': 64.0,
     'L3_ffn_keys_table': 64.0,
     'L3_ffn_values_table': 64.0,
     'L3_ffn_Wo': 64.0,
     'L1_ffn_sl_ccv': 3.587,
     'L3_gnn_a_dst': 6.655}
    for name, (base, spread) in spreads.items():
        noise = np.random.default_rng([zlib.crc32(name.encode()), seed]).standard_normal(out[name].shape)
        drawn = base * np.exp(spread * noise) if base else spread * noise
        out[name] = jnp.asarray(drawn.astype(out[name].dtype))
    for name, factor in factors.items():
        out[name] = (out[name] * factor).astype(out[name].dtype)
    return out
```

```python
from contextlib import ExitStack, contextmanager

import concourse.bass as bass
from concourse import mybir

F32 = mybir.dt.float32
BF16 = mybir.dt.bfloat16
I32 = mybir.dt.int32
U32 = mybir.dt.uint32
ALU = mybir.AluOpType
ACT = mybir.ActivationFunctionType
AX_X = mybir.AxisListType.X

P = 128
D = 128
GRAPHS = 16
NODES = 512
TILES = NODES // P
ALL_TILES = GRAPHS * TILES
TOKENS = GRAPHS * NODES
EPS = 1e-5
NEG = -9000000000000000.0
MINUS_BIG = -1e30


def hold(eng, sem, value):
    eng.wait_ge(sem, value)
    eng.nop(nofuse=True)


class Core:

    def __init__(self, nc, ctx):
        self.nc, self.ctx = nc, ctx
        self.x = self.sbuf("x_resident", [P, ALL_TILES, D], F32)
        self.ident = self.sbuf("ident", [P, P], F32)
        self.ident_bf = self.sbuf("ident_bf", [P, P], BF16)
        self.ones_row = self.sbuf("ones_row", [1, P], F32)
        self.mean = self.sbuf("mean", [P, ALL_TILES], F32)
        self.rstd = self.sbuf("rstd", [P, ALL_TILES], F32)
        self.bank = [ctx.enter_context(nc.psum_tensor(f"bank{i}", [P, 512], F32)) for i in range(8)]
        self.edges_gathered = [ctx.enter_context(nc.semaphore(f"edges_gathered{i}")) for i in range(4)]
        self.memory_gathered = [ctx.enter_context(nc.semaphore(f"memory_gathered{i}")) for i in range(4)]
        self.stages = 0
        self.serial = 0

    @contextmanager
    def stage(self):
        outer = self.ctx
        self.stages += 1
        with ExitStack() as own:
            self.ctx, self.sems = own, []
            yield
            with self.nc.Block() as block:
                @block.gpsimd
                def _(pool):
                    for s in self.sems:
                        pool.sem_clear(s)
        self.ctx = outer

    def sbuf(self, name, shape, dt):
        return self.ctx.enter_context(self.nc.sbuf_tensor(name, shape, dt))

    def sem(self, name):
        self.sems.append(self.ctx.enter_context(self.nc.semaphore(f"s{self.stages}_{name}")))
        return self.sems[-1]


def load_and_constants(core, x_in):
    nc = core.nc
    s_x, s_zero, s_ident = core.sem("x_loaded"), core.sem("constants_cleared"), core.sem("identities_made")
    with nc.Block() as block:
        @block.sync
        def _(sp):
            sp.dma_start(core.x[:, :, :], x_in.rearrange("b (t p) d -> p (b t) d", p=P)).then_inc(s_x, 16)
            sp.wait_ge(s_x, 16)

        @block.gpsimd
        def _(pool):
            pool.memset(core.ident[:, :], 0.0).then_inc(s_zero, 1)
            pool.memset(core.ident_bf[:, :], 0.0).then_inc(s_zero, 1)
            pool.memset(core.ones_row[:, :], 1.0).then_inc(s_ident, 1)
            pool.wait_ge(s_zero, 2)
            for m in (core.ident, core.ident_bf):
                pool.affine_select(out=m[:, :], in_=m[:, :], compare_op=ALU.not_equal, fill=1.0, base=0,
                                   pattern=[[-1, P]], channel_multiplier=1).then_inc(s_ident, 1)


def store_result(core, out):
    nc = core.nc
    s_out = core.sem("result_stored")
    with nc.Block() as block:
        @block.sync
        def _(sp):
            sp.dma_start(out.rearrange("b (t p) d -> p (b t) d", p=P), core.x[:, :, :]).then_inc(s_out, 16)
            sp.wait_ge(s_out, 16)


def row_statistics(core, src):
    nc = core.nc
    core.serial += 1
    tag = core.serial
    s_stats, s_sqrt = core.sem(f"row_statistics{tag}"), core.sem(f"square_roots{tag}")
    with ExitStack() as own, nc.Block() as block:
        stats = own.enter_context(nc.sbuf_tensor(f"stats{tag}", [P, ALL_TILES, 6], F32))
        half_gap = own.enter_context(nc.sbuf_tensor(f"half_gap{tag}", [P, ALL_TILES], F32))
        var = own.enter_context(nc.sbuf_tensor(f"var{tag}", [P, ALL_TILES], F32))
        std = own.enter_context(nc.sbuf_tensor(f"std{tag}", [P, ALL_TILES], F32))
        even_mean, odd_mean = stats[:, :, 1], stats[:, :, 4]
        even_sq, odd_sq = stats[:, :, 2], stats[:, :, 5]
        steps = [0]

        @block.vector
        def _(dve):
            with dve.Fori(0, ALL_TILES) as t:
                dve.bn_stats(stats[:, bass.ds(t, 1), :].rearrange("p a s -> p (a s)"),
                             src[:, bass.ds(t, 1), :].rearrange("p a d -> p (a d)")).then_inc(s_stats, 1)
            steps[0] = ALL_TILES

            def then(ins):
                ins.then_inc(s_stats, 1)
                steps[0] += 1
                dve.wait_ge(s_stats, steps[0])

            dve.wait_ge(s_stats, steps[0])
            then(dve.tensor_tensor(core.mean[:, :], even_mean, odd_mean, ALU.add))
            then(dve.tensor_scalar(core.mean[:, :], core.mean[:, :], 0.5, None, ALU.mult))
            then(dve.tensor_tensor(half_gap[:, :], even_mean, odd_mean, ALU.subtract))
            then(dve.scalar_tensor_tensor(out=half_gap[:, :], in0=half_gap[:, :], scalar=0.25, in1=half_gap[:, :],
                                          op0=ALU.mult, op1=ALU.mult))
            then(dve.tensor_tensor(var[:, :], even_sq, odd_sq, ALU.add))
            then(dve.scalar_tensor_tensor(out=var[:, :], in0=var[:, :], scalar=1.0 / D, in1=half_gap[:, :],
                                          op0=ALU.mult, op1=ALU.add))
            then(dve.tensor_scalar(var[:, :], var[:, :], EPS, None, ALU.add))
            dve.wait_ge(s_sqrt, 1)
            then(dve.reciprocal(core.rstd[:, :], std[:, :]))

        @block.scalar
        def _(act):
            act.wait_ge(s_stats, ALL_TILES + 7)
            act.activation(std[:, :], var[:, :], ACT.Sqrt).then_inc(s_sqrt, 1)


def graph_layer(core, tag, adj, w_in, row_in, col_in, slope, over_rows, elu, keep_neg):
    nc = core.nc
    mask_value = NEG if keep_neg else MINUS_BIG
    with ExitStack() as own:
        def sb(name, shape, dt=F32):
            return own.enter_context(nc.sbuf_tensor(f"{tag}_{name}", shape, dt))

        def sem(name):
            return core.sem(f"{tag}_{name}")

        w = sb("w", [P, D])
        row_w = sb("row_w", [P, P])
        col_w = sb("col_w", [P, 1])
        adj_t = [sb(f"adj{k}", [P, TILES, NODES], I32) for k in range(2)]
        bias = [sb(f"bias{k}", [P, TILES, NODES], BF16) for k in range(2)]
        bias_use = [sb(f"bias_turned{k}", [P, TILES, NODES], BF16) for k in range(2)] if over_rows else bias
        xn = [sb(f"xn{k}", [P, TILES, D]) for k in range(2)]
        xnT = [sb(f"xnT{k}", [P, NODES]) for k in range(2)]
        h = [sb(f"h{k}", [P, TILES, D]) for k in range(2)]
        hT = [sb(f"hT{k}", [P, NODES]) for k in range(2)]
        row = [sb(f"row{k}", [P, NODES]) for k in range(2)]
        col = [sb(f"col{k}", [P, TILES]) for k in range(2)]
        e = [sb(f"e{k}", [P, NODES]) for k in range(2)]
        lk = [sb(f"leaky{k}", [P, NODES]) for k in range(2)] if slope else None
        em = [sb(f"em{k}", [P, TILES, NODES]) for k in range(2)]
        prob = [sb(f"prob{k}", [P, TILES, NODES]) for k in range(2)]
        probT = [sb(f"probT{k}", [P, TILES, NODES]) for k in range(2)] if not over_rows else None
        top = [sb(f"top{k}", [P, TILES]) for k in range(2)]
        ntop = [sb(f"ntop{k}", [P, TILES]) for k in range(2)]
        den = [sb(f"den{k}", [P, TILES]) for k in range(2)]
        rden = [sb(f"rden{k}", [P, TILES]) for k in range(2)]
        y = [sb(f"y{k}", [P, TILES, D]) for k in range(2)]
        low = [sb(f"low{k}", [P, TILES, D]) for k in range(2)]

        s_w, s_adj, s_bias, s_turn, s_biasT = sem("w"), [sem("adj0"), sem("adj1")], sem("bias"), sem("turned"), sem("biasT")
        s_xn, s_xT, s_xTc = sem("xn"), sem("xT"), sem("xTc")
        s_h, s_hTc, s_hc = sem("h"), sem("hTc"), sem("hc")
        s_sc, s_rowc, s_colc = sem("scores"), sem("rowc"), sem("colc")
        s_e, s_lk, s_em, s_nt, s_p = sem("e"), sem("leaky"), sem("em"), sem("ntop"), sem("prob")
        s_rd, s_hs = sem("rden"), sem("hs")
        s_pT, s_pTc = sem("pT"), sem("pTc")
        s_o, s_y, s_exp, s_acc = sem("o"), sem("y"), sem("expy"), sem("acc")
        b_xT, b_hT, b_h, b_row, b_col, b_o = (core.bank[i] for i in range(6))
        b_turn = [core.bank[6], core.bank[7]]

        def pairs(eng):
            return eng.Fori(0, GRAPHS // 2)

        with nc.Block() as block:
            @block.sync
            def _(sp):
                for dst, src in ((w, w_in), (row_w, row_in), (col_w, col_in)):
                    sp.dma_start(dst[:, :], src).then_inc(s_w, 16)
                with pairs(sp) as i:
                    for k in range(2):
                        n = i * 2 + k
                        hold(sp, s_bias, n)
                        sp.dma_start(adj_t[k][:, :, :],
                                     adj[bass.ds(n, 1)].rearrange("a (t p) m -> p (a t) m", p=P)).then_inc(s_adj[k], 16)

            @block.gpsimd
            def _(pool):
                pool.sem_inc(s_bias, 1)
                with pairs(pool) as i:
                    for k in range(2):
                        n = i * 2 + k
                        hold(pool, s_adj[k], i * 16 + 16)
                        hold(pool, s_turn if over_rows else s_em, n * TILES)
                        pool.tensor_scalar(bias[k][:, :, :], adj_t[k][:, :, :], 0, mask_value, ALU.is_le,
                                           ALU.mult).then_inc(s_bias, 1)

            @block.vector
            def _(dve):
                for s, c in ((s_em, TILES), (s_turn, TILES)):
                    dve.sem_inc(s, c)
                with pairs(dve) as i:
                    for k in range(2):
                        n = i * 2 + k
                        hold(dve, s_h, n)
                        for t in range(TILES):
                            tile = n * TILES + t
                            dve.tensor_scalar(
                                xn[k][:, t, :], core.x[:, bass.ds(tile, 1), :].rearrange("p a d -> p (a d)"),
                                core.mean[:, bass.ds(tile, 1)], core.rstd[:, bass.ds(tile, 1)],
                                ALU.subtract, ALU.mult).then_inc(s_xn, 1)
                        hold(dve, s_h, n + 2)
                        hold(dve, s_o, n)
                        dve.tensor_copy(h[k][:, :, :], b_h[:, :].rearrange("p (t d) -> p t d", t=TILES)).then_inc(s_hc, 1)
                        hold(dve, s_sc, n + 1)
                        dve.tensor_copy(col[k][:, :], b_col[:, 0:TILES]).then_inc(s_colc, 1)
                        if over_rows:
                            for t in range(TILES):
                                hold(dve, s_turn, n * TILES + TILES + t + 1)
                                dve.tensor_copy(bias_use[k][:, t, :],
                                                b_turn[t % 2][:, 0:NODES // 2].bitcast(BF16)).then_inc(s_biasT, 1)
                            hold(dve, s_biasT, n * TILES + TILES)
                        else:
                            hold(dve, s_bias, n + 2)
                        for t in range(TILES):
                            hold(dve, s_e, n * TILES + t + 1)
                            score = e[t % 2]
                            if slope:
                                dve.scalar_tensor_tensor(out=lk[t % 2][:, :], in0=e[t % 2][:, :], scalar=slope,
                                                         in1=e[t % 2][:, :], op0=ALU.mult, op1=ALU.max).then_inc(s_lk, 1)
                                hold(dve, s_lk, n * TILES + t + 1)
                                score = lk[t % 2]
                            dve.tensor_tensor(em[k][:, t, :], score[:, :], bias_use[k][:, t, :],
                                              ALU.add).then_inc(s_em, 1)
                        hold(dve, s_em, n * TILES + 2 * TILES)
                        dve.tensor_reduce(top[k][:, :], em[k][:, :, :], AX_X, ALU.max).then_inc(s_nt, 1)
                        hold(dve, s_nt, n * 2 + 1)
                        dve.tensor_scalar(ntop[k][:, :], top[k][:, :], -1.0, None, ALU.mult).then_inc(s_nt, 1)
                        hold(dve, s_p, n * TILES + TILES)
                        if not keep_neg:
                            dve.tensor_scalar(top[k][:, :], top[k][:, :], MINUS_BIG / 2, None, ALU.is_gt).then_inc(s_rd, 1)
                        else:
                            dve.memset(top[k][:, :], 1.0).then_inc(s_rd, 1)
                        dve.reciprocal(rden[k][:, :], den[k][:, :]).then_inc(s_rd, 1)
                        hold(dve, s_rd, n * 3 + 2)
                        dve.tensor_tensor(rden[k][:, :], rden[k][:, :], top[k][:, :], ALU.mult).then_inc(s_rd, 1)
                        hold(dve, s_rd, n * 3 + 3)
                        if over_rows:
                            hold(dve, s_hc, n + 1)
                            for t in range(TILES):
                                dve.tensor_scalar(h[k][:, t, :], h[k][:, t, :], rden[k][:, t:t + 1], None,
                                                  ALU.mult).then_inc(s_hs, 1)
                        else:
                            for t in range(TILES):
                                hold(dve, s_pT, n * TILES + t + 1)
                                dve.tensor_copy(probT[k][:, :, t * P:(t + 1) * P],
                                                b_turn[t % 2][:, :].rearrange("p (m n) -> p m n", m=TILES)).then_inc(s_pTc, 1)
                        hold(dve, s_o, n + 2)
                        rows = b_o[:, :].rearrange("p (t d) -> p t d", t=TILES)
                        if over_rows:
                            dve.tensor_copy(y[k][:, :, :], rows).then_inc(s_y, 1)
                        else:
                            dve.tensor_tensor(y[k][:, :, :], rows,
                                              rden[k][:, :].unsqueeze(2).to_broadcast([P, TILES, D]), ALU.mult).then_inc(s_y, 1)
                        hold(dve, s_y, n * 2 + 1)
                        xg = core.x[:, bass.ds(n * TILES, TILES), :]
                        if elu:
                            dve.tensor_scalar(low[k][:, :, :], y[k][:, :, :], 0.0, None, ALU.min).then_inc(s_y, 1)
                            hold(dve, s_exp, n + 1)
                            dve.scalar_tensor_tensor(out=y[k][:, :, :], in0=y[k][:, :, :], scalar=0.0,
                                                     in1=low[k][:, :, :], op0=ALU.max, op1=ALU.add).then_inc(s_acc, 1)
                            hold(dve, s_acc, n * 2 + 1)
                            dve.scalar_tensor_tensor(out=xg, in0=y[k][:, :, :], scalar=-1.0, in1=xg,
                                                     op0=ALU.add, op1=ALU.add).then_inc(s_acc, 1)
                        else:
                            dve.tensor_tensor(xg, xg, y[k][:, :, :], ALU.add).then_inc(s_y, 1)

            @block.scalar
            def _(act):
                with pairs(act) as i:
                    for k in range(2):
                        n = i * 2 + k
                        hold(act, s_xT, n + 1)
                        act.activation(xnT[k][:, :], b_xT[:, :], ACT.Copy).then_inc(s_xTc, 1)
                        hold(act, s_h, n + 2)
                        act.activation(hT[k][:, :], b_hT[:, :], ACT.Copy).then_inc(s_hTc, 1)
                        hold(act, s_sc, n + 1)
                        act.activation(row[k][:, :], b_row[:, :], ACT.Copy).then_inc(s_rowc, 1)
                        hold(act, s_rowc, n + 1)
                        hold(act, s_colc, n + 1)
                        for t in range(TILES):
                            hold(act, s_em, n * TILES + TILES + max(t - 1, 0))
                            act.activation(e[t % 2][:, :], row[k][:, :], ACT.Identity if slope else ACT.Relu,
                                           bias=col[k][:, t:t + 1], scale=1.0).then_inc(s_e, 1)
                        hold(act, s_nt, n * 2 + 2)
                        hold(act, s_o, n)
                        for t in range(TILES):
                            act.activation(prob[k][:, t, :], em[k][:, t, :], ACT.Exp, bias=ntop[k][:, t:t + 1],
                                           scale=1.0, accum_out=den[k][:, t:t + 1]).then_inc(s_p, 1)
                        if elu:
                            hold(act, s_y, n * 2 + 2)
                            act.activation(low[k][:, :, :], low[k][:, :, :], ACT.Exp).then_inc(s_exp, 1)

            @block.tensor
            def _(pe):
                pe.wait_ge(s_w, 48)
                pe.sem_inc(s_h, 1)
                pe.sem_inc(s_o, 1)
                with pairs(pe) as i:
                    for k in range(2):
                        n = i * 2 + k
                        hold(pe, s_xn, n * TILES + TILES)
                        hold(pe, s_xTc, n)
                        for t in range(TILES):
                            last = pe.transpose(b_xT[:, t * P:(t + 1) * P], xn[k][:, t, :], core.ident[:, :])
                        last.then_inc(s_xT, 1)
                        hold(pe, s_xTc, n + 1)
                        hold(pe, s_hTc, n)
                        hold(pe, s_hc, n)
                        pe.matmul(b_hT[:, :], w[:, :], xnT[k][:, :], start=True, stop=True)
                        for t in range(TILES):
                            last = pe.matmul(b_h[:, t * P:(t + 1) * P], xnT[k][:, t * P:(t + 1) * P], w[:, :],
                                             start=True, stop=True)
                        last.then_inc(s_h, 1)
                        hold(pe, s_hTc, n + 1)
                        hold(pe, s_rowc, n)
                        hold(pe, s_colc, n)
                        pe.matmul(b_row[:, :], row_w[:, :], hT[k][:, :], start=True, stop=True)
                        for t in range(TILES):
                            last = pe.matmul(b_col[:, t:t + 1], hT[k][:, t * P:(t + 1) * P], col_w[:, :],
                                             start=True, stop=True)
                        last.then_inc(s_sc, 1)
                        if over_rows:
                            hold(pe, s_bias, n + 2)
                            for t in range(TILES):
                                hold(pe, s_biasT, n * TILES + max(t - 1, 0))
                                turned = b_turn[t % 2][:, 0:NODES // 2].bitcast(BF16)
                                for m in range(TILES):
                                    last = pe.transpose(turned[:, m * P:(m + 1) * P],
                                                        bias[k][:, m, t * P:(t + 1) * P], core.ident_bf[:, :])
                                last.then_inc(s_turn, 1)
                            hold(pe, s_hs, n * TILES + TILES)
                            weights = prob[k]
                        else:
                            for t in range(TILES):
                                hold(pe, s_p, n * TILES + t + 1)
                                hold(pe, s_pTc, n * TILES + max(t - 1, 0))
                                for m in range(TILES):
                                    last = pe.transpose(b_turn[t % 2][:, m * P:(m + 1) * P],
                                                        prob[k][:, t, m * P:(m + 1) * P], core.ident[:, :])
                                last.then_inc(s_pT, 1)
                            hold(pe, s_pTc, n * TILES + TILES)
                            weights = probT[k]
                        hold(pe, s_y, n * 2)
                        for t in range(TILES):
                            for m in range(TILES):
                                last = pe.matmul(b_o[:, t * P:(t + 1) * P], weights[:, m, t * P:(t + 1) * P],
                                                 h[k][:, m, :], start=(m == 0), stop=(m == TILES - 1))
                        last.then_inc(s_o, 1)


def normed_transposed(core, tag, src, dst, gain=None, shift=None):
    nc = core.nc
    with ExitStack() as own:
        xn = [own.enter_context(nc.sbuf_tensor(f"{tag}_xn{k}", [P, TILES, D], F32)) for k in range(2)]
        s_xn, s_turned, s_copied = (core.sem(f"{tag}_{s}") for s in ("normed", "turned", "copied"))
        with nc.Block() as block:
            @block.vector
            def _(dve):
                with dve.Fori(0, GRAPHS // 2) as i:
                    for k in range(2):
                        n = i * 2 + k
                        hold(dve, s_turned, n)
                        for t in range(TILES):
                            tile = n * TILES + t
                            dve.tensor_scalar(
                                xn[k][:, t, :], src[:, bass.ds(tile, 1), :].rearrange("p a d -> p (a d)"),
                                core.mean[:, bass.ds(tile, 1)], core.rstd[:, bass.ds(tile, 1)],
                                ALU.subtract, ALU.mult).then_inc(s_xn, 1)

            @block.tensor
            def _(pe):
                pe.sem_inc(s_turned, 1)
                with pe.Fori(0, GRAPHS // 2) as i:
                    for k in range(2):
                        n = i * 2 + k
                        hold(pe, s_xn, n * TILES + TILES)
                        hold(pe, s_copied, n)
                        for t in range(TILES):
                            last = pe.transpose(core.bank[k][:, t * P:(t + 1) * P], xn[k][:, t, :], core.ident[:, :])
                        last.then_inc(s_turned, 1)

            @block.scalar
            def _(act):
                act.sem_inc(s_copied, 1)
                with act.Fori(0, GRAPHS // 2) as i:
                    for k in range(2):
                        n = i * 2 + k
                        hold(act, s_turned, n + 2)
                        out = dst[:, bass.ds(n, 1), :].rearrange("p a m -> p (a m)")
                        if gain is None:
                            act.activation(out, core.bank[k][:, :], ACT.Copy).then_inc(s_copied, 1)
                        else:
                            act.activation(out, core.bank[k][:, :], ACT.Identity, bias=shift[:, :],
                                           scale=gain[:, :]).then_inc(s_copied, 1)


def top_two_gates(core, tag, scores, gates, experts, apart):
    nc = core.nc
    with ExitStack() as own:
        def sb(name, shape):
            return own.enter_context(nc.sbuf_tensor(f"{tag}_{name}", shape, F32))

        best = [sb(f"best{r}", [P, ALL_TILES]) for r in range(2)]
        pick = [sb(f"pick{r}", [P, ALL_TILES, experts]) for r in range(2)]
        left = sb("left", [P, ALL_TILES, experts])
        free = sb("free", [P, ALL_TILES])
        share = [sb(f"share{r}", [P, ALL_TILES]) for r in range(2)]
        s_step, s_exp = core.sem(f"{tag}_gate_step"), core.sem(f"{tag}_gate_exp")
        whole = [P, ALL_TILES, experts]
        with nc.Block() as block:
            marks = {}

            @block.vector
            def _(dve):
                steps = 0

                def then(ins):
                    nonlocal steps
                    steps += 1
                    ins.then_inc(s_step, 1)
                    dve.wait_ge(s_step, steps)

                for r, pool_of in ((0, scores), (1, left)):
                    then(dve.tensor_reduce(best[r][:, :], pool_of[:, :, :], AX_X, ALU.max))
                    then(dve.tensor_tensor(pick[r][:, :, :], pool_of[:, :, :],
                                           best[r][:, :].unsqueeze(2).to_broadcast(whole), ALU.is_equal))
                    then(dve.memset(free[:, :], 1.0))
                    for e in range(experts):
                        then(dve.tensor_tensor(pick[r][:, :, e], pick[r][:, :, e], free[:, :], ALU.mult))
                        then(dve.tensor_tensor(free[:, :], free[:, :], pick[r][:, :, e], ALU.subtract))
                    if r == 0:
                        then(dve.scalar_tensor_tensor(out=left[:, :, :], in0=pick[0][:, :, :], scalar=-apart,
                                                      in1=scores[:, :, :], op0=ALU.mult, op1=ALU.add))
                then(dve.tensor_tensor(share[1][:, :], best[1][:, :], best[0][:, :], ALU.subtract))
                marks["gap"] = steps
                dve.wait_ge(s_exp, 1)
                then(dve.tensor_scalar(free[:, :], share[1][:, :], 1.0, None, ALU.add))
                then(dve.reciprocal(share[0][:, :], free[:, :]))
                then(dve.tensor_tensor(share[1][:, :], share[1][:, :], share[0][:, :], ALU.mult))
                for r in range(2):
                    then(dve.tensor_tensor(pick[r][:, :, :], pick[r][:, :, :],
                                           share[r][:, :].unsqueeze(2).to_broadcast(whole), ALU.mult))
                then(dve.tensor_tensor(gates[:, :, :], pick[0][:, :, :], pick[1][:, :, :], ALU.add))

            @block.scalar
            def _(act):
                act.wait_ge(s_step, marks["gap"])
                act.activation(share[1][:, :], share[1][:, :], ACT.Exp).then_inc(s_exp, 1)


def gelu_experts(core, tag, xT, w1_in, b1_in, w2_in, b2_in, gates, target):
    nc = core.nc
    _, E, F, _ = w1_in.shape
    with ExitStack() as own:
        def sb(name, shape):
            return own.enter_context(nc.sbuf_tensor(f"{tag}_{name}", shape, F32))

        w1, b1 = sb("w1", [P, E, F, P]), sb("b1", [P, E, F])
        w2, b2 = sb("w2", [P, E, F, D]), sb("b2", [1, E, D])
        hidden = [[sb(f"hidden{k}_{f}", [P, NODES]) for f in range(F)] for k in range(2)]
        s_w = core.sem(f"{tag}_weights")
        s_up, s_act = core.sem(f"{tag}_up"), core.sem(f"{tag}_gelu")
        s_down, s_add = core.sem(f"{tag}_down"), core.sem(f"{tag}_added")
        up, down = core.bank[0:4], core.bank[4:6]
        assert E == 1 or E % 2 == 0
        G = 2 if E == 1 else 1
        turns = G * E
        with nc.Block() as block:
            @block.sync
            def _(sp):
                for dst, src in ((w1, w1_in), (b1, b1_in), (w2, w2_in), (b2, b2_in)):
                    sp.dma_start(dst[:], src).then_inc(s_w, 16)

            @block.tensor
            def _(pe):
                pe.wait_ge(s_w, 64)

                def rise(i, j):
                    graph = i * G + j // E
                    for f in range(F):
                        c = (j * F + f) % 4
                        hold(pe, s_act, i * (turns * F) + j * F + f + 1)
                        pe.matmul(up[c][:, :], w1[:, j % E, f, :],
                                  xT[:, bass.ds(graph, 1), :].rearrange("p a m -> p (a m)"),
                                  start=True, stop=True).then_inc(s_up, 1)

                def fall(i, j):
                    hold(pe, s_act, i * (turns * F) + (j + 1) * F + 3 + 1)
                    hold(pe, s_add, i * turns + j)
                    for t in range(TILES):
                        o = down[j % 2][:, t * P:(t + 1) * P]
                        for f in range(F):
                            pe.matmul(o, hidden[j % 2][f][:, t * P:(t + 1) * P], w2[:, j % E, f, :],
                                      start=(f == 0), stop=False)
                        last = pe.matmul(o, core.ones_row[:, :], b2[:, j % E, :], start=False, stop=True)
                    last.then_inc(s_down, 1)

                with pe.Fori(0, GRAPHS // G) as i:
                    for j in range(turns + 1):
                        if j < turns:
                            rise(i, j)
                        if j >= 1:
                            fall(i, j - 1)

            @block.scalar
            def _(act):
                act.wait_ge(s_w, 64)
                act.sem_inc(s_act, 4)
                with act.Fori(0, GRAPHS // G) as i:
                    for j in range(turns):
                        hold(act, s_down, i * turns + max(j - 1, 0))
                        for f in range(F):
                            hold(act, s_up, i * (turns * F) + j * F + f + 1)
                            act.activation(hidden[j % 2][f][:, :], up[(j * F + f) % 4][:, :], ACT.Gelu,
                                           bias=b1[:, j % E, f:f + 1], scale=1.0).then_inc(s_act, 1)

            @block.vector
            def _(dve):
                dve.sem_inc(s_add, 1)
                with dve.Fori(0, GRAPHS // G) as i:
                    for j in range(turns):
                        graph = i * G + j // E
                        hold(dve, s_down, i * turns + j + 1)
                        hold(dve, s_add, i * turns + j + 1)
                        if gates is None:
                            xg = target[:, bass.ds(graph * TILES, TILES), :]
                            dve.tensor_tensor(xg, down[j % 2][:, :].rearrange("p (t d) -> p t d", t=TILES), xg,
                                              ALU.add).then_inc(s_add, 1)
                        else:
                            for t in range(TILES):
                                tile = graph * TILES + t
                                xt = target[:, bass.ds(tile, 1), :].rearrange("p a d -> p (a d)")
                                last = dve.scalar_tensor_tensor(
                                    out=xt, in0=down[j % 2][:, t * P:(t + 1) * P],
                                    scalar=gates[:, bass.ds(tile, 1), j % E:j % E + 1].rearrange("p a b -> p (a b)"),
                                    in1=xt, op0=ALU.mult, op1=ALU.add)
                            last.then_inc(s_add, 1)


def routed_experts(core, r1_in, rb1_in, r2_in, rb2_in, w_in, b12_in, b3_in, experts):
    nc = core.nc
    E, R = experts, r1_in.shape[1]
    row_statistics(core, core.x)
    with ExitStack() as own:
        def sb(name, shape):
            return own.enter_context(nc.sbuf_tensor(f"f2_{name}", shape, F32))

        def sem(name):
            return core.sem(f"f2_{name}")

        xT = sb("xT", [P, GRAPHS, NODES])
        normed_transposed(core, "f2n", core.x, xT)
        r1, rb1, r2, rb2 = sb("r1", [P, R]), sb("rb1", [R, 1]), sb("r2", [R, E]), sb("rb2", [1, E])
        w, b12, b3 = sb("w", [P, 3, E, P]), sb("b12", [P, 2, E]), sb("b3", [1, E, D])
        logits, gates = sb("logits", [P, ALL_TILES, E]), sb("gates", [P, ALL_TILES, E])
        rh = [sb(f"rh{k}", [R, NODES]) for k in range(2)]
        s_w, s_r, s_rc, s_l, s_lc = sem("w"), sem("router_up"), sem("router_relu"), sem("logits"), sem("logits_copied")

        with nc.Block() as block:
            @block.sync
            def _(sp):
                for dst, src in ((r1, r1_in), (rb1, rb1_in), (r2, r2_in), (rb2, rb2_in), (w, w_in), (b12, b12_in),
                                 (b3, b3_in)):
                    sp.dma_start(dst[:], src).then_inc(s_w, 16)
                sp.wait_ge(s_w, 7 * 16)

            @block.tensor
            def _(pe):
                pe.wait_ge(s_w, 7 * 16)
                with pe.Fori(0, GRAPHS // 2) as i:
                    for k in range(2):
                        n = i * 2 + k
                        hold(pe, s_rc, n)
                        pe.matmul(core.bank[k][0:R, :], r1[:, :], xT[:, bass.ds(n, 1), :].rearrange("p a m -> p (a m)"),
                                  start=True, stop=True).then_inc(s_r, 1)
                        hold(pe, s_rc, n + 2)
                        hold(pe, s_lc, n)
                        for t in range(TILES):
                            o = core.bank[2 + k][:, t * E:(t + 1) * E]
                            pe.matmul(o, rh[k][:, t * P:(t + 1) * P], r2[:, :], start=True, stop=False)
                            last = pe.matmul(o, core.ones_row[:, :], rb2[:, :], start=False, stop=True)
                        last.then_inc(s_l, 1)

            @block.scalar
            def _(act):
                act.wait_ge(s_w, 7 * 16)
                act.sem_inc(s_rc, 1)
                with act.Fori(0, GRAPHS // 2) as i:
                    for k in range(2):
                        n = i * 2 + k
                        hold(act, s_r, n + 1)
                        hold(act, s_l, (i * 2) + max(k - 1, 0))
                        act.activation(rh[k][:, :], core.bank[k][0:R, :], ACT.Relu, bias=rb1[:, :],
                                       scale=1.0).then_inc(s_rc, 1)

            @block.vector
            def _(dve):
                dve.sem_inc(s_lc, 1)
                with dve.Fori(0, GRAPHS // 2) as i:
                    for k in range(2):
                        n = i * 2 + k
                        hold(dve, s_l, n + 1)
                        dve.tensor_copy(logits[:, bass.ds(n * TILES, TILES), :],
                                        core.bank[2 + k][:, 0:TILES * E].rearrange("p (t e) -> p t e", t=TILES)
                                        ).then_inc(s_lc, 1)

        top, total = sb("top", [P, ALL_TILES]), sb("total", [P, ALL_TILES])
        s_step, s_exp = sem("softmax_step"), sem("softmax_exp")
        whole = [P, ALL_TILES, E]
        with nc.Block() as block:
            @block.vector
            def _(dve):
                dve.tensor_reduce(top[:, :], logits[:, :, :], AX_X, ALU.max).then_inc(s_step, 1)
                dve.wait_ge(s_step, 1)
                dve.tensor_tensor(logits[:, :, :], logits[:, :, :], top[:, :].unsqueeze(2).to_broadcast(whole),
                                  ALU.subtract).then_inc(s_step, 1)
                dve.wait_ge(s_exp, 1)
                dve.tensor_reduce(total[:, :], logits[:, :, :], AX_X, ALU.add).then_inc(s_step, 1)
                dve.wait_ge(s_step, 3)
                dve.reciprocal(total[:, :], total[:, :]).then_inc(s_step, 1)
                dve.wait_ge(s_step, 4)
                dve.tensor_tensor(logits[:, :, :], logits[:, :, :], total[:, :].unsqueeze(2).to_broadcast(whole),
                                  ALU.mult).then_inc(s_step, 1)

            @block.scalar
            def _(act):
                act.wait_ge(s_step, 2)
                act.activation(logits[:, :, :], logits[:, :, :], ACT.Exp).then_inc(s_exp, 1)
        top_two_gates(core, "f2", logits, gates, E, 4.0)

        h1 = [sb(f"h1_{k}", [P, NODES]) for k in range(2)]
        h2 = [sb(f"h2_{k}", [P, NODES]) for k in range(2)]
        s_1, s_1c, s_2, s_2c, s_3, s_add = (sem(s) for s in ("first", "first_relu", "second", "second_relu", "third",
                                                             "added"))
        first, second, third = core.bank[0:2], core.bank[2:4], core.bank[4:6]
        with nc.Block() as block:
            @block.tensor
            def _(pe):
                with pe.Fori(0, GRAPHS) as n:
                    for j in range(E + 2):
                        if j < E:
                            hold(pe, s_1c, n * E + j)
                            pe.matmul(first[j % 2][:, :], w[:, 0, j, :],
                                      xT[:, bass.ds(n, 1), :].rearrange("p a m -> p (a m)"),
                                      start=True, stop=True).then_inc(s_1, 1)
                        if 1 <= j <= E:
                            c = j - 1
                            hold(pe, s_1c, n * E + c + 2)
                            hold(pe, s_2c, n * E + c)
                            pe.matmul(second[c % 2][:, :], w[:, 1, c, :], h1[c % 2][:, :],
                                      start=True, stop=True).then_inc(s_2, 1)
                        if j >= 2:
                            c = j - 2
                            hold(pe, s_2c, n * E + c + 2)
                            hold(pe, s_add, n * E + c)
                            for t in range(TILES):
                                o = third[c % 2][:, t * P:(t + 1) * P]
                                pe.matmul(o, h2[c % 2][:, t * P:(t + 1) * P], w[:, 2, c, :], start=True, stop=False)
                                last = pe.matmul(o, core.ones_row[:, :], b3[:, c, :], start=False, stop=True)
                            last.then_inc(s_3, 1)

            @block.scalar
            def _(act):
                act.sem_inc(s_1c, 1)
                act.sem_inc(s_2c, 1)
                with act.Fori(0, GRAPHS) as n:
                    for j in range(E + 1):
                        if j < E:
                            hold(act, s_1, n * E + j + 1)
                            hold(act, s_2, n * E + max(j - 1, 0))
                            act.activation(h1[j % 2][:, :], first[j % 2][:, :], ACT.Relu, bias=b12[:, 0, j:j + 1],
                                           scale=1.0).then_inc(s_1c, 1)
                        if j >= 1:
                            c = j - 1
                            hold(act, s_2, n * E + c + 1)
                            hold(act, s_3, n * E + max(c - 1, 0))
                            act.activation(h2[c % 2][:, :], second[c % 2][:, :], ACT.Relu, bias=b12[:, 1, c:c + 1],
                                           scale=1.0).then_inc(s_2c, 1)

            @block.vector
            def _(dve):
                dve.sem_inc(s_add, 1)
                with dve.Fori(0, GRAPHS) as n:
                    for j in range(E):
                        hold(dve, s_3, n * E + j + 1)
                        hold(dve, s_add, n * E + j + 1)
                        for t in range(TILES):
                            tile = n * TILES + t
                            xt = core.x[:, bass.ds(tile, 1), :].rearrange("p a d -> p (a d)")
                            last = dve.scalar_tensor_tensor(
                                out=xt, in0=third[j % 2][:, t * P:(t + 1) * P],
                                scalar=gates[:, bass.ds(tile, 1), j:j + 1].rearrange("p a b -> p (a b)"),
                                in1=xt, op0=ALU.mult, op1=ALU.add)
                        last.then_inc(s_add, 1)


def attention_layer(core, adj, head_scale_in, gain1_in, shift1_in, gain2_in, shift2_in, w1_in, b1_in, w2_in, b2_in,
                    heads):
    nc = core.nc
    H, HD = heads, D // heads
    UNITS = H * TILES
    with ExitStack() as own:
        def sb(name, shape, dt=F32):
            return own.enter_context(nc.sbuf_tensor(f"g0_{name}", shape, dt))

        def sem(name):
            return core.sem(f"g0_{name}")

        y = sb("y", [P, ALL_TILES, D])
        s_w, s_y0 = sem("w"), sem("y_made")
        gain2, shift2 = sb("gain2", [P, 1]), sb("shift2", [P, 1])
        row_statistics(core, core.x)
        with nc.Block() as block:
            @block.sync
            def _(sp):
                sp.dma_start(gain2[:, :], gain2_in).then_inc(s_w, 16)
                sp.dma_start(shift2[:, :], shift2_in).then_inc(s_w, 16)
                sp.wait_ge(s_w, 32)

            @block.vector
            def _(dve):
                with dve.Fori(0, ALL_TILES) as t:
                    dve.tensor_scalar(y[:, bass.ds(t, 1), :].rearrange("p a d -> p (a d)"),
                                      core.x[:, bass.ds(t, 1), :].rearrange("p a d -> p (a d)"),
                                      core.mean[:, bass.ds(t, 1)], core.rstd[:, bass.ds(t, 1)],
                                      ALU.subtract, ALU.mult).then_inc(s_y0, 1)
        row_statistics(core, y)

        with ExitStack() as attn:
            def sba(name, shape, dt=F32):
                return attn.enter_context(nc.sbuf_tensor(f"g0_{name}", shape, dt))

            head_scale = sba("head_scale", [P, H])
            gain1, shift1 = sba("gain1", [P, D]), sba("shift1", [P, D])
            adj_t = [sba(f"adj{k}", [P, TILES, NODES], I32) for k in range(2)]
            bias = [sba(f"bias{k}", [P, TILES, NODES], BF16) for k in range(2)]
            nrm = [sba(f"normed{k}", [P, TILES, D]) for k in range(2)]
            nT = [sba(f"normedT{k}", [P, NODES]) for k in range(2)]
            one_head = [sba(f"one_head{k}", [P, NODES]) for k in range(2)]
            ntop = [sba(f"ntop{k}", [P, UNITS]) for k in range(2)]
            den = [sba(f"den{k}", [P, TILES, H]) for k in range(2)]
            rden = [sba(f"rden{k}", [P, TILES, H]) for k in range(2)]
            prob = [sba(f"prob{k}", [P, NODES]) for k in range(2)]
            probT = [sba(f"probT{k}", [P, TILES, P]) for k in range(2)]
            o_sb = [sba(f"o{k}", [P, TILES, D]) for k in range(2)]
            s_adj = [sem("adj0"), sem("adj1")]
            s_bias, s_nrm, s_turned, s_nT = sem("bias"), sem("normed"), sem("turned"), sem("normedT")
            s_head, s_s, s_top, s_p = sem("one_head"), sem("scores"), sem("top"), sem("prob")
            s_pT, s_pTc, s_o, s_done, s_y = sem("probT"), sem("probT_copied"), sem("out"), sem("out_scaled"), sem("y")
            score, turn, out_bank, nT_bank = core.bank[0:2], core.bank[2:4], core.bank[4:6], core.bank[6]

            with nc.Block() as block:
                @block.sync
                def _(sp):
                    for dst, src in ((head_scale, head_scale_in), (gain1, gain1_in), (shift1, shift1_in)):
                        sp.dma_start(dst[:, :], src).then_inc(s_w, 16)
                    with sp.Fori(0, GRAPHS // 2) as i:
                        for k in range(2):
                            n = i * 2 + k
                            hold(sp, s_bias, n)
                            sp.dma_start(adj_t[k][:, :, :],
                                         adj[bass.ds(n, 1)].rearrange("a (t p) m -> p (a t) m", p=P)
                                         ).then_inc(s_adj[k], 16)

                @block.gpsimd
                def _(pool):
                    pool.sem_inc(s_bias, 1)
                    pool.wait_ge(s_w, 80)
                    with pool.Fori(0, GRAPHS // 2) as i:
                        for k in range(2):
                            n = i * 2 + k
                            hold(pool, s_adj[k], i * 16 + 16)
                            pool.tensor_scalar(bias[k][:, :, :], adj_t[k][:, :, :], 0, MINUS_BIG, ALU.is_le,
                                               ALU.mult).then_inc(s_bias, 1)
                            hold(pool, s_nT, n + 1)
                            for h in range(H):
                                hold(pool, s_s, n * UNITS + max(h - 1, 0) * TILES)
                                pool.tensor_scalar(one_head[h % 2][:, :], nT[k][:, :], head_scale[:, h:h + 1], None,
                                                   ALU.mult).then_inc(s_head, 1)

                @block.vector
                def _(dve):
                    dve.wait_ge(s_w, 80)
                    dve.sem_inc(s_pTc, 2)
                    dve.sem_inc(s_done, 1)
                    with dve.Fori(0, GRAPHS // 2) as i:
                        for k in range(2):
                            n = i * 2 + k
                            for t in range(TILES):
                                tile = n * TILES + t
                                dve.tensor_scalar(
                                    nrm[k][:, t, :], y[:, bass.ds(tile, 1), :].rearrange("p a d -> p (a d)"),
                                    core.mean[:, bass.ds(tile, 1)], core.rstd[:, bass.ds(tile, 1)],
                                    ALU.subtract, ALU.mult).then_inc(s_nrm, 1)
                            base = n * (TILES + 2)
                            hold(dve, s_nrm, base + TILES)
                            dve.tensor_tensor(nrm[k][:, :, :], nrm[k][:, :, :],
                                              gain1[:, :].unsqueeze(1).to_broadcast([P, TILES, D]), ALU.mult).then_inc(s_nrm, 1)
                            hold(dve, s_nrm, base + TILES + 1)
                            dve.tensor_tensor(nrm[k][:, :, :], nrm[k][:, :, :],
                                              shift1[:, :].unsqueeze(1).to_broadcast([P, TILES, D]), ALU.add).then_inc(s_nrm, 1)
                            for u in range(UNITS + 1):
                                if u < UNITS:
                                    hold(dve, s_s, n * UNITS + u + 1)
                                    dve.tensor_reduce(ntop[k][:, u:u + 1], score[u % 2][:, :], AX_X, ALU.max,
                                                      negate=True).then_inc(s_top, 1)
                                if u >= 1:
                                    v = u - 1
                                    hold(dve, s_pT, n * UNITS + v + 1)
                                    hold(dve, s_o, n * UNITS + max(v - 1, 0))
                                    dve.tensor_copy(probT[v % 2][:, :, :],
                                                    turn[v % 2][:, :].rearrange("p (m q) -> p m q", m=TILES)
                                                    ).then_inc(s_pTc, 1)
                            hold(dve, s_p, n * UNITS + UNITS)
                            dve.reciprocal(rden[k][:, :, :], den[k][:, :, :]).then_inc(s_y, 1)
                            hold(dve, s_y, n * 2 + 1)
                            hold(dve, s_o, n * UNITS + UNITS)
                            for t in range(TILES):
                                dve.tensor_tensor(
                                    o_sb[k][:, t, :].rearrange("p (h c) -> p h c", h=H),
                                    out_bank[k][:, t * P:(t + 1) * P].rearrange("p (h c) -> p h c", h=H),
                                    rden[k][:, t, :].unsqueeze(2).to_broadcast([P, H, HD]), ALU.mult
                                    ).then_inc(s_done, 1)
                            hold(dve, s_done, n * TILES + TILES + 1)
                            yg = y[:, bass.ds(n * TILES, TILES), :]
                            dve.tensor_tensor(yg, yg, o_sb[k][:, :, :], ALU.add).then_inc(s_y, 1)

                @block.scalar
                def _(act):
                    with act.Fori(0, GRAPHS // 2) as i:
                        for k in range(2):
                            n = i * 2 + k
                            hold(act, s_turned, n + 1)
                            act.activation(nT[k][:, :], nT_bank[:, :], ACT.Copy).then_inc(s_nT, 1)
                            for u in range(UNITS):
                                h, t = divmod(u, TILES)
                                hold(act, s_top, n * UNITS + u + 1)
                                hold(act, s_pT, n * UNITS + max(u - 1, 0))
                                act.activation(prob[u % 2][:, :], score[u % 2][:, :], ACT.Exp,
                                               bias=ntop[k][:, u:u + 1], scale=1.0,
                                               accum_out=den[k][:, t, h:h + 1]).then_inc(s_p, 1)

                @block.tensor
                def _(pe):
                    with pe.Fori(0, GRAPHS // 2) as i:
                        for k in range(2):
                            n = i * 2 + k
                            hold(pe, s_nrm, n * (TILES + 2) + TILES + 2)
                            hold(pe, s_nT, n)
                            for t in range(TILES):
                                last = pe.transpose(nT_bank[:, t * P:(t + 1) * P], nrm[k][:, t, :], core.ident[:, :])
                            last.then_inc(s_turned, 1)
                            hold(pe, s_nT, n + 1)
                            hold(pe, s_bias, n + 2)
                            hold(pe, s_done, n * TILES)
                            for u in range(UNITS + 2):
                                if u < UNITS:
                                    h, t = divmod(u, TILES)
                                    if t == 0:
                                        hold(pe, s_head, n * H + h + 1)
                                    hold(pe, s_p, n * UNITS + max(u - 1, 0))
                                    pe.matmul(score[u % 2][:, :], one_head[h % 2][:, t * P:(t + 1) * P],
                                              nT[k][:, :], start=True, stop=False)
                                    pe.matmul(score[u % 2][:, :], core.ident_bf[:, :], bias[k][:, t, :],
                                              start=False, stop=True).then_inc(s_s, 1)
                                if 1 <= u <= UNITS:
                                    v = u - 1
                                    hold(pe, s_p, n * UNITS + v + 1)
                                    hold(pe, s_pTc, n * UNITS + v + 1)
                                    for m in range(TILES):
                                        last = pe.transpose(turn[v % 2][:, m * P:(m + 1) * P],
                                                            prob[v % 2][:, m * P:(m + 1) * P], core.ident[:, :])
                                    last.then_inc(s_pT, 1)
                                if u >= 2:
                                    v = u - 2
                                    h, t = divmod(v, TILES)
                                    hold(pe, s_pTc, n * UNITS + v + 3)
                                    o = out_bank[k][:, t * P + h * HD:t * P + (h + 1) * HD]
                                    for m in range(TILES):
                                        last = pe.matmul(o, probT[v % 2][:, m, :],
                                                         nrm[k][:, m, h * HD:(h + 1) * HD],
                                                         start=(m == 0), stop=(m == TILES - 1))
                                    last.then_inc(s_o, 1)

        row_statistics(core, y)
        yT = sb("yT", [P, GRAPHS, NODES])
        normed_transposed(core, "g0n", y, yT, gain2, shift2)
        s_res = sem("residual")
        with nc.Block() as block:
            @block.vector
            def _(dve):
                dve.tensor_tensor(core.x[:, :, :], core.x[:, :, :], y[:, :, :], ALU.add).then_inc(s_res, 1)
        gelu_experts(core, "g0m", yT, w1_in, b1_in, w2_in, b2_in, None, core.x)


def edge_routed_experts(core, edges, wgat_in, att_in, post_in, w1_in, b1_in, w2_in, b2_in, experts, scratch):
    nc = core.nc
    X = experts
    HEADS = att_in.shape[2] // X
    HX = HEADS * X
    F = HEADS + HX
    EDGE_COLS = edges.shape[2]
    BATCH = 16
    BATCHES = EDGE_COLS // BATCH
    RING = 4
    LOW = 1024
    BLOCKS, HIGH = LOW // P, TOKENS // LOW
    COLS = 3 * HIGH * F
    HEADROOM = 60.0
    assert COLS <= 512 and BLOCKS == 8
    row_statistics(core, core.x)
    with ExitStack() as own:
        def sb(name, shape, dt=F32):
            return own.enter_context(nc.sbuf_tensor(f"f0_{name}", shape, dt))

        def sem(name):
            return core.sem(f"f0_{name}")

        xT = sb("xT", [P, GRAPHS, NODES])
        normed_transposed(core, "f0n", core.x, xT)
        gates = sb("gates", [P, ALL_TILES, X])
        with ExitStack() as edge_part:
            def sbe(name, shape, dt=F32):
                return edge_part.enter_context(nc.sbuf_tensor(f"f0_{name}", shape, dt))

            wgat, att, post = sbe("wgat", [P, HX]), sbe("att", [P, 2, HX]), sbe("post", [P, 3, HX])
            source = sbe("source", [P, ALL_TILES, F])
            target = sbe("target", [P, ALL_TILES, 2 * HEADS])
            prod = sbe("prod", [P, ALL_TILES, HX])
            peak, peak_all = sbe("peak", [P, HEADS]), sbe("peak_all", [P, HEADS])
            hT = [sbe(f"hT{k}", [HX, NODES]) for k in range(2)]
            s_w, s_h, s_hc, s_t, s_tc = sem("w"), sem("h"), sem("h_copied"), sem("h_turned"), sem("h_turned_copied")
            s_tab, s_peak, s_store = sem("table_step"), sem("peak"), sem("tables_stored")
            src, dst = sbe("src", [P, EDGE_COLS + BATCH], I32), sbe("dst", [P, EDGE_COLS + BATCH], I32)
            s_edges = sem("edges")
            with nc.Block() as block:
                @block.sync
                def _(sp):
                    for to, of in ((wgat, wgat_in), (att, att_in), (post, post_in)):
                        sp.dma_start(to[:], of).then_inc(s_w, 16)
                    sp.dma_start(src[:, 0:EDGE_COLS], edges[0]).then_inc(s_edges, 16)
                    sp.dma_start(dst[:, 0:EDGE_COLS], edges[1]).then_inc(s_edges, 16)
                    sp.wait_ge(s_w, 48)
                    sp.wait_ge(s_tab, 9)
                    with nc.allow_non_contiguous_dma(reason="rows of a few floats"):
                        sp.dma_start(scratch[0].rearrange("(t p) f -> p t f", p=P), source[:, :, :]).then_inc(s_store, 16)
                        sp.dma_start(scratch[1].rearrange("(t p) f -> p t f", p=P), target[:, :, :]).then_inc(s_store, 16)
                    sp.wait_ge(s_store, 32)
                    sp.wait_ge(s_edges, 32)

                @block.tensor
                def _(pe):
                    pe.wait_ge(s_w, 48)
                    with pe.Fori(0, GRAPHS // 2) as i:
                        for k in range(2):
                            n = i * 2 + k
                            hold(pe, s_hc, n)
                            pe.matmul(core.bank[k][0:HX, :], wgat[:, :],
                                      xT[:, bass.ds(n, 1), :].rearrange("p a m -> p (a m)"),
                                      start=True, stop=True).then_inc(s_h, 1)
                            hold(pe, s_hc, n + 2)
                            hold(pe, s_tc, n)
                            for t in range(TILES):
                                last = pe.transpose(core.bank[2 + k][:, t * HX:(t + 1) * HX],
                                                    hT[k][:, t * P:(t + 1) * P], core.ident[0:HX, 0:HX])
                            last.then_inc(s_t, 1)

                @block.scalar
                def _(act):
                    act.sem_inc(s_hc, 1)
                    with act.Fori(0, GRAPHS // 2) as i:
                        for k in range(2):
                            n = i * 2 + k
                            hold(act, s_h, n + 1)
                            hold(act, s_t, i * 2 + max(k - 1, 0))
                            act.activation(hT[k][:, :], core.bank[k][0:HX, :], ACT.Copy).then_inc(s_hc, 1)

                @block.vector
                def _(dve):
                    dve.sem_inc(s_tc, 1)
                    with dve.Fori(0, GRAPHS // 2) as i:
                        for k in range(2):
                            n = i * 2 + k
                            hold(dve, s_t, n + 1)
                            dve.tensor_copy(source[:, bass.ds(n * TILES, TILES), HEADS:F],
                                            core.bank[2 + k][:, 0:TILES * HX].rearrange("p (t e) -> p t e", t=TILES)
                                            ).then_inc(s_tc, 1)
                    dve.wait_ge(s_tc, GRAPHS + 1)
                    dve.wait_ge(s_w, 48)
                    steps = 0

                    def then(ins):
                        nonlocal steps
                        steps += 1
                        ins.then_inc(s_tab, 1)
                        dve.wait_ge(s_tab, steps)

                    for side, into in ((0, source[:, :, 0:HEADS]), (1, target[:, :, 0:HEADS])):
                        then(dve.tensor_tensor(prod[:, :, :], source[:, :, HEADS:F],
                                               att[:, side, :].unsqueeze(1).to_broadcast([P, ALL_TILES, HX]), ALU.mult))
                        then(dve.tensor_reduce(into, prod[:, :, :].rearrange("p t (h e) -> p t h e", h=HEADS),
                                               AX_X, ALU.add))
                    then(dve.tensor_reduce(peak[:, :], source[:, :, 0:HEADS].rearrange("p t h -> p h t"), AX_X, ALU.max))
                    dve.wait_ge(s_peak, 1)
                    reference = target[:, :, HEADS:2 * HEADS]
                    then(dve.tensor_tensor(reference, target[:, :, 0:HEADS],
                                           peak_all[:, :].unsqueeze(1).to_broadcast([P, ALL_TILES, HEADS]), ALU.add))
                    then(dve.tensor_scalar(prod[:, :, 0:HEADS], reference, 0.2, None, ALU.mult))
                    then(dve.tensor_tensor(reference, prod[:, :, 0:HEADS], reference, ALU.max))
                    then(dve.tensor_scalar(reference, reference, -HEADROOM, None, ALU.add))

                @block.gpsimd
                def _(pool):
                    pool.wait_ge(s_tab, 5)
                    pool.partition_all_reduce(peak_all[:, :], peak[:, :], P, bass.bass_isa.ReduceOp.max).then_inc(s_peak, 1)

            agg = sbe("agg", [P, ALL_TILES, F])
            with ExitStack() as loop_part:
                def sbl(name, shape, dt=F32):
                    return loop_part.enter_context(nc.sbuf_tensor(f"f0_{name}", shape, dt))

                lanes_i, highs_i = sbl("lanes_i", [P, LOW], I32), sbl("highs_i", [P, HIGH], I32)
                lanes, highs = sbl("lanes", [P, LOW], mybir.dt.float16), sbl("highs", [P, HIGH])
                src_row = [sbl(f"src_row{k}", [P, BATCH], U32) for k in range(2)]
                dst_row = [sbl(f"dst_row{k}", [P, BATCH], U32) for k in range(2)]
                bits = [sbl(f"bits{k}", [P, 2, BATCH], I32) for k in range(2)]
                low = [sbl(f"low{k}", [P, 2, BATCH]) for k in range(2)]
                is_high = [sbl(f"is_high{k}", [P, BATCH, HIGH], BF16) for k in range(2)]
                from_src = [sbl(f"from_src{k}", [P, BATCH, F]) for k in range(2)]
                from_dst = [sbl(f"from_dst{k}", [P, BATCH, 2 * HEADS]) for k in range(2)]
                score, steep = sbl("score", [P, BATCH, HEADS]), sbl("steep", [P, BATCH, HEADS])
                feat = sbl("feat", [P, BATCH, F])
                parts = [sbl(f"parts{k}", [P, 3, BATCH, F], BF16) for k in range(2)]
                is_low = [sbl(f"is_low{r}", [P, LOW], BF16) for r in range(RING)]
                spread = [sbl(f"spread{r}", [P, 3, HIGH, F], BF16) for r in range(RING)]
                nothing = sbl("nothing", [P, 512], BF16)
                s_iota, s_idx, s_feat, s_exp = sem("iota"), sem("indices"), sem("features"), sem("exp")
                s_gs, s_gd = core.edges_gathered[0:2], core.edges_gathered[2:4]
                s_hot, s_sum, s_agg = sem("one_hots"), sem("summed"), sem("collected")
                IDX, FEAT = 7, 10
                sums = core.bank

                with nc.Block() as block:
                    @block.gpsimd
                    def _(pool):
                        pool.iota(lanes_i[:, :], pattern=[[1, LOW]], base=0, channel_multiplier=0).then_inc(s_iota, 1)
                        pool.iota(highs_i[:, :], pattern=[[1, HIGH]], base=0, channel_multiplier=0).then_inc(s_iota, 1)
                        with pool.Fori(0, BATCHES // 2) as i:
                            for k in range(2):
                                m = i * 2 + k
                                hold(pool, s_idx, m * IDX + IDX + 2)
                                hold(pool, s_feat, m * FEAT)
                                for c in range(BATCH):
                                    for rows, table, idx, s in ((from_src, 0, src_row, s_gs), (from_dst, 1, dst_row, s_gd)):
                                        pool.indirect_dma_start(
                                            out=rows[k][:, c, :], out_offset=None, in_=scratch[table][:, :],
                                            in_offset=bass.IndirectOffsetOnAxis(ap=idx[k][:, c:c + 1], axis=0)
                                            ).then_inc(s[k], 16)

                    @block.vector
                    def _(dve):
                        dve.memset(nothing[:, :], 0.0).then_inc(s_idx, 1)
                        dve.wait_ge(s_iota, 2)
                        dve.tensor_copy(lanes[:, :], lanes_i[:, :]).then_inc(s_iota, 1)
                        dve.tensor_copy(highs[:, :], highs_i[:, :]).then_inc(s_iota, 1)
                        dve.memset(src[:, EDGE_COLS:], 0).then_inc(s_iota, 1)
                        dve.memset(dst[:, EDGE_COLS:], 0).then_inc(s_iota, 1)
                        dve.sem_inc(s_feat, FEAT)
                        dve.wait_ge(s_iota, 6)
                        dve.sem_inc(s_idx, 1)
                        dve.wait_ge(s_idx, 2)

                        def indices(m, k):
                            cols = bass.ds(m * BATCH, BATCH)
                            base = m * IDX + 2
                            dve.tensor_scalar(src_row[k][:, :], src[:, cols], TOKENS - 1, None, ALU.min).then_inc(s_idx, 1)
                            dve.tensor_scalar(dst_row[k][:, :], dst[:, cols], TOKENS - 1, None, ALU.min).then_inc(s_idx, 1)
                            dve.tensor_scalar(bits[k][:, 0, :], dst[:, cols], LOW - 1, None, ALU.bitwise_and).then_inc(s_idx, 1)
                            dve.tensor_scalar(bits[k][:, 1, :], dst[:, cols], LOW.bit_length() - 1, None,
                                              ALU.logical_shift_right).then_inc(s_idx, 1)
                            hold(dve, s_idx, base + 4)
                            dve.tensor_copy(low[k][:, :, :], bits[k][:, :, :]).then_inc(s_idx, 1)
                            hold(dve, s_idx, base + 5)
                            dve.tensor_tensor(is_high[k][:, :, :],
                                              low[k][:, 1, :].unsqueeze(2).to_broadcast([P, BATCH, HIGH]),
                                              highs[:, :].unsqueeze(1).to_broadcast([P, BATCH, HIGH]),
                                              ALU.is_equal).then_inc(s_idx, 2)

                        indices(0, 0)
                        with dve.Fori(0, BATCHES // 2) as i:
                            for k in range(2):
                                m = i * 2 + k
                                if k == 1:
                                    hold(dve, s_gs[0], i * (BATCH * 16) + BATCH * 16)
                                    hold(dve, s_gd[0], i * (BATCH * 16) + BATCH * 16)
                                else:
                                    hold(dve, s_gs[1], i * (BATCH * 16))
                                    hold(dve, s_gd[1], i * (BATCH * 16))
                                hold(dve, s_hot, m * (2 * BATCH))
                                indices(m + 1, (k + 1) % 2)
                                hold(dve, s_gs[k], i * (BATCH * 16) + BATCH * 16)
                                hold(dve, s_gd[k], i * (BATCH * 16) + BATCH * 16)
                                base = m * FEAT + FEAT
                                weights, messages = feat[:, :, 0:HEADS], feat[:, :, HEADS:F]
                                dve.tensor_tensor(score[:, :, :], from_src[k][:, :, 0:HEADS],
                                                  from_dst[k][:, :, 0:HEADS], ALU.add).then_inc(s_feat, 1)
                                hold(dve, s_feat, base + 1)
                                dve.scalar_tensor_tensor(out=steep[:, :, :], in0=score[:, :, :], scalar=0.2,
                                                         in1=score[:, :, :], op0=ALU.mult, op1=ALU.max).then_inc(s_feat, 1)
                                hold(dve, s_feat, base + 2)
                                dve.tensor_tensor(steep[:, :, :], steep[:, :, :], from_dst[k][:, :, HEADS:2 * HEADS],
                                                  ALU.subtract).then_inc(s_feat, 1)
                                hold(dve, s_exp, m + 1)
                                dve.tensor_tensor(messages.rearrange("p c (h e) -> p c h e", h=HEADS),
                                                  from_src[k][:, :, HEADS:F].rearrange("p c (h e) -> p c h e", h=HEADS),
                                                  weights.unsqueeze(3).to_broadcast([P, BATCH, HEADS, X]), ALU.mult).then_inc(s_feat, 1)
                                hold(dve, s_feat, base + 4)
                                hold(dve, s_hot, m * (2 * BATCH))
                                dve.tensor_copy(parts[k][:, 0, :, :], feat[:, :, :]).then_inc(s_feat, 1)
                                hold(dve, s_feat, base + 5)
                                dve.tensor_tensor(feat[:, :, :], feat[:, :, :], parts[k][:, 0, :, :],
                                                  ALU.subtract).then_inc(s_feat, 1)
                                hold(dve, s_feat, base + 6)
                                dve.tensor_copy(parts[k][:, 1, :, :], feat[:, :, :]).then_inc(s_feat, 1)
                                hold(dve, s_feat, base + 7)
                                dve.tensor_tensor(parts[k][:, 2, :, :], feat[:, :, :], parts[k][:, 1, :, :],
                                                  ALU.subtract).then_inc(s_feat, 3)
                                hold(dve, s_feat, base + 10)
                                hold(dve, s_idx, m * IDX + 2 + IDX)
                                for c in range(BATCH):
                                    hold(dve, s_sum, m * BATCH + c + 1)
                                    dve.tensor_scalar(is_low[c % RING][:, :], lanes[:, :], low[k][:, 0, c:c + 1], None,
                                                      ALU.is_equal).then_inc(s_hot, 1)
                                    dve.tensor_tensor(
                                        spread[c % RING][:, :, :, :],
                                        parts[k][:, :, c, :].unsqueeze(2).to_broadcast([P, 3, HIGH, F]),
                                        is_high[k][:, c, :].unsqueeze(1).unsqueeze(3).to_broadcast([P, 3, HIGH, F]),
                                        ALU.mult).then_inc(s_hot, 1)

                        dve.wait_ge(s_sum, EDGE_COLS + RING + 1)
                        by_block = agg[:, :, :].rearrange("p (h b) f -> p h b f", b=BLOCKS)
                        steps = 0
                        for q in range(3):
                            for b in range(BLOCKS):
                                piece = sums[b][:, q * HIGH * F:(q + 1) * HIGH * F].rearrange("p (h f) -> p h f", h=HIGH)
                                here = by_block[:, :, b, :]
                                if q == 0:
                                    dve.tensor_copy(here, piece).then_inc(s_agg, 1)
                                else:
                                    dve.tensor_tensor(here, here, piece, ALU.add).then_inc(s_agg, 1)
                                steps += 1
                            dve.wait_ge(s_agg, steps)

                    @block.scalar
                    def _(act):
                        with act.Fori(0, BATCHES) as m:
                            hold(act, s_feat, m * FEAT + FEAT + 3)
                            act.activation(feat[:, :, 0:HEADS], steep[:, :, :], ACT.Exp).then_inc(s_exp, 1)

                    @block.tensor
                    def _(pe):
                        pe.wait_ge(s_idx, 2)
                        pe.sem_inc(s_sum, RING)
                        for b in range(BLOCKS):
                            pe.matmul(sums[b][:, 0:COLS], nothing[:, 0:P], nothing[:, 0:COLS], start=True, stop=False)
                        with pe.Fori(0, EDGE_COLS // RING) as i:
                            for r in range(RING):
                                hold(pe, s_hot, (i * RING + r) * 2 + 2)
                                for b in range(BLOCKS):
                                    last = pe.matmul(sums[b][:, 0:COLS], is_low[r][:, b * P:(b + 1) * P],
                                                     spread[r][:, :, :, :].rearrange("p q h f -> p (q h f)"),
                                                     start=False, stop=False)
                                last.then_inc(s_sum, 1)
                        for b in range(BLOCKS):
                            last = pe.matmul(sums[b][:, 0:COLS], nothing[:, 0:P], nothing[:, 0:COLS], start=False, stop=True)
                        last.then_inc(s_sum, 1)

            own_w = sbe("own_w", [P, ALL_TILES, HEADS])
            tmp_w = sbe("tmp_w", [P, ALL_TILES, HEADS])
            mean, var, std = sbe("mean", [P, ALL_TILES]), sbe("var", [P, ALL_TILES]), sbe("std", [P, ALL_TILES])
            scores = sbe("scores", [P, ALL_TILES, X])
            s_fin, s_root = sem("finish_step"), sem("finish_act")
            whole = [P, ALL_TILES, HX]
            marks = {}
            with nc.Block() as block:
                @block.vector
                def _(dve):
                    steps = 0

                    def then(ins):
                        nonlocal steps
                        steps += 1
                        ins.then_inc(s_fin, 1)
                        dve.wait_ge(s_fin, steps)

                    def heads_of(ap):
                        return ap.rearrange("p t (h e) -> p (t h) e", h=HEADS)

                    def spread_heads(ap):
                        return ap.rearrange("p t h -> p (t h)").unsqueeze(2).to_broadcast([P, ALL_TILES * HEADS, X])

                    sums_w, sums_m = agg[:, :, 0:HEADS], agg[:, :, HEADS:F]
                    then(dve.tensor_tensor(tmp_w[:, :, :], source[:, :, 0:HEADS], target[:, :, 0:HEADS], ALU.add))
                    then(dve.scalar_tensor_tensor(out=own_w[:, :, :], in0=tmp_w[:, :, :], scalar=0.2, in1=tmp_w[:, :, :],
                                                  op0=ALU.mult, op1=ALU.max))
                    then(dve.tensor_tensor(own_w[:, :, :], own_w[:, :, :], target[:, :, HEADS:2 * HEADS], ALU.subtract))
                    marks["own"] = steps
                    dve.wait_ge(s_root, 1)
                    then(dve.tensor_copy(prod[:, :, :], source[:, :, HEADS:F]))
                    then(dve.tensor_tensor(heads_of(prod[:, :, :]), heads_of(prod[:, :, :]), spread_heads(own_w[:, :, :]),
                                           ALU.mult))
                    then(dve.tensor_tensor(prod[:, :, :], prod[:, :, :], sums_m, ALU.add))
                    then(dve.tensor_tensor(own_w[:, :, :], own_w[:, :, :], sums_w, ALU.add))
                    then(dve.reciprocal(own_w[:, :, :], own_w[:, :, :]))
                    then(dve.tensor_tensor(heads_of(prod[:, :, :]), heads_of(prod[:, :, :]), spread_heads(own_w[:, :, :]),
                                           ALU.mult))

                    def rowwise(vec):
                        return vec.unsqueeze(1).to_broadcast(whole)

                    then(dve.tensor_tensor(prod[:, :, :], prod[:, :, :], rowwise(post[:, 0, :]), ALU.add))
                    then(dve.tensor_reduce(mean[:, :], prod[:, :, :], AX_X, ALU.add))
                    then(dve.tensor_scalar(mean[:, :], mean[:, :], 1.0 / HX, None, ALU.mult))
                    then(dve.tensor_tensor(prod[:, :, :], prod[:, :, :], mean[:, :].unsqueeze(2).to_broadcast(whole),
                                           ALU.subtract))
                    squares = agg[:, :, HEADS:F]
                    then(dve.tensor_tensor(squares, prod[:, :, :], prod[:, :, :], ALU.mult))
                    then(dve.tensor_reduce(var[:, :], squares, AX_X, ALU.add))
                    then(dve.tensor_scalar(var[:, :], var[:, :], 1.0 / HX, EPS, ALU.mult, ALU.add))
                    marks["var"] = steps
                    dve.wait_ge(s_root, 2)
                    then(dve.reciprocal(std[:, :], std[:, :]))
                    then(dve.tensor_tensor(prod[:, :, :], prod[:, :, :], std[:, :].unsqueeze(2).to_broadcast(whole), ALU.mult))
                    then(dve.tensor_tensor(prod[:, :, :], prod[:, :, :], rowwise(post[:, 1, :]), ALU.mult))
                    then(dve.tensor_tensor(prod[:, :, :], prod[:, :, :], rowwise(post[:, 2, :]), ALU.add))
                    then(dve.tensor_reduce(scores[:, :, :], prod[:, :, :].rearrange("p t (h e) -> p t e h", h=HEADS),
                                           AX_X, ALU.add))
                    then(dve.tensor_scalar(scores[:, :, :], scores[:, :, :], 1.0 / HEADS, None, ALU.mult))

                @block.scalar
                def _(act):
                    act.wait_ge(s_fin, marks["own"])
                    act.activation(own_w[:, :, :], own_w[:, :, :], ACT.Exp).then_inc(s_root, 1)
                    act.wait_ge(s_fin, marks["var"])
                    act.activation(std[:, :], var[:, :], ACT.Sqrt).then_inc(s_root, 1)
            top_two_gates(core, "f0", scores, gates, X, -MINUS_BIG)
        gelu_experts(core, "f0m", xT, w1_in, b1_in, w2_in, b2_in, gates, core.x)


def tropical_layer(core, wt_in, cols_in, sl_cvx_in, of_cvx_in, sl_ccv_in, of_ccv_in, wc_in, wg_in, wd_in, bd_in):
    nc = core.nc
    _, FC, _ = wt_in.shape
    PIECES = sl_cvx_in.shape[2]
    STEP = 4
    LOWEST = -3.0e38
    row_statistics(core, core.x)
    with ExitStack() as own:
        def sb(name, shape, dt=F32):
            return own.enter_context(nc.sbuf_tensor(f"f1_{name}", shape, dt))

        def sem(name):
            return core.sem(f"f1_{name}")

        xT = sb("xT", [P, GRAPHS, NODES])
        normed_transposed(core, "f1n", core.x, xT)
        part = [sb(f"part{q}", [P, GRAPHS, NODES], BF16) for q in range(3)]
        wt = sb("wt", [P, FC, D])
        cols = sb("cols", [P, 4, FC])
        sl_cvx, of_cvx, sl_ccv, of_ccv = (sb(s, [P, FC, PIECES]) for s in ("sl_cvx", "of_cvx", "sl_ccv", "of_ccv"))
        wc, wg, wd, bd = sb("wc", [P, FC, P]), sb("wg", [P, FC, P]), sb("wd", [P, FC, D]), sb("bd", [1, D])
        mix, one_less_mix = sb("mix", [P, FC]), sb("one_less_mix", [P, FC])
        s_w, s_split, s_mix = sem("w"), sem("split"), sem("mix")
        loads = ((wt, wt_in), (cols, cols_in), (sl_cvx, sl_cvx_in), (of_cvx, of_cvx_in), (sl_ccv, sl_ccv_in),
                 (of_ccv, of_ccv_in), (wc, wc_in), (wg, wg_in), (wd, wd_in), (bd, bd_in))

        with ExitStack() as early, nc.Block() as block:
            rest = early.enter_context(nc.sbuf_tensor("f1_rest", [P, GRAPHS // 4, NODES], F32))

            @block.sync
            def _(sp):
                for dst, src in loads:
                    sp.dma_start(dst[:], src).then_inc(s_w, 16)
                sp.wait_ge(s_w, 16 * len(loads))

            @block.scalar
            def _(act):
                act.wait_ge(s_w, 16 * len(loads))
                act.activation(mix[:, :], cols[:, 1, :], ACT.Sigmoid).then_inc(s_mix, 1)

            @block.vector
            def _(dve):
                dve.wait_ge(s_mix, 1)
                dve.tensor_scalar(one_less_mix[:, :], mix[:, :], -1.0, 1.0, ALU.mult, ALU.add).then_inc(s_mix, 1)
                steps = 0
                for g in range(0, GRAPHS, GRAPHS // 4):
                    block_of = slice(g, g + GRAPHS // 4)
                    whole, (high, mid, low) = xT[:, block_of, :], (p[:, block_of, :] for p in part)
                    for ins in (lambda: dve.tensor_copy(high, whole),
                                lambda: dve.tensor_tensor(rest[:, :, :], whole, high, ALU.subtract),
                                lambda: dve.tensor_copy(mid, rest[:, :, :]),
                                lambda: dve.tensor_tensor(low, rest[:, :, :], mid, ALU.subtract)):
                        ins().then_inc(s_split, 1)
                        steps += 1
                        dve.wait_ge(s_split, steps)

        acc, z = sb("acc", [P, FC, NODES]), sb("z", [P, FC, NODES])
        piece = [sb(f"piece{r}", [P, NODES]) for r in range(2)]
        cvx, ccv = sb("cvx", [P, FC, NODES]), sb("ccv", [P, FC, NODES])
        classic, gate = sb("classic", [P, FC, NODES]), sb("gate", [P, FC, NODES])
        trop, fused = sb("trop", [P, FC, NODES]), sb("fused", [P, FC, NODES])
        s_cast, s_max, s_z = sem("spread"), sem("max_plus"), sem("z")
        s_acc0, s_env0 = sem("acc_cleared"), sem("envelopes_cleared")
        s_lin, s_linc, s_piece, s_take = sem("linear"), sem("linear_copied"), sem("piece"), sem("piece_taken")
        s_trop, s_fuse, s_out, s_add = sem("tropical"), sem("fused"), sem("out"), sem("added")
        cast, lin, out_bank = core.bank[0:4], core.bank[4:6], core.bank[6]
        AHEAD = STEP * FC
        TURNS = D // STEP // FC
        assert TURNS == PIECES
        TAKES = FC * PIECES * 2

        def turns_of(body):
            def with_loop(eng):
                body(0, True, False, False)
                body(1, True, True, False)
                with eng.Fori(2, GRAPHS) as n:
                    body(n, True, True, True)
                body(GRAPHS, False, True, True)
                body(GRAPHS + 1, False, False, True)
            return with_loop

        with nc.Block() as block:
            @block.tensor
            def _(pe):
                def body(n, now, last_one, before):
                    if now:
                        with pe.Fori(0, D // STEP) as turn:
                            for j in range(STEP):
                                d = turn * STEP + j
                                hold(pe, s_max, (n * D + d) * FC + FC)
                                row = core.ident_bf[:, bass.ds(d, 1)].to_broadcast([P, P])
                                for q in range(3):
                                    last = pe.matmul(cast[j][:, :], row,
                                                     part[q][:, bass.ds(n, 1), :].rearrange("p a m -> p (a m)"),
                                                     start=(q == 0), stop=(q == 2))
                                last.then_inc(s_cast, 1)
                    if before:
                        m = n - 2
                        hold(pe, s_fuse, (m + 1) * (FC * 4))
                        hold(pe, s_add, m)
                        for t in range(TILES):
                            o = out_bank[:, t * P:(t + 1) * P]
                            for c in range(FC):
                                pe.matmul(o, fused[:, c, t * P:(t + 1) * P], wd[:, c, :], start=(c == 0), stop=False)
                            last = pe.matmul(o, core.ones_row[:, :], bd[:, :], start=False, stop=True)
                        last.then_inc(s_out, 1)
                    if last_one:
                        m = n - 1
                        for r, w in ((0, wc), (1, wg)):
                            for c in range(FC):
                                q = r * FC + c
                                hold(pe, s_linc, m * (2 * FC) + q + 1)
                                pe.matmul(lin[q % 2][:, :], w[:, c, :],
                                          xT[:, bass.ds(m, 1), :].rearrange("p a m -> p (a m)"),
                                          start=True, stop=True).then_inc(s_lin, 1)

                turns_of(body)(pe)

            @block.vector
            def _(dve):
                dve.sem_inc(s_max, AHEAD)

                def take(m, c, p):
                    base = m * TAKES + (c * PIECES + p) * 2
                    for r, (env, op) in enumerate(((cvx, ALU.max), (ccv, ALU.min))):
                        hold(dve, s_piece, base + r + 1)
                        if r == 0:
                            hold(dve, s_take, base)
                        here = env[:, bass.ds(c, 1), :].rearrange("p a m -> p (a m)")
                        dve.tensor_tensor(here, here, piece[r][:, :], op).then_inc(s_take, 1)

                def body(n, now, last_one, before):
                    if now:
                        hold(dve, s_z, n * FC)
                        dve.memset(acc[:, :, :], LOWEST).then_inc(s_acc0, 1)
                        hold(dve, s_acc0, n + 1)
                    if last_one:
                        m = n - 1
                        hold(dve, s_trop, m * (2 * FC))
                        dve.memset(cvx[:, :, :], LOWEST).then_inc(s_env0, 1)
                        dve.memset(ccv[:, :, :], -LOWEST).then_inc(s_env0, 1)
                        hold(dve, s_env0, m * 2 + 2)
                    if now:
                        with dve.Fori(0, FC) as c_now, dve.Fori(0, TURNS) as p_now:
                            turn = c_now * TURNS + p_now
                            for j in range(STEP):
                                d = turn * STEP + j
                                done = (n * D + d) * FC
                                hold(dve, s_cast, n * D + d + 1)
                                for c in range(FC):
                                    if c % 2 == 0:
                                        hold(dve, s_max, done + (AHEAD - FC) + c + 2)
                                    dve.scalar_tensor_tensor(out=acc[:, c, :], in0=cast[j][:, :],
                                                             scalar=wt[:, c, bass.ds(d, 1)], in1=acc[:, c, :],
                                                             op0=ALU.add, op1=ALU.max).then_inc(s_max, 1)
                            if last_one:
                                take(n - 1, c_now, p_now)
                    elif last_one:
                        with dve.Fori(0, FC) as c_now, dve.Fori(0, PIECES) as p_now:
                            take(n - 1, c_now, p_now)
                    if last_one:
                        m = n - 1
                        hold(dve, s_take, m * TAKES + TAKES)
                        hold(dve, s_fuse, m * (FC * 4))
                        for c in range(FC):
                            dve.tensor_scalar(ccv[:, c, :], ccv[:, c, :], one_less_mix[:, c:c + 1], None,
                                              ALU.mult).then_inc(s_trop, 1)
                        for c in range(FC):
                            hold(dve, s_trop, m * (2 * FC) + FC + c)
                            dve.scalar_tensor_tensor(out=trop[:, c, :], in0=cvx[:, c, :], scalar=mix[:, c:c + 1],
                                                     in1=ccv[:, c, :], op0=ALU.mult, op1=ALU.add).then_inc(s_trop, 1)
                    if now:
                        hold(dve, s_max, (n + 1) * (D * FC) + AHEAD)
                        hold(dve, s_piece, n * TAKES)
                        for c in range(FC):
                            dve.tensor_scalar(z[:, c, :], acc[:, c, :], cols[:, 0, c:c + 1], None,
                                              ALU.add).then_inc(s_z, 1)
                    if before:
                        m = n - 2
                        hold(dve, s_out, m + 1)
                        xg = core.x[:, bass.ds(m * TILES, TILES), :]
                        dve.tensor_tensor(xg, out_bank[:, :].rearrange("p (t d) -> p t d", t=TILES), xg,
                                          ALU.add).then_inc(s_add, 1)

                turns_of(body)(dve)

            @block.scalar
            def _(act):
                act.sem_inc(s_linc, 2)

                def body(n, now, last_one, before):
                    if last_one:
                        m = n - 1
                        for r, func, dst in ((0, ACT.Gelu, classic), (1, ACT.Sigmoid, gate)):
                            for c in range(FC):
                                q = r * FC + c
                                hold(act, s_lin, m * (2 * FC) + q + 1)
                                if q == 0:
                                    hold(act, s_fuse, m * (FC * 4))
                                act.activation(dst[:, c, :], lin[q % 2][:, :], func, bias=cols[:, 2 + r, c:c + 1],
                                               scale=1.0).then_inc(s_linc, 1)
                    if now:
                        hold(act, s_z, n * FC + FC)
                        for c in range(FC):
                            for p in range(PIECES):
                                for r, (sl, of) in enumerate(((sl_cvx, of_cvx), (sl_ccv, of_ccv))):
                                    q = (c * PIECES + p) * 2 + r
                                    hold(act, s_take, n * TAKES + max(q - 1, 0))
                                    act.activation(piece[r][:, :], z[:, c, :], ACT.Identity, bias=of[:, c, p:p + 1],
                                                   scale=sl[:, c, p:p + 1]).then_inc(s_piece, 1)

                turns_of(body)(act)

            @block.gpsimd
            def _(pool):
                def body(n, now, last_one, before):
                    if not last_one:
                        return
                    m = n - 1
                    hold(pool, s_linc, m * (2 * FC) + 2 * FC + 2)
                    hold(pool, s_out, m)
                    for c in range(FC):
                        mark = m * (FC * 4) + c * 4
                        hold(pool, s_trop, m * (2 * FC) + FC + c + 1)
                        pool.tensor_tensor(fused[:, c, :], trop[:, c, :], gate[:, c, :], ALU.mult).then_inc(s_fuse, 1)
                        hold(pool, s_fuse, mark + 1)
                        pool.tensor_scalar(gate[:, c, :], gate[:, c, :], -1.0, 1.0, ALU.mult,
                                           ALU.add).then_inc(s_fuse, 1)
                        hold(pool, s_fuse, mark + 2)
                        pool.tensor_tensor(gate[:, c, :], gate[:, c, :], classic[:, c, :], ALU.mult).then_inc(s_fuse, 1)
                        hold(pool, s_fuse, mark + 3)
                        pool.tensor_tensor(fused[:, c, :], fused[:, c, :], gate[:, c, :], ALU.add).then_inc(s_fuse, 1)

                turns_of(body)(pool)


def memory_attention(core, wpk_in, keys_in, wq_in, wo_in, tri_in, table, heads, top):
    nc = core.nc
    H, K = heads, top
    NK = keys_in.shape[0]
    DK = keys_in.shape[2] // H
    PAIRS = 2 * H // 2
    KV = 2 * D
    ROUNDS = K
    RING = 4
    LOWEST = -3.0e38
    QSCALE = float(D) ** -0.5
    STEPS = H * TILES
    ROWS = [(i, K // (i + 1)) for i in range(K)]
    FULL = [(i, c) for i, c in ROWS if c > 2]
    TWOS, ONES = [i for i, c in ROWS if c == 2], [i for i, c in ROWS if c == 1]
    CAND = sum(c for _, c in ROWS)
    FULL_END = sum(c for _, c in FULL)
    TWOS_END = FULL_END + 2 * len(TWOS)
    SUMS = len(FULL) + 2
    RANK, CANDS, FINAL, WEIGH = 10, 3 + 2 * SUMS, 9, 5
    assert K == ROUNDS == 16 and H == 8 and 2 * DK == P and NK == P
    row_statistics(core, core.x)
    with ExitStack() as own:
        def sb(name, shape, dt=F32):
            return own.enter_context(nc.sbuf_tensor(f"f3_{name}", shape, dt))

        def sem(name):
            return core.sem(f"f3_{name}")

        wpk, wq, wo = sb("wpk", [P, PAIRS, P]), sb("wq", [P, H, D]), sb("wo", [P, H, D])
        keysT = sb("keysT", [P, PAIRS, NK])
        tri = sb("tri", [P, P], BF16)
        tri_f = sb("tri_f", [P, P])
        places_i, places = sb("places_i", [P, CAND], I32), sb("places", [P, CAND])
        offset_i, offset = sb("offset_i", [P, H, K], I32), sb("offset", [P, H, K])
        s_w, s_const, s_kt, s_ktc = sem("w"), sem("constants"), sem("keys_turned"), sem("keys_copied")
        with ExitStack() as early, nc.Block() as block:
            keys = early.enter_context(nc.sbuf_tensor("f3_keys", [NK, 2, H * DK], F32))
            keys_p = keys[:, :, :].rearrange("k p (a c) -> k (p a) c", c=P)

            @block.sync
            def _(sp):
                for dst, src in ((wpk, wpk_in), (wq, wq_in), (wo, wo_in), (keys, keys_in), (tri_f, tri_in)):
                    sp.dma_start(dst[:], src).then_inc(s_w, 16)
                sp.wait_ge(s_w, 80)

            @block.gpsimd
            def _(pool):
                pool.iota(places_i[:, :], pattern=[[1, CAND]], base=0, channel_multiplier=0).then_inc(s_const, 1)
                pool.iota(offset_i[:, :, :], pattern=[[NK, H], [0, K]], base=0, channel_multiplier=0).then_inc(s_const, 1)

            @block.vector
            def _(dve):
                dve.wait_ge(s_const, 2)
                dve.wait_ge(s_w, 80)
                dve.tensor_copy(places[:, :], places_i[:, :]).then_inc(s_const, 1)
                dve.tensor_scalar(offset[:, :, :], offset_i[:, :, :], float(NK), None, ALU.mult).then_inc(s_const, 1)
                dve.tensor_copy(tri[:, :], tri_f[:, :]).then_inc(s_const, 1)

            @block.tensor
            def _(pe):
                pe.wait_ge(s_w, 80)
                for half in range(2):
                    for a in range(4):
                        last = pe.transpose(core.bank[half][:, a * P:(a + 1) * P], keys_p[:, half * 4 + a, :],
                                            core.ident[:, :])
                    last.then_inc(s_kt, 1)

            @block.scalar
            def _(act):
                for half in range(2):
                    act.wait_ge(s_kt, half + 1)
                    act.activation(keysT[:, half * 4:half * 4 + 4, :].rearrange("p a k -> p (a k)"),
                                   core.bank[half][:, :], ACT.Copy).then_inc(s_ktc, 1)

        xn, xnT = sb("xn", [P, D]), sb("xnT", [P, P])
        qT = sb("qT", [P, PAIRS, P])
        work = [sb(f"work{p}", [P, NK]) for p in range(2)]
        best = sb("best", [P, 2, H, K])
        place = sb("place", [P, 2, H, K], U32)
        place_f = sb("place_f", [P, 2, H, K])
        cand, cand_row = sb("cand", [P, H, CAND]), sb("cand_row", [P, H, CAND])
        work2 = sb("work2", [P, CAND])
        final = sb("final", [P, H, K])
        pos, pos_f = sb("pos", [P, K], U32), sb("pos_f", [P, K])
        same = sb("same", [P, K, CAND])
        row_f = sb("row_f", [P, H, K])
        total = sb("total", [P, H])
        weight = [sb(f"weight{k}", [P, H, K]) for k in range(2)]
        rows = [sb(f"rows{k}", [P, H, K], U32) for k in range(2)]
        ring = [sb(f"ring{r}", [P, H, KV]) for r in range(RING)]
        kv = [sb(f"kv{k}", [P, H, KV]) for k in range(2)]
        kT_new, kT = sb("kT_new", [P, H, NODES]), sb("kT", [P, H, NODES])
        v_new, v = sb("v_new", [P, TILES, H, D]), sb("v", [P, TILES, H, D])
        axn, axnT = sb("axn", [P, TILES, D]), sb("axnT", [P, NODES])
        qh = sb("qh", [P, NODES])
        ntop, den, rden = sb("ntop", [P, STEPS]), sb("den", [P, STEPS]), sb("rden", [P, STEPS])
        prob, probT = sb("prob", [P, NODES]), sb("probT", [P, NODES])
        o, oT = sb("o", [P, D]), sb("oT", [P, TILES, P])

        s_xn, s_q, s_qc = sem("xn"), sem("q_bank"), sem("q_bank_copied")
        s_sim, s_rank, s_cand, s_final = sem("sim"), sem("ranked"), sem("candidates"), sem("final")
        s_wt, s_wexp, s_rows, s_acc = sem("weigh"), sem("weigh_exp"), sem("rows_ready"), sem("accumulated")
        s_land = core.memory_gathered[0:RING]
        s_v, s_turnover = sem("v_copied"), sem("turnover")
        s_axn, s_m, s_mc = sem("axn"), sem("misc_bank"), sem("misc_bank_copied")
        s_s, s_top, s_p, s_pT, s_pTc = sem("scores"), sem("top"), sem("prob"), sem("probT"), sem("probT_copied")
        s_pv, s_rd, s_o, s_out, s_add = sem("pv"), sem("rden"), sem("o"), sem("out"), sem("added")
        sim, q_bank, s_bank, t_bank, o_bank, m_bank, out_bank = core.bank[0:2], *core.bank[2:8]
        Q_TILE = 5
        M_GRAPH = 1 + H + STEPS

        def use_q(h):
            return 1 + h + max(TILES * h - 1, 0)

        def use_o(g):
            return 1 + min((g + 1) // TILES + 1, H) + g

        def program(eng_body):
            def run(eng, prologue=None):
                if prologue:
                    prologue()
                eng_body(0, True, False, True)
                with eng.Fori(1, GRAPHS - 1) as n:
                    eng_body(n, True, True, True)
                eng_body(GRAPHS - 1, True, True, False)
                eng_body(GRAPHS, False, True, False)
            return run

        RANK_ROUND = {k: k - 1 for k in range(1, 9)}
        FINAL_ROUND = {10: (0, 1), 11: (2, 3), 12: (4,), 13: (5,), 14: (6,), 15: (7,)}

        with nc.Block() as block:
            @block.gpsimd
            def _(pool):
                with pool.Fori(0, ALL_TILES // 2) as i:
                    for b in range(2):
                        tile = i * 2 + b
                        hold(pool, s_rows, tile + 1)
                        for k in range(ROUNDS):
                            hold(pool, s_acc, (tile * ROUNDS + k + 1) * H)
                            for h in range(H):
                                pool.indirect_dma_start(
                                    out=ring[k % RING][:, h, :], out_offset=None, in_=table[:, :],
                                    in_offset=bass.IndirectOffsetOnAxis(ap=rows[b][:, h, k:k + 1], axis=0)
                                    ).then_inc(s_land[k % RING], 16)

            @block.vector
            def _(dve):
                def prepare(T, first=False):
                    if not first:
                        hold(dve, s_q, T * Q_TILE - 2)
                    dve.tensor_scalar(xn[:, :], core.x[:, bass.ds(T, 1), :].rearrange("p a d -> p (a d)"),
                                      core.mean[:, bass.ds(T, 1)], core.rstd[:, bass.ds(T, 1)],
                                      ALU.subtract, ALU.mult).then_inc(s_xn, 1)

                def rank(T, h):
                    base = (T * H + h) * RANK + RANK
                    hold(dve, s_sim, T * H + h + 1)
                    if h == 0:
                        hold(dve, s_cand, T * CANDS)
                    sims = [sim[h % 2][:, p * NK:(p + 1) * NK] for p in range(2)]
                    for p in range(2):
                        dve.max(best[:, p, h, 0:8], sims[p]).then_inc(s_rank, 1)
                    hold(dve, s_rank, base + 2)
                    for p in range(2):
                        dve.max_index(place[:, p, h, 0:8], best[:, p, h, 0:8], sims[p]).then_inc(s_rank, 1)
                    for p in range(2):
                        dve.match_replace(work[p][:, :], best[:, p, h, 0:8], sims[p], LOWEST).then_inc(s_rank, 1)
                    hold(dve, s_rank, base + 6)
                    for p in range(2):
                        dve.max(best[:, p, h, 8:16], work[p][:, :]).then_inc(s_rank, 1)
                    hold(dve, s_rank, base + 8)
                    for p in range(2):
                        dve.max_index(place[:, p, h, 8:16], best[:, p, h, 8:16], work[p][:, :]).then_inc(s_rank, 1)
                    hold(dve, s_rank, base + 10)

                def candidates(T):
                    base = T * CANDS
                    hold(dve, s_final, T * (H * FINAL))
                    dve.tensor_copy(place_f[:, :, :, :], place[:, :, :, :]).then_inc(s_cand, 1)
                    hold(dve, s_cand, base + 1)
                    dve.tensor_scalar(place_f[:, 1, :, :], place_f[:, 1, :, :], float(NK), None, ALU.mult).then_inc(s_cand, 1)
                    dve.tensor_tensor(place_f[:, 0, :, :], place_f[:, 0, :, :], offset[:, :, :], ALU.add).then_inc(s_cand, 1)
                    hold(dve, s_cand, base + 3)
                    for out, of in ((cand, best), (cand_row, place_f)):
                        first, second = of[:, 0, :, :], of[:, 1, :, :]
                        at = 0
                        for i, c in FULL:
                            dve.tensor_tensor(out[:, :, at:at + c], first[:, :, i:i + 1].to_broadcast([P, H, c]),
                                              second[:, :, 0:c], ALU.add).then_inc(s_cand, 1)
                            at += c
                        n2 = len(TWOS)
                        dve.tensor_tensor(
                            out[:, :, FULL_END:TWOS_END].rearrange("p h (i j) -> p h i j", j=2),
                            first[:, :, TWOS[0]:TWOS[0] + n2].unsqueeze(3).to_broadcast([P, H, n2, 2]),
                            second[:, :, 0:2].unsqueeze(2).to_broadcast([P, H, n2, 2]), ALU.add).then_inc(s_cand, 1)
                        dve.tensor_tensor(out[:, :, TWOS_END:CAND], first[:, :, ONES[0]:K],
                                          second[:, :, 0:1].to_broadcast([P, H, len(ONES)]), ALU.add).then_inc(s_cand, 1)
                    hold(dve, s_cand, base + CANDS)

                def finals(T, h):
                    base = (T * H + h) * FINAL
                    if h == 0:
                        hold(dve, s_wt, T * WEIGH)
                    hold(dve, s_final, base)
                    dve.max(final[:, h, 0:8], cand[:, h, :]).then_inc(s_final, 1)
                    hold(dve, s_final, base + 1)
                    dve.max_index(pos[:, 0:8], final[:, h, 0:8], cand[:, h, :]).then_inc(s_final, 1)
                    dve.match_replace(work2[:, :], final[:, h, 0:8], cand[:, h, :], LOWEST).then_inc(s_final, 1)
                    hold(dve, s_final, base + 3)
                    dve.max(final[:, h, 8:16], work2[:, :]).then_inc(s_final, 1)
                    hold(dve, s_final, base + 4)
                    dve.max_index(pos[:, 8:16], final[:, h, 8:16], work2[:, :]).then_inc(s_final, 1)
                    hold(dve, s_final, base + 5)
                    dve.tensor_copy(pos_f[:, :], pos[:, :]).then_inc(s_final, 1)
                    hold(dve, s_final, base + 6)
                    dve.tensor_tensor(same[:, :, :], places[:, :].unsqueeze(1).to_broadcast([P, K, CAND]),
                                      pos_f[:, :].unsqueeze(2).to_broadcast([P, K, CAND]), ALU.is_equal).then_inc(s_final, 1)
                    hold(dve, s_final, base + 7)
                    dve.tensor_tensor(same[:, :, :], same[:, :, :],
                                      cand_row[:, h, :].unsqueeze(1).to_broadcast([P, K, CAND]), ALU.mult).then_inc(s_final, 1)
                    hold(dve, s_final, base + 8)
                    dve.tensor_reduce(row_f[:, h, :], same[:, :, :], AX_X, ALU.add).then_inc(s_final, 1)

                def weigh(T, b):
                    base = T * WEIGH
                    hold(dve, s_final, (T + 1) * (H * FINAL))
                    dve.tensor_copy(rows[b][:, :, :], row_f[:, :, :]).then_inc(s_rows, 1)
                    dve.tensor_tensor(weight[b][:, :, :], final[:, :, :], final[:, :, 0:1].to_broadcast([P, H, K]),
                                      ALU.subtract).then_inc(s_wt, 1)
                    hold(dve, s_wexp, T + 1)
                    dve.tensor_reduce(total[:, :], weight[b][:, :, :], AX_X, ALU.add).then_inc(s_wt, 1)
                    hold(dve, s_wt, base + 2)
                    dve.reciprocal(total[:, :], total[:, :]).then_inc(s_wt, 1)
                    hold(dve, s_wt, base + 3)
                    dve.tensor_tensor(weight[b][:, :, :], weight[b][:, :, :],
                                      total[:, :].unsqueeze(2).to_broadcast([P, H, K]), ALU.mult).then_inc(s_wt, 2)
                    hold(dve, s_wt, base + 5)
                    hold(dve, s_rows, T + 1)

                def add_rows(T, b, k):
                    hold(dve, s_land[k % RING], T * (ROUNDS // RING * H * 16) + (k // RING + 1) * (H * 16))
                    hold(dve, s_acc, (T * ROUNDS + k + RING) * H)
                    if k == 0:
                        hold(dve, s_v, T)
                    for h in range(H):
                        row, w = ring[k % RING][:, h, :], weight[b][:, h, k:k + 1]
                        if k == 0:
                            dve.tensor_scalar(kv[b][:, h, :], row, w, None, ALU.mult).then_inc(s_acc, 1)
                        else:
                            dve.scalar_tensor_tensor(out=kv[b][:, h, :], in0=row, scalar=w, in1=kv[b][:, h, :],
                                                     op0=ALU.mult, op1=ALU.add).then_inc(s_acc, 1)

                def scale_out(m, g):
                    hold(dve, s_p, m * STEPS + g + 1)
                    dve.reciprocal(rden[:, g:g + 1], den[:, g:g + 1]).then_inc(s_rd, 1)
                    hold(dve, s_rd, m * STEPS + g + 1)
                    hold(dve, s_pv, m * STEPS + g + 1)
                    hold(dve, s_m, m * M_GRAPH + (use_o(g - 1) + 1 if g else 0))
                    dve.tensor_scalar(o[:, :], o_bank[:, 0:D], rden[:, g:g + 1], None, ALU.mult).then_inc(s_o, 1)

                def add_out(m, h):
                    hold(dve, s_out, m * H + h + 1)
                    hold(dve, s_add, m * H + h)
                    xg = core.x[:, bass.ds(m * TILES, TILES), :]
                    dve.tensor_tensor(xg, out_bank[:, :].rearrange("p (t d) -> p t d", t=TILES), xg,
                                      ALU.add).then_inc(s_add, 1)

                def attend(m, t, k):
                    g = t * (STEPS // TILES) + k // 2
                    h, i = divmod(g, TILES)
                    n_cols = (i + 1) * P
                    if k % 2 == 0:
                        hold(dve, s_s, m * STEPS + g + 1)
                        dve.tensor_reduce(ntop[:, g:g + 1], s_bank[:, 0:n_cols], AX_X, ALU.max, negate=True).then_inc(s_top, 1)
                        if g >= 1:
                            scale_out(m, g - 1)
                    else:
                        hold(dve, s_pT, m * STEPS + g + 1)
                        hold(dve, s_pv, m * STEPS + g)
                        dve.tensor_copy(probT[:, 0:n_cols], t_bank[:, 0:n_cols]).then_inc(s_pTc, 1)
                        if i == 1 and h >= 1:
                            add_out(m, h - 1)

                def body(n, now, attention, ahead):
                    m = n - 1
                    if attention:
                        hold(dve, s_m, m * M_GRAPH)
                        for t in range(TILES):
                            tile = m * TILES + t
                            dve.tensor_scalar(axn[:, t, :], core.x[:, bass.ds(tile, 1), :].rearrange("p a d -> p (a d)"),
                                              core.mean[:, bass.ds(tile, 1)], core.rstd[:, bass.ds(tile, 1)],
                                              ALU.subtract, ALU.mult).then_inc(s_axn, 1)
                    for t in range(TILES):
                        T, b = n * TILES + t, t % 2
                        more = now and (ahead or t < TILES - 1)
                        for k in range(ROUNDS):
                            if more:
                                if k == 0:
                                    prepare(T + 1)
                                if k in RANK_ROUND:
                                    rank(T + 1, RANK_ROUND[k])
                                if k == 9:
                                    candidates(T + 1)
                                for h in FINAL_ROUND.get(k, ()):
                                    finals(T + 1, h)
                                if k == ROUNDS - 1:
                                    weigh(T + 1, 1 - b)
                            if attention:
                                attend(m, t, k)
                            if now:
                                add_rows(T, b, k)
                    if attention:
                        scale_out(m, STEPS - 1)
                        add_out(m, H - 1)

                def prologue():
                    dve.sem_inc(s_acc, RING * H)
                    dve.sem_inc(s_rank, RANK)
                    prepare(0, first=True)
                    for h in range(H):
                        rank(0, h)
                    candidates(0)
                    for h in range(H):
                        finals(0, h)
                    weigh(0, 0)

                program(body)(dve, prologue)

            @block.scalar
            def _(act):
                def q_copies(use):
                    hold(act, s_q, use + 1)
                    act.activation(xnT[:, :], q_bank[:, 0:P], ACT.Copy).then_inc(s_qc, 1)
                    for half in range(2):
                        hold(act, s_q, use + 2 + half)
                        act.activation(qT[:, half * 4:half * 4 + 4, :].rearrange("p a k -> p (a k)"), q_bank[:, :],
                                       ACT.Copy).then_inc(s_qc, 1)

                def weigh_exp(T, b):
                    hold(act, s_wt, T * WEIGH + 1)
                    act.activation(weight[b][:, :, :], weight[b][:, :, :], ACT.Exp).then_inc(s_wexp, 1)

                def copy_o(m, g):
                    h, i = divmod(g, TILES)
                    hold(act, s_m, m * M_GRAPH + use_o(g) + 1)
                    if i == 0:
                        hold(act, s_out, m * H + h)
                    act.activation(oT[:, i, :], m_bank[:, 0:P], ACT.Copy).then_inc(s_mc, 1)

                def attend(m, t, k):
                    g = t * (STEPS // TILES) + k // 2
                    h, i = divmod(g, TILES)
                    n_cols = (i + 1) * P
                    if k % 2 == 0:
                        if i == 0:
                            hold(act, s_m, m * M_GRAPH + use_q(h) + 1)
                            hold(act, s_s, m * STEPS + g)
                            act.activation(qh[:, :], m_bank[:, :], ACT.Copy, scale=QSCALE).then_inc(s_mc, 1)
                        hold(act, s_top, m * STEPS + g + 1)
                        hold(act, s_pT, m * STEPS + g)
                        act.activation(prob[:, 0:n_cols], s_bank[:, 0:n_cols], ACT.Exp, bias=ntop[:, g:g + 1], scale=1.0,
                                       accum_out=den[:, g:g + 1]).then_inc(s_p, 1)
                    elif g >= 1:
                        copy_o(m, g - 1)

                def body(n, now, attention, ahead):
                    m = n - 1
                    if attention:
                        hold(act, s_m, m * M_GRAPH + 1)
                        act.activation(axnT[:, :], m_bank[:, :], ACT.Copy).then_inc(s_mc, 1)
                    for t in range(TILES):
                        T, b = n * TILES + t, t % 2
                        more = now and (ahead or t < TILES - 1)
                        for k in range(ROUNDS):
                            if more and k == 0:
                                q_copies(T * Q_TILE + 3)
                            if more and k == ROUNDS - 1:
                                weigh_exp(T + 1, 1 - b)
                            if attention:
                                attend(m, t, k)
                        if now:
                            after = T * Q_TILE + 6
                            if t == 0:
                                hold(act, s_turnover, n * 2)
                            for half in range(2):
                                hold(act, s_q, after + half + 1 if more else T * Q_TILE + 3 + half + 1)
                                act.activation(kT_new[:, half * 4:half * 4 + 4, t * P:(t + 1) * P],
                                               q_bank[:, :].rearrange("p (a k) -> p a k", a=4), ACT.Copy).then_inc(s_qc, 1)
                            hold(act, s_acc, (T + 1) * (ROUNDS * H) + RING * H)
                            act.activation(v_new[:, t, :, :], kv[b][:, :, D:KV], ACT.Copy).then_inc(s_v, 1)
                    if attention:
                        copy_o(m, STEPS - 1)
                    if now:
                        hold(act, s_pv, n * STEPS)
                        hold(act, s_qc, (n + 1) * (TILES * Q_TILE) + 3 if ahead else (n + 1) * (TILES * Q_TILE))
                        hold(act, s_v, (n + 1) * TILES + 1)
                        act.activation(kT[:, :, :], kT_new[:, :, :], ACT.Copy).then_inc(s_turnover, 1)
                        act.activation(v[:, :, :, :], v_new[:, :, :, :], ACT.Copy).then_inc(s_turnover, 1)

                def prologue():
                    act.sem_inc(s_v, 1)
                    q_copies(0)
                    weigh_exp(0, 0)

                program(body)(act, prologue)

            @block.tensor
            def _(pe):
                def q_of(T, use):
                    hold(pe, s_xn, T + 1)
                    hold(pe, s_qc, use)
                    pe.transpose(q_bank[:, 0:P], xn[:, :], core.ident[:, :]).then_inc(s_q, 1)
                    hold(pe, s_sim, T * H)
                    for half in range(2):
                        hold(pe, s_qc, use + 1 + half)
                        for a in range(4):
                            last = pe.matmul(q_bank[:, a * P:(a + 1) * P], wpk[:, half * 4 + a, :], xnT[:, :],
                                             start=True, stop=True)
                        last.then_inc(s_q, 1)

                def sims_of(T, h, use):
                    if h == 0:
                        hold(pe, s_qc, use + 3)
                    hold(pe, s_rank, (T * H + h) * RANK)
                    at = (h % 2) * DK
                    for p in range(2):
                        pair = p * (H // 2) + h // 2
                        last = pe.matmul(sim[h % 2][:, p * NK:(p + 1) * NK], qT[at:at + DK, pair, :],
                                         keysT[at:at + DK, pair, :], start=True, stop=True)
                    last.then_inc(s_sim, 1)

                def pv(m, g):
                    h, i = divmod(g, TILES)
                    hold(pe, s_pTc, m * STEPS + g + 1)
                    hold(pe, s_o, m * STEPS + g)
                    for j in range(i + 1):
                        last = pe.matmul(o_bank[:, 0:D], probT[:, j * P:(j + 1) * P], v[:, j, h, :],
                                         start=(j == 0), stop=(j == i))
                    last.then_inc(s_pv, 1)

                def turn_o(m, g):
                    hold(pe, s_o, m * STEPS + g + 1)
                    hold(pe, s_mc, m * M_GRAPH + use_o(g))
                    pe.transpose(m_bank[:, 0:P], o[:, :], core.ident[:, :]).then_inc(s_m, 1)

                def out_of(m, h):
                    hold(pe, s_mc, m * M_GRAPH + use_o(TILES * h + TILES - 1) + 1)
                    hold(pe, s_add, m * H + h)
                    for i in range(TILES):
                        last = pe.matmul(out_bank[:, i * P:(i + 1) * P], oT[:, i, :], wo[:, h, :], start=True, stop=True)
                    last.then_inc(s_out, 1)

                def attend(m, t, k):
                    g = t * (STEPS // TILES) + k // 2
                    h, i = divmod(g, TILES)
                    if k % 2 == 0:
                        if i == 0:
                            hold(pe, s_mc, m * M_GRAPH + use_q(h))
                            pe.matmul(m_bank[:, :], wq[:, h, :], axnT[:, :], start=True, stop=True).then_inc(s_m, 1)
                            hold(pe, s_mc, m * M_GRAPH + use_q(h) + 1)
                        if i == 1 and h >= 1:
                            out_of(m, h - 1)
                        hold(pe, s_p, m * STEPS + g)
                        q = qh[:, i * P:(i + 1) * P]
                        if i:
                            pe.matmul(s_bank[:, 0:i * P], q, kT[:, h, 0:i * P], start=True, stop=True)
                        here = s_bank[:, i * P:(i + 1) * P]
                        pe.matmul(here, q, kT[:, h, i * P:(i + 1) * P], start=True, stop=False)
                        pe.matmul(here, core.ident_bf[:, :], tri[:, :], start=False, stop=True).then_inc(s_s, 1)
                        if g >= 1:
                            pv(m, g - 1)
                    else:
                        hold(pe, s_p, m * STEPS + g + 1)
                        hold(pe, s_pTc, m * STEPS + g)
                        for j in range(i + 1):
                            last = pe.transpose(t_bank[:, j * P:(j + 1) * P], prob[:, j * P:(j + 1) * P], core.ident[:, :])
                        last.then_inc(s_pT, 1)
                        if g >= 1:
                            turn_o(m, g - 1)

                def body(n, now, attention, ahead):
                    m = n - 1
                    if attention:
                        hold(pe, s_axn, (m + 1) * TILES)
                        hold(pe, s_mc, m * M_GRAPH)
                        for t in range(TILES):
                            last = pe.transpose(m_bank[:, t * P:(t + 1) * P], axn[:, t, :], core.ident[:, :])
                        last.then_inc(s_m, 1)
                        hold(pe, s_turnover, n * 2)
                    for t in range(TILES):
                        T, b = n * TILES + t, t % 2
                        more = now and (ahead or t < TILES - 1)
                        use = T * Q_TILE + 3
                        for k in range(ROUNDS):
                            if more:
                                if k == 0:
                                    q_of(T + 1, use)
                                if k in RANK_ROUND:
                                    sims_of(T + 1, RANK_ROUND[k], use)
                            if attention:
                                attend(m, t, k)
                        if now:
                            after = T * Q_TILE + 6 if more else use
                            hold(pe, s_acc, (T + 1) * (ROUNDS * H) + RING * H)
                            for half in range(2):
                                hold(pe, s_qc, after + half)
                                for a in range(4):
                                    last = pe.transpose(q_bank[:, a * P:(a + 1) * P], kv[b][:, half * 4 + a, 0:D],
                                                        core.ident[:, :])
                                last.then_inc(s_q, 1)
                    if attention:
                        pv(m, STEPS - 1)
                        turn_o(m, STEPS - 1)
                        out_of(m, H - 1)

                def prologue():
                    q_of(0, 0)
                    for h in range(H):
                        sims_of(0, h, 0)

                program(body)(pe, prologue)


def build_program(nc, io):
    with ExitStack() as ctx:
        core = Core(nc, ctx)
        with core.stage():
            load_and_constants(core, io["x"])
        with core.stage():
            attention_layer(core, io["adj"], io["head_scale"], io["gain1"], io["shift1"], io["gain2"], io["shift2"],
                            io["mlp_w1"], io["mlp_b1"], io["mlp_w2"], io["mlp_b2"], heads=8)
        with core.stage():
            edge_routed_experts(core, io["edges"], io["w_gat"], io["att"], io["post"], io["moe_w1"], io["moe_b1"],
                                io["moe_w2"], io["moe_b2"], 4, (io["source_table"], io["target_table"]))
        with core.stage():
            row_statistics(core, core.x)
            graph_layer(core, "g1", io["adj"], io["g1_w"], io["g1_row"], io["g1_col"], slope=0.2, over_rows=True,
                        elu=True, keep_neg=True)
        with core.stage():
            tropical_layer(core, io["wt"], io["trop_cols"], io["sl_cvx"], io["of_cvx"], io["sl_ccv"], io["of_ccv"],
                           io["wc"], io["wg"], io["wd"], io["bd"])
        with core.stage():
            row_statistics(core, core.x)
            graph_layer(core, "g2", io["adj"], io["g2_w"], io["g2_row"], io["g2_col"], slope=0.0, over_rows=False,
                        elu=True, keep_neg=True)
        with core.stage():
            routed_experts(core, io["router_w1"], io["router_b1"], io["router_w2"], io["router_b2"], io["experts_w"],
                           io["experts_b12"], io["experts_b3"], 6)
        with core.stage():
            row_statistics(core, core.x)
            graph_layer(core, "g3", io["adj"], io["g3_w"], io["g3_row"], io["g3_col"], slope=0.2, over_rows=False,
                        elu=False, keep_neg=False)
        with core.stage():
            memory_attention(core, io["wpk"], io["pk_keys"], io["wq"], io["wo"], io["causal"], io["table"],
                             heads=8, top=16)
        with core.stage():
            store_result(core, io["out"])


def lay_out(i):
    import numpy as np

    heads, head_dim, chunks = 8, 16, 4

    def repeated(a):
        return np.broadcast_to(a, (P,) + a.shape)

    def chunked(a):
        return a.reshape(chunks, P, -1).transpose(1, 0, 2)

    def columns(a):
        return np.repeat(a.reshape(P, 1), P, 1)

    head_scale = np.zeros((P, heads), np.float32)
    head_scale[np.arange(P), np.arange(P) // head_dim] = head_dim ** -0.5
    causal = np.where(np.arange(P)[None, :] > np.arange(P)[:, None], MINUS_BIG, 0.0).astype(np.float32)
    a1, a2 = i["L1_gnn_a"], i["L2_gnn_a"]
    return {
        "x": i["x"], "adj": i["adj"], "head_scale": head_scale,
        "gain1": repeated(i["L0_gnn_gamma1"]), "shift1": repeated(i["L0_gnn_beta1"]),
        "gain2": i["L0_gnn_gamma2"][:, None], "shift2": i["L0_gnn_beta2"][:, None],
        "mlp_w1": i["L0_gnn_W1"].reshape(P, 1, chunks, P), "mlp_b1": i["L0_gnn_b1"].reshape(1, chunks, P).transpose(2, 0, 1),
        "mlp_w2": i["L0_gnn_W2"].reshape(1, chunks, P, D).transpose(2, 0, 1, 3), "mlp_b2": i["L0_gnn_b2"].reshape(1, 1, D),
        "edges": i["L0_ffn_edge_index"].reshape(2, P, -1), "w_gat": i["L0_ffn_W_gat"],
        "att": repeated(np.stack([i["L0_ffn_att_src"].ravel(), i["L0_ffn_att_dst"].ravel()])),
        "post": repeated(np.stack([i["L0_ffn_b_gat"], i["L0_ffn_ln_gamma"], i["L0_ffn_ln_beta"]])),
        "moe_w1": i["L0_ffn_W1"].reshape(4, P, 2, P).transpose(1, 0, 2, 3),
        "moe_b1": i["L0_ffn_b1"].reshape(4, 2, P).transpose(2, 0, 1),
        "moe_w2": i["L0_ffn_W2"].reshape(4, 2, P, D).transpose(2, 0, 1, 3), "moe_b2": i["L0_ffn_b2"][None],
        "g1_w": i["L1_gnn_W"], "g1_row": columns(a1[:P]), "g1_col": a1[P:],
        "g2_w": i["L2_gnn_W"], "g2_row": columns(a2[P:]), "g2_col": a2[:P],
        "g3_w": i["L3_gnn_W"], "g3_row": columns(i["L3_gnn_a_dst"]), "g3_col": i["L3_gnn_a_src"][:, None],
        "wt": chunked(i["L1_ffn_Wt"]),
        "trop_cols": np.stack([i["L1_ffn_" + k] for k in ("bt", "alpha", "bc", "bg")]).reshape(4, chunks, P).transpose(2, 0, 1),
        "sl_cvx": chunked(i["L1_ffn_sl_cvx"]), "of_cvx": chunked(i["L1_ffn_of_cvx"]),
        "sl_ccv": chunked(i["L1_ffn_sl_ccv"]), "of_ccv": chunked(i["L1_ffn_of_ccv"]),
        "wc": i["L1_ffn_Wc"].reshape(P, chunks, P), "wg": i["L1_ffn_Wg"].reshape(P, chunks, P),
        "wd": chunked(i["L1_ffn_Wd"]), "bd": i["L1_ffn_bd"][None],
        "router_w1": i["L2_ffn_router_w1"], "router_b1": i["L2_ffn_router_b1"][:, None],
        "router_w2": i["L2_ffn_router_w2"], "router_b2": i["L2_ffn_router_b2"][None],
        "experts_w": np.stack([i["L2_ffn_expert_w1"], i["L2_ffn_expert_w2"], i["L2_ffn_expert_w3"]]).transpose(2, 0, 1, 3),
        "experts_b12": np.stack([i["L2_ffn_expert_b1"], i["L2_ffn_expert_b2"]]).transpose(2, 0, 1),
        "experts_b3": i["L2_ffn_expert_b3"][None],
        "wpk": i["L3_ffn_Wq_pk"].reshape(P, heads, P),
        "pk_keys": i["L3_ffn_pk_keys"].transpose(1, 0, 2, 3).reshape(P, 2, -1),
        "wq": i["L3_ffn_Wq"].reshape(P, heads, D), "wo": i["L3_ffn_Wo"].reshape(heads, D, D).transpose(1, 0, 2),
        "causal": causal, "table": np.concatenate([i["L3_ffn_keys_table"], i["L3_ffn_values_table"]], 1),
    }


def kernel(**inputs):
    import numpy as np
    import concourse.bacc as bacc
    from concourse.bass_utils import run_bass_kernel_spmd

    nc = bacc.Bacc("TRN2", target_bir_lowering=False, num_devices=1)
    arrays, io = {}, {}
    for name, a in lay_out({k: np.asarray(v) for k, v in inputs.items()}).items():
        a = np.ascontiguousarray(a)
        arrays[f"in_{name}"] = a
        io[name] = nc.dram_tensor(f"in_{name}", a.shape, mybir.dt.from_np(a.dtype), kind="ExternalInput").ap()
    io["source_table"] = nc.dram_tensor("source_table", (TOKENS, 20), F32, kind="Internal").ap()
    io["target_table"] = nc.dram_tensor("target_table", (TOKENS, 8), F32, kind="Internal").ap()
    io["out"] = nc.dram_tensor("out", (GRAPHS, NODES, D), F32, kind="ExternalOutput").ap()
    build_program(nc, io)
    return run_bass_kernel_spmd(nc, [arrays], core_ids=[0]).results[0]["out"]
```

```python
from contextlib import ExitStack, contextmanager

import concourse.bass as bass
from concourse import mybir

F32 = mybir.dt.float32
BF16 = mybir.dt.bfloat16
I32 = mybir.dt.int32
U32 = mybir.dt.uint32
ALU = mybir.AluOpType
ACT = mybir.ActivationFunctionType
AX_X = mybir.AxisListType.X

P = 128
D = 128
GRAPHS = 16
NODES = 512
TILES = NODES // P
ALL_TILES = GRAPHS * TILES
TOKENS = GRAPHS * NODES
EPS = 1e-5
NEG = -9000000000000000.0
MINUS_BIG = -1e30


START = 1

class Core:

    def __init__(self, nc, ctx):
        self.nc, self.ctx = nc, ctx
        self.x = self.sbuf("x_resident", [P, ALL_TILES, D], F32)
        self.ident = self.sbuf("ident", [P, P], F32)
        self.ident_bf = self.sbuf("ident_bf", [P, P], BF16)
        self.ones_row = self.sbuf("ones_row", [1, P], F32)
        self.mean = self.sbuf("mean", [P, ALL_TILES], F32)
        self.rstd = self.sbuf("rstd", [P, ALL_TILES], F32)
        self.bank = [ctx.enter_context(nc.psum_tensor(f"bank{i}", [P, 512], F32)) for i in range(8)]
        self.edges_gathered = [ctx.enter_context(nc.semaphore(f"edges_gathered{i}")) for i in range(4)]
        self.memory_gathered = [ctx.enter_context(nc.semaphore(f"memory_gathered{i}")) for i in range(4)]
        self.stages = 0
        self.serial = 0

    @contextmanager
    def stage(self):
        outer = self.ctx
        self.stages += 1
        with ExitStack() as own:
            self.ctx, self.sems, self.started = own, [], 0
            yield
            with self.nc.Block() as block:
                @block.gpsimd
                def _(pool):
                    for s in self.sems:
                        pool.sem_clear(s)
        self.ctx = outer

    @contextmanager
    def block(self):
        new, self.started = self.sems[self.started:], len(self.sems)
        with self.nc.Block() as block:
            @block.gpsimd
            def _(pool):
                for s in new:
                    pool.sem_inc(s, START)
        with self.nc.Block() as block:
            yield block

    def sbuf(self, name, shape, dt):
        return self.ctx.enter_context(self.nc.sbuf_tensor(name, shape, dt))

    def sem(self, name):
        self.sems.append(self.ctx.enter_context(self.nc.semaphore(f"s{self.stages}_{name}")))
        return self.sems[-1]


def load_and_constants(core, x_in):
    nc = core.nc
    s_x, s_zero, s_ident = core.sem("x_loaded"), core.sem("constants_cleared"), core.sem("identities_made")
    with core.block() as block:
        @block.sync
        def _(sp):
            sp.dma_start(core.x[:, :, :], x_in.rearrange("b (t p) d -> p (b t) d", p=P)).then_inc(s_x, 16)
            sp.wait_ge(s_x, START + 16)

        @block.gpsimd
        def _(pool):
            pool.memset(core.ident[:, :], 0.0).then_inc(s_zero, 1)
            pool.memset(core.ident_bf[:, :], 0.0).then_inc(s_zero, 1)
            pool.memset(core.ones_row[:, :], 1.0).then_inc(s_ident, 1)
            pool.wait_ge(s_zero, START + 2)
            for m in (core.ident, core.ident_bf):
                pool.affine_select(out=m[:, :], in_=m[:, :], compare_op=ALU.not_equal, fill=1.0, base=0,
                                   pattern=[[-1, P]], channel_multiplier=1).then_inc(s_ident, 1)


def store_result(core, out):
    nc = core.nc
    s_out = core.sem("result_stored")
    with core.block() as block:
        @block.sync
        def _(sp):
            sp.dma_start(out.rearrange("b (t p) d -> p (b t) d", p=P), core.x[:, :, :]).then_inc(s_out, 16)
            sp.wait_ge(s_out, START + 16)


def row_statistics(core, src):
    nc = core.nc
    core.serial += 1
    tag = core.serial
    s_stats, s_sqrt = core.sem(f"row_statistics{tag}"), core.sem(f"square_roots{tag}")
    with ExitStack() as own, core.block() as block:
        stats = own.enter_context(nc.sbuf_tensor(f"stats{tag}", [P, ALL_TILES, 6], F32))
        half_gap = own.enter_context(nc.sbuf_tensor(f"half_gap{tag}", [P, ALL_TILES], F32))
        var = own.enter_context(nc.sbuf_tensor(f"var{tag}", [P, ALL_TILES], F32))
        std = own.enter_context(nc.sbuf_tensor(f"std{tag}", [P, ALL_TILES], F32))
        even_mean, odd_mean = stats[:, :, 1], stats[:, :, 4]
        even_sq, odd_sq = stats[:, :, 2], stats[:, :, 5]
        steps = [0]

        @block.vector
        def _(dve):
            with dve.Fori(0, GRAPHS) as n:
                for k in range(TILES):
                    t = n * TILES + k
                    dve.bn_stats(stats[:, bass.ds(t, 1), :].rearrange("p a s -> p (a s)"),
                                 src[:, bass.ds(t, 1), :].rearrange("p a d -> p (a d)")).then_inc(s_stats, 1)
            steps[0] = ALL_TILES

            def then(ins):
                ins.then_inc(s_stats, 1)
                steps[0] += 1
                dve.wait_ge(s_stats, START + steps[0])

            dve.wait_ge(s_stats, START + steps[0])
            then(dve.tensor_tensor(core.mean[:, :], even_mean, odd_mean, ALU.add))
            then(dve.tensor_scalar(core.mean[:, :], core.mean[:, :], 0.5, None, ALU.mult))
            then(dve.tensor_tensor(half_gap[:, :], even_mean, odd_mean, ALU.subtract))
            then(dve.scalar_tensor_tensor(out=half_gap[:, :], in0=half_gap[:, :], scalar=0.25, in1=half_gap[:, :],
                                          op0=ALU.mult, op1=ALU.mult))
            then(dve.tensor_tensor(var[:, :], even_sq, odd_sq, ALU.add))
            then(dve.scalar_tensor_tensor(out=var[:, :], in0=var[:, :], scalar=1.0 / D, in1=half_gap[:, :],
                                          op0=ALU.mult, op1=ALU.add))
            then(dve.tensor_scalar(var[:, :], var[:, :], EPS, None, ALU.add))
            dve.wait_ge(s_sqrt, START + 1)
            then(dve.reciprocal(core.rstd[:, :], std[:, :]))

        @block.scalar
        def _(act):
            act.wait_ge(s_stats, START + ALL_TILES + 7)
            act.activation(std[:, :], var[:, :], ACT.Sqrt).then_inc(s_sqrt, 1)


def graph_layer(core, tag, adj, w_in, row_in, col_in, slope, over_rows, elu, keep_neg):
    nc = core.nc
    mask_value = NEG if keep_neg else MINUS_BIG
    with ExitStack() as own:
        def sb(name, shape, dt=F32):
            return own.enter_context(nc.sbuf_tensor(f"{tag}_{name}", shape, dt))

        def sem(name):
            return core.sem(f"{tag}_{name}")

        w = sb("w", [P, D])
        row_w = sb("row_w", [P, P])
        col_w = sb("col_w", [P, 1])
        adj_t = [sb(f"adj{k}", [P, TILES, NODES], I32) for k in range(2)]
        bias = [sb(f"bias{k}", [P, TILES, NODES], BF16) for k in range(2)]
        bias_use = [sb(f"bias_turned{k}", [P, TILES, NODES], BF16) for k in range(2)] if over_rows else bias
        xn = [sb(f"xn{k}", [P, TILES, D]) for k in range(2)]
        xnT = [sb(f"xnT{k}", [P, NODES]) for k in range(2)]
        h = [sb(f"h{k}", [P, TILES, D]) for k in range(2)]
        hT = [sb(f"hT{k}", [P, NODES]) for k in range(2)]
        row = [sb(f"row{k}", [P, NODES]) for k in range(2)]
        col = [sb(f"col{k}", [P, TILES]) for k in range(2)]
        e = [sb(f"e{k}", [P, NODES]) for k in range(2)]
        lk = [sb(f"leaky{k}", [P, NODES]) for k in range(2)] if slope else None
        em = [sb(f"em{k}", [P, TILES, NODES]) for k in range(2)]
        prob = [sb(f"prob{k}", [P, TILES, NODES]) for k in range(2)]
        probT = [sb(f"probT{k}", [P, TILES, NODES]) for k in range(2)] if not over_rows else None
        top = [sb(f"top{k}", [P, TILES]) for k in range(2)]
        ntop = [sb(f"ntop{k}", [P, TILES]) for k in range(2)]
        den = [sb(f"den{k}", [P, TILES]) for k in range(2)]
        rden = [sb(f"rden{k}", [P, TILES]) for k in range(2)]
        y = [sb(f"y{k}", [P, TILES, D]) for k in range(2)]
        low = [sb(f"low{k}", [P, TILES, D]) for k in range(2)]

        s_w, s_adj, s_bias, s_turn, s_biasT = sem("w"), [sem("adj0"), sem("adj1")], sem("bias"), sem("turned"), sem("biasT")
        s_xn, s_xT, s_xTc = sem("xn"), sem("xT"), sem("xTc")
        s_h, s_hTc, s_hc = sem("h"), sem("hTc"), sem("hc")
        s_sc, s_rowc, s_colc = sem("scores"), sem("rowc"), sem("colc")
        s_e, s_lk, s_em, s_nt, s_p = sem("e"), sem("leaky"), sem("em"), sem("ntop"), sem("prob")
        s_rd, s_hs = sem("rden"), sem("hs")
        s_pT, s_pTc = sem("pT"), sem("pTc")
        s_o, s_y, s_exp, s_acc = sem("o"), sem("y"), sem("expy"), sem("acc")
        b_xT, b_hT, b_h, b_row, b_col, b_o = (core.bank[i] for i in range(6))
        b_turn = [core.bank[6], core.bank[7]]

        def pairs(eng):
            return eng.Fori(0, GRAPHS // 2)

        def pipelined(eng, turn):
            turn((0, 0), None)
            with eng.Fori(0, GRAPHS // 2 - 1) as i:
                turn((i * 2 + 1, 1), (i * 2, 0))
                turn((i * 2 + 2, 0), (i * 2 + 1, 1))
            turn((GRAPHS - 1, 1), (GRAPHS - 2, 0))
            turn(None, (GRAPHS - 1, 1))

        with core.block() as block:
            @block.sync
            def _(sp):
                for dst, src in ((w, w_in), (row_w, row_in), (col_w, col_in)):
                    sp.dma_start(dst[:, :], src).then_inc(s_w, 16)
                with pairs(sp) as i:
                    for k in range(2):
                        n = i * 2 + k
                        sp.wait_ge(s_bias, START + n)
                        sp.nop(nofuse=True)
                        sp.dma_start(adj_t[k][:, :, :],
                                     adj[bass.ds(n, 1)].rearrange("a (t p) m -> p (a t) m", p=P)).then_inc(s_adj[k], 16)

            @block.gpsimd
            def _(pool):
                pool.sem_inc(s_bias, 1)
                with pairs(pool) as i:
                    for k in range(2):
                        n = i * 2 + k
                        pool.wait_ge(s_adj[k], START + i * 16 + 16)
                        pool.nop(nofuse=True)
                        pool.wait_ge(s_turn if over_rows else s_em, START + n * TILES)
                        pool.nop(nofuse=True)
                        pool.tensor_scalar(bias[k][:, :, :], adj_t[k][:, :, :], 0, mask_value, ALU.is_le,
                                           ALU.mult).then_inc(s_bias, 1)

            @block.vector
            def _(dve):
                for s, c in ((s_em, TILES), (s_turn, TILES)):
                    dve.sem_inc(s, c)

                def norm(n, k):
                    dve.wait_ge(s_h, START + n)
                    dve.nop(nofuse=True)
                    for t in range(TILES):
                        tile = n * TILES + t
                        dve.tensor_scalar(
                            xn[k][:, t, :], core.x[:, bass.ds(tile, 1), :].rearrange("p a d -> p (a d)"),
                            core.mean[:, bass.ds(tile, 1)], core.rstd[:, bass.ds(tile, 1)],
                            ALU.subtract, ALU.mult).then_inc(s_xn, 1)

                def copy_h(n, k):
                    dve.wait_ge(s_h, START + n + 2)
                    dve.nop(nofuse=True)
                    dve.wait_ge(s_o, START + n)
                    dve.nop(nofuse=True)
                    dve.tensor_copy(h[k][:, :, :], b_h[:, :].rearrange("p (t d) -> p t d", t=TILES)).then_inc(s_hc, 1)

                def copy_col(n, k):
                    dve.wait_ge(s_sc, START + n + 1)
                    dve.nop(nofuse=True)
                    dve.tensor_copy(col[k][:, :], b_col[:, 0:TILES]).then_inc(s_colc, 1)

                def bias_turned(n, k, t):
                    dve.wait_ge(s_turn, START + n * TILES + TILES + t + 1)
                    dve.nop(nofuse=True)
                    dve.tensor_copy(bias_use[k][:, t, :],
                                    b_turn[t % 2][:, 0:NODES // 2].bitcast(BF16)).then_inc(s_biasT, 1)

                def mask_scores(n, k, t):
                    if over_rows:
                        dve.wait_ge(s_biasT, START + n * TILES + TILES)
                        dve.nop(nofuse=True)
                    else:
                        dve.wait_ge(s_bias, START + n + 2)
                        dve.nop(nofuse=True)
                    dve.wait_ge(s_e, START + n * TILES + t + 1)
                    dve.nop(nofuse=True)
                    score = e[t % 2]
                    if slope:
                        dve.scalar_tensor_tensor(out=lk[t % 2][:, :], in0=e[t % 2][:, :], scalar=slope,
                                                 in1=e[t % 2][:, :], op0=ALU.mult, op1=ALU.max).then_inc(s_lk, 1)
                        dve.wait_ge(s_lk, START + n * TILES + t + 1)
                        dve.nop(nofuse=True)
                        score = lk[t % 2]
                    dve.tensor_tensor(em[k][:, t, :], score[:, :], bias_use[k][:, t, :], ALU.add).then_inc(s_em, 1)

                def find_top(n, k):
                    dve.wait_ge(s_em, START + n * TILES + 2 * TILES)
                    dve.nop(nofuse=True)
                    dve.tensor_reduce(top[k][:, :], em[k][:, :, :], AX_X, ALU.max).then_inc(s_nt, 1)
                    dve.wait_ge(s_nt, START + n * 2 + 1)
                    dve.nop(nofuse=True)
                    dve.tensor_scalar(ntop[k][:, :], top[k][:, :], -1.0, None, ALU.mult).then_inc(s_nt, 1)

                def invert_sums(n, k):
                    dve.wait_ge(s_p, START + n * TILES + TILES)
                    dve.nop(nofuse=True)
                    if not keep_neg:
                        dve.tensor_scalar(top[k][:, :], top[k][:, :], MINUS_BIG / 2, None, ALU.is_gt).then_inc(s_rd, 1)
                    else:
                        dve.memset(top[k][:, :], 1.0).then_inc(s_rd, 1)
                    dve.reciprocal(rden[k][:, :], den[k][:, :]).then_inc(s_rd, 1)
                    dve.wait_ge(s_rd, START + n * 3 + 2)
                    dve.nop(nofuse=True)
                    dve.tensor_tensor(rden[k][:, :], rden[k][:, :], top[k][:, :], ALU.mult).then_inc(s_rd, 1)
                    dve.wait_ge(s_rd, START + n * 3 + 3)
                    dve.nop(nofuse=True)
                    if over_rows:
                        dve.wait_ge(s_hc, START + n + 1)
                        dve.nop(nofuse=True)
                        for t in range(TILES):
                            dve.tensor_scalar(h[k][:, t, :], h[k][:, t, :], rden[k][:, t:t + 1], None,
                                              ALU.mult).then_inc(s_hs, 1)

                def weights_turned(n, k, t):
                    dve.wait_ge(s_pT, START + n * TILES + t + 1)
                    dve.nop(nofuse=True)
                    dve.tensor_copy(probT[k][:, :, t * P:(t + 1) * P],
                                    b_turn[t % 2][:, :].rearrange("p (m n) -> p m n", m=TILES)).then_inc(s_pTc, 1)

                def take_product(n, k):
                    dve.wait_ge(s_o, START + n + 2)
                    dve.nop(nofuse=True)
                    rows = b_o[:, :].rearrange("p (t d) -> p t d", t=TILES)
                    if over_rows:
                        dve.tensor_copy(y[k][:, :, :], rows).then_inc(s_y, 1)
                    else:
                        dve.tensor_tensor(y[k][:, :, :], rows,
                                          rden[k][:, :].unsqueeze(2).to_broadcast([P, TILES, D]), ALU.mult).then_inc(s_y, 1)
                    dve.wait_ge(s_y, START + n * 2 + 1)
                    dve.nop(nofuse=True)
                    if elu:
                        dve.tensor_scalar(low[k][:, :, :], y[k][:, :, :], 0.0, None, ALU.min).then_inc(s_y, 1)

                def add_to_x(n, k):
                    xg = core.x[:, bass.ds(n * TILES, TILES), :]
                    if elu:
                        dve.wait_ge(s_exp, START + n + 1)
                        dve.nop(nofuse=True)
                        dve.scalar_tensor_tensor(out=y[k][:, :, :], in0=y[k][:, :, :], scalar=0.0,
                                                 in1=low[k][:, :, :], op0=ALU.max, op1=ALU.add).then_inc(s_acc, 1)
                        dve.wait_ge(s_acc, START + n * 2 + 1)
                        dve.nop(nofuse=True)
                        dve.scalar_tensor_tensor(out=xg, in0=y[k][:, :, :], scalar=-1.0, in1=xg,
                                                 op0=ALU.add, op1=ALU.add).then_inc(s_acc, 1)
                    else:
                        dve.tensor_tensor(xg, xg, y[k][:, :, :], ALU.add).then_inc(s_y, 1)

                def turn(front, back):
                    if front:
                        norm(*front)
                        copy_h(*front)
                    for t in range(0, 2):
                        if back and not over_rows:
                            weights_turned(*back, t)
                    if front:
                        copy_col(*front)
                    for t in range(2, 4):
                        if back and not over_rows:
                            weights_turned(*back, t)
                    if front and over_rows:
                        for t in range(TILES):
                            bias_turned(*front, t)
                    if back:
                        invert_sums(*back)
                    for t in range(0, 2):
                        if front:
                            mask_scores(*front, t)
                    if back:
                        take_product(*back)
                    for t in range(2, 4):
                        if front:
                            mask_scores(*front, t)
                    if back:
                        add_to_x(*back)
                    if front:
                        find_top(*front)

                pipelined(dve, turn)

            @block.scalar
            def _(act):
                def copy_xT(n, k):
                    act.wait_ge(s_xT, START + n + 1)
                    act.nop(nofuse=True)
                    act.activation(xnT[k][:, :], b_xT[:, :], ACT.Copy).then_inc(s_xTc, 1)

                def weigh(n, k):
                    act.wait_ge(s_nt, START + n * 2 + 2)
                    act.nop(nofuse=True)
                    act.wait_ge(s_o, START + n)
                    act.nop(nofuse=True)
                    for t in range(TILES):
                        act.activation(prob[k][:, t, :], em[k][:, t, :], ACT.Exp, bias=ntop[k][:, t:t + 1],
                                       scale=1.0, accum_out=den[k][:, t:t + 1]).then_inc(s_p, 1)

                def copy_hT(n, k):
                    act.wait_ge(s_h, START + n + 2)
                    act.nop(nofuse=True)
                    act.activation(hT[k][:, :], b_hT[:, :], ACT.Copy).then_inc(s_hTc, 1)

                def copy_row(n, k):
                    act.wait_ge(s_sc, START + n + 1)
                    act.nop(nofuse=True)
                    act.activation(row[k][:, :], b_row[:, :], ACT.Copy).then_inc(s_rowc, 1)
                    act.wait_ge(s_rowc, START + n + 1)
                    act.nop(nofuse=True)
                    act.wait_ge(s_colc, START + n + 1)
                    act.nop(nofuse=True)

                def pair_scores(n, k, t):
                    act.wait_ge(s_em, START + n * TILES + TILES + max(t - 1, 0))
                    act.nop(nofuse=True)
                    act.activation(e[t % 2][:, :], row[k][:, :], ACT.Identity if slope else ACT.Relu,
                                   bias=col[k][:, t:t + 1], scale=1.0).then_inc(s_e, 1)

                def exp_low(n, k):
                    act.wait_ge(s_y, START + n * 2 + 2)
                    act.nop(nofuse=True)
                    act.activation(low[k][:, :, :], low[k][:, :, :], ACT.Exp).then_inc(s_exp, 1)

                def turn(front, back):
                    if front:
                        copy_xT(*front)
                    if back:
                        weigh(*back)
                    if front:
                        copy_hT(*front)
                        copy_row(*front)
                        pair_scores(*front, 0)
                        pair_scores(*front, 1)
                        pair_scores(*front, 2)
                    if back and elu:
                        exp_low(*back)
                    if front:
                        pair_scores(*front, 3)

                pipelined(act, turn)

            @block.tensor
            def _(pe):
                pe.wait_ge(s_w, START + 48)
                pe.sem_inc(s_h, 1)
                pe.sem_inc(s_o, 1)

                def turn_x(n, k):
                    pe.wait_ge(s_xn, START + n * TILES + TILES)
                    pe.nop(nofuse=True)
                    pe.wait_ge(s_xTc, START + n)
                    pe.nop(nofuse=True)
                    for t in range(TILES):
                        last = pe.transpose(b_xT[:, t * P:(t + 1) * P], xn[k][:, t, :], core.ident[:, :])
                    last.then_inc(s_xT, 1)

                def product_h(n, k):
                    pe.wait_ge(s_xTc, START + n + 1)
                    pe.nop(nofuse=True)
                    pe.wait_ge(s_hTc, START + n)
                    pe.nop(nofuse=True)
                    pe.wait_ge(s_hc, START + n)
                    pe.nop(nofuse=True)
                    pe.matmul(b_hT[:, :], w[:, :], xnT[k][:, :], start=True, stop=True)
                    for t in range(TILES):
                        last = pe.matmul(b_h[:, t * P:(t + 1) * P], xnT[k][:, t * P:(t + 1) * P], w[:, :],
                                         start=True, stop=True)
                    last.then_inc(s_h, 1)

                def row_and_col(n, k):
                    pe.wait_ge(s_hTc, START + n + 1)
                    pe.nop(nofuse=True)
                    pe.wait_ge(s_rowc, START + n)
                    pe.nop(nofuse=True)
                    pe.wait_ge(s_colc, START + n)
                    pe.nop(nofuse=True)
                    pe.matmul(b_row[:, :], row_w[:, :], hT[k][:, :], start=True, stop=True)
                    for t in range(TILES):
                        last = pe.matmul(b_col[:, t:t + 1], hT[k][:, t * P:(t + 1) * P], col_w[:, :],
                                         start=True, stop=True)
                    last.then_inc(s_sc, 1)

                def turn_bias(n, k, t):
                    pe.wait_ge(s_bias, START + n + 2)
                    pe.nop(nofuse=True)
                    pe.wait_ge(s_biasT, START + n * TILES + max(t - 1, 0))
                    pe.nop(nofuse=True)
                    turned = b_turn[t % 2][:, 0:NODES // 2].bitcast(BF16)
                    for m in range(TILES):
                        last = pe.transpose(turned[:, m * P:(m + 1) * P],
                                            bias[k][:, m, t * P:(t + 1) * P], core.ident_bf[:, :])
                    last.then_inc(s_turn, 1)

                def turn_weights(n, k, t):
                    pe.wait_ge(s_p, START + n * TILES + t + 1)
                    pe.nop(nofuse=True)
                    pe.wait_ge(s_pTc, START + n * TILES + max(t - 1, 0))
                    pe.nop(nofuse=True)
                    for m in range(TILES):
                        last = pe.transpose(b_turn[t % 2][:, m * P:(m + 1) * P],
                                            prob[k][:, t, m * P:(m + 1) * P], core.ident[:, :])
                    last.then_inc(s_pT, 1)

                def product(n, k):
                    if over_rows:
                        pe.wait_ge(s_hs, START + n * TILES + TILES)
                        pe.nop(nofuse=True)
                        weights = prob[k]
                    else:
                        pe.wait_ge(s_pTc, START + n * TILES + TILES)
                        pe.nop(nofuse=True)
                        weights = probT[k]
                    pe.wait_ge(s_y, START + n * 2)
                    pe.nop(nofuse=True)
                    for t in range(TILES):
                        for m in range(TILES):
                            last = pe.matmul(b_o[:, t * P:(t + 1) * P], weights[:, m, t * P:(t + 1) * P],
                                             h[k][:, m, :], start=(m == 0), stop=(m == TILES - 1))
                    last.then_inc(s_o, 1)

                def turn(front, back):
                    if front:
                        turn_x(*front)
                        product_h(*front)
                    for t in range(0, 2):
                        if back and not over_rows:
                            turn_weights(*back, t)
                    if front:
                        row_and_col(*front)
                    for t in range(2, 4):
                        if back and not over_rows:
                            turn_weights(*back, t)
                    if front and over_rows:
                        for t in range(TILES):
                            turn_bias(*front, t)
                    if back:
                        product(*back)

                pipelined(pe, turn)


def normed_transposed(core, tag, src, dst, gain=None, shift=None):
    nc = core.nc
    with ExitStack() as own:
        xn = [own.enter_context(nc.sbuf_tensor(f"{tag}_xn{k}", [P, TILES, D], F32)) for k in range(2)]
        s_xn, s_turned, s_copied = (core.sem(f"{tag}_{s}") for s in ("normed", "turned", "copied"))
        with core.block() as block:
            @block.vector
            def _(dve):
                with dve.Fori(0, GRAPHS // 2) as i:
                    for k in range(2):
                        n = i * 2 + k
                        dve.wait_ge(s_turned, START + n)
                        dve.nop(nofuse=True)
                        for t in range(TILES):
                            tile = n * TILES + t
                            dve.tensor_scalar(
                                xn[k][:, t, :], src[:, bass.ds(tile, 1), :].rearrange("p a d -> p (a d)"),
                                core.mean[:, bass.ds(tile, 1)], core.rstd[:, bass.ds(tile, 1)],
                                ALU.subtract, ALU.mult).then_inc(s_xn, 1)

            @block.tensor
            def _(pe):
                pe.sem_inc(s_turned, 1)
                with pe.Fori(0, GRAPHS // 2) as i:
                    for k in range(2):
                        n = i * 2 + k
                        pe.wait_ge(s_xn, START + n * TILES + TILES)
                        pe.nop(nofuse=True)
                        pe.wait_ge(s_copied, START + n)
                        pe.nop(nofuse=True)
                        for t in range(TILES):
                            last = pe.transpose(core.bank[k][:, t * P:(t + 1) * P], xn[k][:, t, :], core.ident[:, :])
                        last.then_inc(s_turned, 1)

            @block.scalar
            def _(act):
                act.sem_inc(s_copied, 1)
                with act.Fori(0, GRAPHS // 2) as i:
                    for k in range(2):
                        n = i * 2 + k
                        act.wait_ge(s_turned, START + n + 2)
                        act.nop(nofuse=True)
                        out = dst[:, bass.ds(n, 1), :].rearrange("p a m -> p (a m)")
                        if gain is None:
                            act.activation(out, core.bank[k][:, :], ACT.Copy).then_inc(s_copied, 1)
                        else:
                            act.activation(out, core.bank[k][:, :], ACT.Identity, bias=shift[:, :],
                                           scale=gain[:, :]).then_inc(s_copied, 1)


def top_two_gates(core, tag, scores, gates, experts, apart):
    nc = core.nc
    with ExitStack() as own:
        def sb(name, shape):
            return own.enter_context(nc.sbuf_tensor(f"{tag}_{name}", shape, F32))

        best = [sb(f"best{r}", [P, ALL_TILES]) for r in range(2)]
        pick = [sb(f"pick{r}", [P, ALL_TILES, experts]) for r in range(2)]
        left = sb("left", [P, ALL_TILES, experts])
        free = sb("free", [P, ALL_TILES])
        share = [sb(f"share{r}", [P, ALL_TILES]) for r in range(2)]
        s_step, s_exp = core.sem(f"{tag}_gate_step"), core.sem(f"{tag}_gate_exp")
        whole = [P, ALL_TILES, experts]
        with core.block() as block:
            marks = {}

            @block.vector
            def _(dve):
                steps = 0

                def then(ins):
                    nonlocal steps
                    steps += 1
                    ins.then_inc(s_step, 1)
                    dve.wait_ge(s_step, START + steps)

                for r, pool_of in ((0, scores), (1, left)):
                    then(dve.tensor_reduce(best[r][:, :], pool_of[:, :, :], AX_X, ALU.max))
                    then(dve.tensor_tensor(pick[r][:, :, :], pool_of[:, :, :],
                                           best[r][:, :].unsqueeze(2).to_broadcast(whole), ALU.is_equal))
                    then(dve.memset(free[:, :], 1.0))
                    for e in range(experts):
                        then(dve.tensor_tensor(pick[r][:, :, e], pick[r][:, :, e], free[:, :], ALU.mult))
                        then(dve.tensor_tensor(free[:, :], free[:, :], pick[r][:, :, e], ALU.subtract))
                    if r == 0:
                        then(dve.scalar_tensor_tensor(out=left[:, :, :], in0=pick[0][:, :, :], scalar=-apart,
                                                      in1=scores[:, :, :], op0=ALU.mult, op1=ALU.add))
                then(dve.tensor_tensor(share[1][:, :], best[1][:, :], best[0][:, :], ALU.subtract))
                marks["gap"] = steps
                dve.wait_ge(s_exp, START + 1)
                then(dve.tensor_scalar(free[:, :], share[1][:, :], 1.0, None, ALU.add))
                then(dve.reciprocal(share[0][:, :], free[:, :]))
                then(dve.tensor_tensor(share[1][:, :], share[1][:, :], share[0][:, :], ALU.mult))
                for r in range(2):
                    then(dve.tensor_tensor(pick[r][:, :, :], pick[r][:, :, :],
                                           share[r][:, :].unsqueeze(2).to_broadcast(whole), ALU.mult))
                then(dve.tensor_tensor(gates[:, :, :], pick[0][:, :, :], pick[1][:, :, :], ALU.add))

            @block.scalar
            def _(act):
                act.wait_ge(s_step, START + marks["gap"])
                act.activation(share[1][:, :], share[1][:, :], ACT.Exp).then_inc(s_exp, 1)


def gelu_experts(core, tag, xT, w1_in, b1_in, w2_in, b2_in, gates, target):
    nc = core.nc
    _, E, F, _ = w1_in.shape
    with ExitStack() as own:
        def sb(name, shape):
            return own.enter_context(nc.sbuf_tensor(f"{tag}_{name}", shape, F32))

        w1, b1 = sb("w1", [P, E, F, P]), sb("b1", [P, E, F])
        w2, b2 = sb("w2", [P, E, F, D]), sb("b2", [1, E, D])
        hidden = [[sb(f"hidden{k}_{f}", [P, NODES]) for f in range(F)] for k in range(2)]
        s_w = core.sem(f"{tag}_weights")
        s_up, s_act = core.sem(f"{tag}_up"), core.sem(f"{tag}_gelu")
        s_down, s_add = core.sem(f"{tag}_down"), core.sem(f"{tag}_added")
        up, down = core.bank[0:4], core.bank[4:6]
        assert E == 1 or E % 2 == 0
        G = 2 if E == 1 else 1
        turns = G * E
        with core.block() as block:
            @block.sync
            def _(sp):
                for dst, src in ((w1, w1_in), (b1, b1_in), (w2, w2_in), (b2, b2_in)):
                    sp.dma_start(dst[:], src).then_inc(s_w, 16)

            @block.tensor
            def _(pe):
                pe.wait_ge(s_w, START + 64)

                def rise(i, j):
                    graph = i * G + j // E
                    for f in range(F):
                        c = (j * F + f) % 4
                        pe.wait_ge(s_act, START + i * (turns * F) + j * F + f + 1)
                        pe.nop(nofuse=True)
                        pe.matmul(up[c][:, :], w1[:, j % E, f, :],
                                  xT[:, bass.ds(graph, 1), :].rearrange("p a m -> p (a m)"),
                                  start=True, stop=True).then_inc(s_up, 1)

                def fall(i, j):
                    pe.wait_ge(s_act, START + i * (turns * F) + (j + 1) * F + 3 + 1)
                    pe.nop(nofuse=True)
                    pe.wait_ge(s_add, START + i * turns + j)
                    pe.nop(nofuse=True)
                    for t in range(TILES):
                        o = down[j % 2][:, t * P:(t + 1) * P]
                        for f in range(F):
                            pe.matmul(o, hidden[j % 2][f][:, t * P:(t + 1) * P], w2[:, j % E, f, :],
                                      start=(f == 0), stop=False)
                        last = pe.matmul(o, core.ones_row[:, :], b2[:, j % E, :], start=False, stop=True)
                    last.then_inc(s_down, 1)

                with pe.Fori(0, GRAPHS // G) as i:
                    for j in range(turns + 1):
                        if j < turns:
                            rise(i, j)
                        if j >= 1:
                            fall(i, j - 1)

            @block.scalar
            def _(act):
                act.wait_ge(s_w, START + 64)
                act.sem_inc(s_act, 4)
                with act.Fori(0, GRAPHS // G) as i:
                    for j in range(turns):
                        act.wait_ge(s_down, START + i * turns + max(j - 1, 0))
                        act.nop(nofuse=True)
                        for f in range(F):
                            act.wait_ge(s_up, START + i * (turns * F) + j * F + f + 1)
                            act.nop(nofuse=True)
                            act.activation(hidden[j % 2][f][:, :], up[(j * F + f) % 4][:, :], ACT.Gelu,
                                           bias=b1[:, j % E, f:f + 1], scale=1.0).then_inc(s_act, 1)

            @block.vector
            def _(dve):
                dve.sem_inc(s_add, 1)
                with dve.Fori(0, GRAPHS // G) as i:
                    for j in range(turns):
                        graph = i * G + j // E
                        dve.wait_ge(s_down, START + i * turns + j + 1)
                        dve.nop(nofuse=True)
                        dve.wait_ge(s_add, START + i * turns + j + 1)
                        dve.nop(nofuse=True)
                        if gates is None:
                            xg = target[:, bass.ds(graph * TILES, TILES), :]
                            dve.tensor_tensor(xg, down[j % 2][:, :].rearrange("p (t d) -> p t d", t=TILES), xg,
                                              ALU.add).then_inc(s_add, 1)
                        else:
                            for t in range(TILES):
                                tile = graph * TILES + t
                                xt = target[:, bass.ds(tile, 1), :].rearrange("p a d -> p (a d)")
                                last = dve.scalar_tensor_tensor(
                                    out=xt, in0=down[j % 2][:, t * P:(t + 1) * P],
                                    scalar=gates[:, bass.ds(tile, 1), j % E:j % E + 1].rearrange("p a b -> p (a b)"),
                                    in1=xt, op0=ALU.mult, op1=ALU.add)
                            last.then_inc(s_add, 1)


def routed_experts(core, r1_in, rb1_in, r2_in, rb2_in, w_in, b12_in, b3_in, experts):
    nc = core.nc
    E, R = experts, r1_in.shape[1]
    row_statistics(core, core.x)
    with ExitStack() as own:
        def sb(name, shape):
            return own.enter_context(nc.sbuf_tensor(f"f2_{name}", shape, F32))

        def sem(name):
            return core.sem(f"f2_{name}")

        xT = sb("xT", [P, GRAPHS, NODES])
        normed_transposed(core, "f2n", core.x, xT)
        r1, rb1, r2, rb2 = sb("r1", [P, R]), sb("rb1", [R, 1]), sb("r2", [R, E]), sb("rb2", [1, E])
        w, b12, b3 = sb("w", [P, 3, E, P]), sb("b12", [P, 2, E]), sb("b3", [1, E, D])
        logits, gates = sb("logits", [P, ALL_TILES, E]), sb("gates", [P, ALL_TILES, E])
        rh = [sb(f"rh{k}", [R, NODES]) for k in range(2)]
        s_w, s_r, s_rc, s_l, s_lc = sem("w"), sem("router_up"), sem("router_relu"), sem("logits"), sem("logits_copied")

        with core.block() as block:
            @block.sync
            def _(sp):
                for dst, src in ((r1, r1_in), (rb1, rb1_in), (r2, r2_in), (rb2, rb2_in), (w, w_in), (b12, b12_in),
                                 (b3, b3_in)):
                    sp.dma_start(dst[:], src).then_inc(s_w, 16)
                sp.wait_ge(s_w, START + 7 * 16)

            @block.tensor
            def _(pe):
                pe.wait_ge(s_w, START + 7 * 16)
                with pe.Fori(0, GRAPHS // 2) as i:
                    for k in range(2):
                        n = i * 2 + k
                        pe.wait_ge(s_rc, START + n)
                        pe.nop(nofuse=True)
                        pe.matmul(core.bank[k][0:R, :], r1[:, :], xT[:, bass.ds(n, 1), :].rearrange("p a m -> p (a m)"),
                                  start=True, stop=True).then_inc(s_r, 1)
                        pe.wait_ge(s_rc, START + n + 2)
                        pe.nop(nofuse=True)
                        pe.wait_ge(s_lc, START + n)
                        pe.nop(nofuse=True)
                        for t in range(TILES):
                            o = core.bank[2 + k][:, t * E:(t + 1) * E]
                            pe.matmul(o, rh[k][:, t * P:(t + 1) * P], r2[:, :], start=True, stop=False)
                            last = pe.matmul(o, core.ones_row[:, :], rb2[:, :], start=False, stop=True)
                        last.then_inc(s_l, 1)

            @block.scalar
            def _(act):
                act.wait_ge(s_w, START + 7 * 16)
                act.sem_inc(s_rc, 1)
                with act.Fori(0, GRAPHS // 2) as i:
                    for k in range(2):
                        n = i * 2 + k
                        act.wait_ge(s_r, START + n + 1)
                        act.nop(nofuse=True)
                        act.wait_ge(s_l, START + (i * 2) + max(k - 1, 0))
                        act.nop(nofuse=True)
                        act.activation(rh[k][:, :], core.bank[k][0:R, :], ACT.Relu, bias=rb1[:, :],
                                       scale=1.0).then_inc(s_rc, 1)

            @block.vector
            def _(dve):
                dve.sem_inc(s_lc, 1)
                with dve.Fori(0, GRAPHS // 2) as i:
                    for k in range(2):
                        n = i * 2 + k
                        dve.wait_ge(s_l, START + n + 1)
                        dve.nop(nofuse=True)
                        dve.tensor_copy(logits[:, bass.ds(n * TILES, TILES), :],
                                        core.bank[2 + k][:, 0:TILES * E].rearrange("p (t e) -> p t e", t=TILES)
                                        ).then_inc(s_lc, 1)

        top, total = sb("top", [P, ALL_TILES]), sb("total", [P, ALL_TILES])
        s_step, s_exp = sem("softmax_step"), sem("softmax_exp")
        whole = [P, ALL_TILES, E]
        with core.block() as block:
            @block.vector
            def _(dve):
                dve.tensor_reduce(top[:, :], logits[:, :, :], AX_X, ALU.max).then_inc(s_step, 1)
                dve.wait_ge(s_step, START + 1)
                dve.tensor_tensor(logits[:, :, :], logits[:, :, :], top[:, :].unsqueeze(2).to_broadcast(whole),
                                  ALU.subtract).then_inc(s_step, 1)
                dve.wait_ge(s_exp, START + 1)
                dve.tensor_reduce(total[:, :], logits[:, :, :], AX_X, ALU.add).then_inc(s_step, 1)
                dve.wait_ge(s_step, START + 3)
                dve.reciprocal(total[:, :], total[:, :]).then_inc(s_step, 1)
                dve.wait_ge(s_step, START + 4)
                dve.tensor_tensor(logits[:, :, :], logits[:, :, :], total[:, :].unsqueeze(2).to_broadcast(whole),
                                  ALU.mult).then_inc(s_step, 1)

            @block.scalar
            def _(act):
                act.wait_ge(s_step, START + 2)
                act.activation(logits[:, :, :], logits[:, :, :], ACT.Exp).then_inc(s_exp, 1)
        top_two_gates(core, "f2", logits, gates, E, 4.0)

        h1 = [sb(f"h1_{k}", [P, NODES]) for k in range(2)]
        h2 = [sb(f"h2_{k}", [P, NODES]) for k in range(2)]
        s_1, s_1c, s_2, s_2c, s_3, s_add = (sem(s) for s in ("first", "first_relu", "second", "second_relu", "third",
                                                             "added"))
        first, second, third = core.bank[0:2], core.bank[2:4], core.bank[4:6]
        with core.block() as block:
            @block.tensor
            def _(pe):
                with pe.Fori(0, GRAPHS) as n:
                    for j in range(E + 2):
                        if j < E:
                            pe.wait_ge(s_1c, START + n * E + j)
                            pe.nop(nofuse=True)
                            pe.matmul(first[j % 2][:, :], w[:, 0, j, :],
                                      xT[:, bass.ds(n, 1), :].rearrange("p a m -> p (a m)"),
                                      start=True, stop=True).then_inc(s_1, 1)
                        if 1 <= j <= E:
                            c = j - 1
                            pe.wait_ge(s_1c, START + n * E + c + 2)
                            pe.nop(nofuse=True)
                            pe.wait_ge(s_2c, START + n * E + c)
                            pe.nop(nofuse=True)
                            pe.matmul(second[c % 2][:, :], w[:, 1, c, :], h1[c % 2][:, :],
                                      start=True, stop=True).then_inc(s_2, 1)
                        if j >= 2:
                            c = j - 2
                            pe.wait_ge(s_2c, START + n * E + c + 2)
                            pe.nop(nofuse=True)
                            pe.wait_ge(s_add, START + n * E + c)
                            pe.nop(nofuse=True)
                            for t in range(TILES):
                                o = third[c % 2][:, t * P:(t + 1) * P]
                                pe.matmul(o, h2[c % 2][:, t * P:(t + 1) * P], w[:, 2, c, :], start=True, stop=False)
                                last = pe.matmul(o, core.ones_row[:, :], b3[:, c, :], start=False, stop=True)
                            last.then_inc(s_3, 1)

            @block.scalar
            def _(act):
                act.sem_inc(s_1c, 1)
                act.sem_inc(s_2c, 1)
                with act.Fori(0, GRAPHS) as n:
                    for j in range(E + 1):
                        if j < E:
                            act.wait_ge(s_1, START + n * E + j + 1)
                            act.nop(nofuse=True)
                            act.wait_ge(s_2, START + n * E + max(j - 1, 0))
                            act.nop(nofuse=True)
                            act.activation(h1[j % 2][:, :], first[j % 2][:, :], ACT.Relu, bias=b12[:, 0, j:j + 1],
                                           scale=1.0).then_inc(s_1c, 1)
                        if j >= 1:
                            c = j - 1
                            act.wait_ge(s_2, START + n * E + c + 1)
                            act.nop(nofuse=True)
                            act.wait_ge(s_3, START + n * E + max(c - 1, 0))
                            act.nop(nofuse=True)
                            act.activation(h2[c % 2][:, :], second[c % 2][:, :], ACT.Relu, bias=b12[:, 1, c:c + 1],
                                           scale=1.0).then_inc(s_2c, 1)

            @block.vector
            def _(dve):
                dve.sem_inc(s_add, 1)
                with dve.Fori(0, GRAPHS) as n:
                    for j in range(E):
                        dve.wait_ge(s_3, START + n * E + j + 1)
                        dve.nop(nofuse=True)
                        dve.wait_ge(s_add, START + n * E + j + 1)
                        dve.nop(nofuse=True)
                        for t in range(TILES):
                            tile = n * TILES + t
                            xt = core.x[:, bass.ds(tile, 1), :].rearrange("p a d -> p (a d)")
                            last = dve.scalar_tensor_tensor(
                                out=xt, in0=third[j % 2][:, t * P:(t + 1) * P],
                                scalar=gates[:, bass.ds(tile, 1), j:j + 1].rearrange("p a b -> p (a b)"),
                                in1=xt, op0=ALU.mult, op1=ALU.add)
                        last.then_inc(s_add, 1)


def attention_layer(core, adj, head_scale_in, gain1_in, shift1_in, gain2_in, shift2_in, w1_in, b1_in, w2_in, b2_in,
                    heads):
    nc = core.nc
    H, HD = heads, D // heads
    UNITS = H * TILES
    with ExitStack() as own:
        def sb(name, shape, dt=F32):
            return own.enter_context(nc.sbuf_tensor(f"g0_{name}", shape, dt))

        def sem(name):
            return core.sem(f"g0_{name}")

        y = sb("y", [P, ALL_TILES, D])
        s_w, s_y0 = sem("w"), sem("y_made")
        gain2, shift2 = sb("gain2", [P, 1]), sb("shift2", [P, 1])
        row_statistics(core, core.x)
        with core.block() as block:
            @block.sync
            def _(sp):
                sp.dma_start(gain2[:, :], gain2_in).then_inc(s_w, 16)
                sp.dma_start(shift2[:, :], shift2_in).then_inc(s_w, 16)
                sp.wait_ge(s_w, START + 32)

            @block.vector
            def _(dve):
                with dve.Fori(0, GRAPHS) as n:
                    for k in range(TILES):
                        t = n * TILES + k
                        dve.tensor_scalar(y[:, bass.ds(t, 1), :].rearrange("p a d -> p (a d)"),
                                          core.x[:, bass.ds(t, 1), :].rearrange("p a d -> p (a d)"),
                                          core.mean[:, bass.ds(t, 1)], core.rstd[:, bass.ds(t, 1)],
                                          ALU.subtract, ALU.mult).then_inc(s_y0, 1)
        row_statistics(core, y)

        with ExitStack() as attn:
            def sba(name, shape, dt=F32):
                return attn.enter_context(nc.sbuf_tensor(f"g0_{name}", shape, dt))

            head_scale = sba("head_scale", [P, H])
            gain1, shift1 = sba("gain1", [P, D]), sba("shift1", [P, D])
            adj_t = [sba(f"adj{k}", [P, TILES, NODES], I32) for k in range(2)]
            bias = [sba(f"bias{k}", [P, TILES, NODES], BF16) for k in range(2)]
            nrm = [sba(f"normed{k}", [P, TILES, D]) for k in range(2)]
            nT = [sba(f"normedT{k}", [P, NODES]) for k in range(2)]
            one_head = [sba(f"one_head{k}", [P, NODES]) for k in range(2)]
            ntop = [sba(f"ntop{k}", [P, UNITS]) for k in range(2)]
            den = [sba(f"den{k}", [P, TILES, H]) for k in range(2)]
            rden = [sba(f"rden{k}", [P, TILES, H]) for k in range(2)]
            prob = [sba(f"prob{r}", [P, NODES]) for r in range(4)]
            probT = [sba(f"probT{k}", [P, TILES, P]) for k in range(2)]
            o_sb = [sba(f"o{k}", [P, TILES, D]) for k in range(2)]
            s_adj = [sem("adj0"), sem("adj1")]
            s_bias, s_nrm, s_turned, s_nT = sem("bias"), sem("normed"), sem("turned"), sem("normedT")
            s_head, s_s, s_top, s_p = sem("one_head"), sem("scores"), sem("top"), sem("prob")
            s_pT, s_pTc, s_o, s_done, s_y = sem("probT"), sem("probT_copied"), sem("out"), sem("out_scaled"), sem("y")
            score, turn, out_bank = core.bank[0:4], core.bank[4:6], core.bank[6:8]
            TURN, MULT, FINISH, NORM_AT, TURN_AT, COPY_AT, BIAS_AT = 3, 4, 6, 8, 16, 17, 4

            def all_graphs(eng, body):
                body(0, 0, True, False)
                with eng.Fori(0, GRAPHS // 2 - 1) as i:
                    body(i * 2 + 1, 1, False, False)
                    body(i * 2 + 2, 0, False, False)
                body(GRAPHS - 1, 1, False, True)

            with core.block() as block:
                @block.sync
                def _(sp):
                    for dst, src in ((head_scale, head_scale_in), (gain1, gain1_in), (shift1, shift1_in)):
                        sp.dma_start(dst[:, :], src).then_inc(s_w, 16)
                    with sp.Fori(0, GRAPHS // 2) as i:
                        for k in range(2):
                            n = i * 2 + k
                            sp.wait_ge(s_bias, START + n)
                            sp.nop(nofuse=True)
                            sp.dma_start(adj_t[k][:, :, :],
                                         adj[bass.ds(n, 1)].rearrange("a (t p) m -> p (a t) m", p=P)
                                         ).then_inc(s_adj[k], 16)

                @block.gpsimd
                def _(pool):
                    pool.sem_inc(s_bias, 1)
                    pool.wait_ge(s_w, START + 80)

                    def make_bias(n, k, loads):
                        pool.wait_ge(s_adj[k], START + loads * 16)
                        pool.nop(nofuse=True)
                        pool.tensor_scalar(bias[k][:, :, :], adj_t[k][:, :, :], 0, MINUS_BIG, ALU.is_le,
                                           ALU.mult).then_inc(s_bias, 1)

                    def make_head(k, h):
                        pool.tensor_scalar(one_head[h % 2][:, :], nT[k][:, :], head_scale[:, h:h + 1], None,
                                           ALU.mult).then_inc(s_head, 1)

                    def body(n, k, first, last):
                        for h in range(2, H):
                            pool.wait_ge(s_s, START + n * UNITS + (h - 1) * TILES)
                            pool.nop(nofuse=True)
                            make_head(k, h)
                            if h == BIAS_AT and not last:
                                make_bias(n + 1, 1 - k, (n + 1) // 2 + 1 if first else loads_before[0])
                        if not last:
                            pool.wait_ge(s_nT, START + n + 2)
                            pool.nop(nofuse=True)
                            pool.wait_ge(s_s, START + n * UNITS + (H - 1) * TILES)
                            pool.nop(nofuse=True)
                            make_head(1 - k, 0)
                            pool.wait_ge(s_s, START + n * UNITS + UNITS)
                            pool.nop(nofuse=True)
                            make_head(1 - k, 1)

                    make_bias(0, 0, 1)
                    pool.wait_ge(s_nT, START + 1)
                    make_head(0, 0)
                    make_head(0, 1)
                    loads_before = [0]
                    body(0, 0, True, False)
                    with pool.Fori(0, GRAPHS // 2 - 1) as i:
                        loads_before[0] = i + 2
                        body(i * 2 + 1, 1, False, False)
                        body(i * 2 + 2, 0, False, False)
                    body(GRAPHS - 1, 1, False, True)

                @block.vector
                def _(dve):
                    dve.wait_ge(s_w, START + 80)
                    dve.sem_inc(s_pTc, 2)

                    def norm(n, k, step):
                        base = n * (TILES + 2)
                        if step < TILES:
                            tile = n * TILES + step
                            dve.tensor_scalar(
                                nrm[k][:, step, :], y[:, bass.ds(tile, 1), :].rearrange("p a d -> p (a d)"),
                                core.mean[:, bass.ds(tile, 1)], core.rstd[:, bass.ds(tile, 1)],
                                ALU.subtract, ALU.mult).then_inc(s_nrm, 1)
                        elif step == TILES:
                            dve.wait_ge(s_nrm, START + base + TILES)
                            dve.nop(nofuse=True)
                            dve.tensor_tensor(nrm[k][:, :, :], nrm[k][:, :, :],
                                              gain1[:, :].unsqueeze(1).to_broadcast([P, TILES, D]), ALU.mult).then_inc(s_nrm, 1)
                        else:
                            dve.wait_ge(s_nrm, START + base + TILES + 1)
                            dve.nop(nofuse=True)
                            dve.tensor_tensor(nrm[k][:, :, :], nrm[k][:, :, :],
                                              shift1[:, :].unsqueeze(1).to_broadcast([P, TILES, D]), ALU.add).then_inc(s_nrm, 1)

                    def copy_turned(U, r):
                        dve.wait_ge(s_pT, START + U + 1)
                        dve.nop(nofuse=True)
                        dve.tensor_copy(probT[r][:, :, :],
                                        turn[r][:, :].rearrange("p (m q) -> p m q", m=TILES)).then_inc(s_pTc, 1)

                    def finish(n, k):
                        dve.wait_ge(s_p, START + n * UNITS + UNITS)
                        dve.nop(nofuse=True)
                        dve.reciprocal(rden[k][:, :, :], den[k][:, :, :]).then_inc(s_y, 1)
                        dve.wait_ge(s_y, START + n * 2 + 1)
                        dve.nop(nofuse=True)
                        dve.wait_ge(s_o, START + n * UNITS + UNITS)
                        dve.nop(nofuse=True)
                        for t in range(TILES):
                            dve.tensor_tensor(
                                o_sb[k][:, t, :].rearrange("p (h c) -> p h c", h=H),
                                out_bank[k][:, t * P:(t + 1) * P].rearrange("p (h c) -> p h c", h=H),
                                rden[k][:, t, :].unsqueeze(2).to_broadcast([P, H, HD]), ALU.mult
                                ).then_inc(s_done, 1)
                        dve.wait_ge(s_done, START + n * TILES + TILES)
                        dve.nop(nofuse=True)
                        yg = y[:, bass.ds(n * TILES, TILES), :]
                        dve.tensor_tensor(yg, yg, o_sb[k][:, :, :], ALU.add).then_inc(s_y, 1)

                    def body(n, k, first, last):
                        for u in range(UNITS):
                            dve.wait_ge(s_s, START + n * UNITS + u + 1)
                            dve.nop(nofuse=True)
                            dve.tensor_reduce(ntop[k][:, u:u + 1], score[u % 4][:, :], AX_X, ALU.max,
                                              negate=True).then_inc(s_top, 1)
                            if u >= TURN or not first:
                                if u >= TURN + 2 or not first:
                                    dve.wait_ge(s_o, START + n * UNITS + (u - TURN - 1))
                                    dve.nop(nofuse=True)
                                copy_turned(n * UNITS + (u - TURN), (u - TURN) % 2)
                            if u == FINISH and not first:
                                finish(n - 1, 1 - k)
                            if NORM_AT <= u < NORM_AT + TILES + 2 and not last:
                                norm(n + 1, 1 - k, u - NORM_AT)

                    for step in range(TILES + 2):
                        norm(0, 0, step)
                    all_graphs(dve, body)
                    for U in range(GRAPHS * UNITS, GRAPHS * UNITS + TURN):
                        dve.wait_ge(s_o, START + U - TURN - 1)
                        dve.nop(nofuse=True)
                        copy_turned(U - TURN, (U - TURN) % 2)
                    finish(GRAPHS - 1, 1)

                @block.scalar
                def _(act):
                    def copy_nT(n, k):
                        act.wait_ge(s_turned, START + n + 1)
                        act.nop(nofuse=True)
                        act.activation(nT[k][:, :], out_bank[k][:, :], ACT.Copy).then_inc(s_nT, 1)

                    def body(n, k, first, last):
                        for u in range(UNITS):
                            h, t = divmod(u, TILES)
                            act.wait_ge(s_top, START + n * UNITS + u + 1)
                            act.nop(nofuse=True)
                            if u >= 4 or not first:
                                act.wait_ge(s_pT, START + n * UNITS + (u - 3))
                                act.nop(nofuse=True)
                            act.activation(prob[u % 4][:, :], score[u % 4][:, :], ACT.Exp,
                                           bias=ntop[k][:, u:u + 1], scale=1.0,
                                           accum_out=den[k][:, t, h:h + 1]).then_inc(s_p, 1)
                            if u == COPY_AT and not last:
                                copy_nT(n + 1, 1 - k)

                    copy_nT(0, 0)
                    all_graphs(act, body)

                @block.tensor
                def _(pe):
                    def turn_tokens(n, k, first):
                        pe.wait_ge(s_nrm, START + n * (TILES + 2) + TILES + 2)
                        pe.nop(nofuse=True)
                        if not first:
                            pe.wait_ge(s_done, START + (n - 1) * TILES)
                            pe.nop(nofuse=True)
                        for t in range(TILES):
                            last = pe.transpose(out_bank[k][:, t * P:(t + 1) * P], nrm[k][:, t, :], core.ident[:, :])
                        last.then_inc(s_turned, 1)

                    def turn_weights(U, u):
                        pe.wait_ge(s_p, START + U + 1)
                        pe.nop(nofuse=True)
                        pe.wait_ge(s_pTc, START + U + 1)
                        pe.nop(nofuse=True)
                        for m in range(TILES):
                            last = pe.transpose(turn[u % 2][:, m * P:(m + 1) * P],
                                                prob[u % 4][:, m * P:(m + 1) * P], core.ident[:, :])
                        last.then_inc(s_pT, 1)

                    def multiply(U, u, k):
                        h, t = divmod(u, TILES)
                        pe.wait_ge(s_pTc, START + U + 3)
                        pe.nop(nofuse=True)
                        o = out_bank[k][:, t * P + h * HD:t * P + (h + 1) * HD]
                        for m in range(TILES):
                            last = pe.matmul(o, probT[u % 2][:, m, :], nrm[k][:, m, h * HD:(h + 1) * HD],
                                             start=(m == 0), stop=(m == TILES - 1))
                        last.then_inc(s_o, 1)

                    def body(n, k, first, last):
                        pe.wait_ge(s_bias, START + n + 2)
                        pe.nop(nofuse=True)
                        for u in range(UNITS):
                            h, t = divmod(u, TILES)
                            U = n * UNITS + u
                            if t == 0:
                                pe.wait_ge(s_head, START + n * H + h + 1)
                                pe.nop(nofuse=True)
                            if u >= 4 or not first:
                                pe.wait_ge(s_p, START + n * UNITS + (u - 3))
                                pe.nop(nofuse=True)
                            pe.matmul(score[u % 4][:, :], one_head[h % 2][:, t * P:(t + 1) * P],
                                      nT[k][:, :], start=True, stop=False)
                            pe.matmul(score[u % 4][:, :], core.ident_bf[:, :], bias[k][:, t, :],
                                      start=False, stop=True).then_inc(s_s, 1)
                            for lag, act_on in ((TURN, turn_weights), (MULT, multiply)):
                                if u < lag and first:
                                    continue
                                of = (u - lag) % UNITS
                                which = k if u >= lag else 1 - k
                                if act_on is turn_weights:
                                    turn_weights(n * UNITS + (u - lag), of)
                                else:
                                    multiply(n * UNITS + (u - lag), of, which)
                            if u == TURN_AT and not last:
                                turn_tokens(n + 1, 1 - k, first)

                    turn_tokens(0, 0, True)
                    all_graphs(pe, body)
                    for step in range(MULT):
                        U = GRAPHS * UNITS + step
                        if step < TURN:
                            turn_weights(U - TURN, (U - TURN) % UNITS)
                        multiply(U - MULT, (U - MULT) % UNITS, 1)

        row_statistics(core, y)
        yT = sb("yT", [P, GRAPHS, NODES])
        normed_transposed(core, "g0n", y, yT, gain2, shift2)
        s_res = sem("residual")
        with core.block() as block:
            @block.vector
            def _(dve):
                dve.tensor_tensor(core.x[:, :, :], core.x[:, :, :], y[:, :, :], ALU.add).then_inc(s_res, 1)
        gelu_experts(core, "g0m", yT, w1_in, b1_in, w2_in, b2_in, None, core.x)


def edge_routed_experts(core, edges, wgat_in, att_in, post_in, w1_in, b1_in, w2_in, b2_in, experts, scratch):
    nc = core.nc
    X = experts
    HEADS = att_in.shape[2] // X
    HX = HEADS * X
    F = HEADS + HX
    EDGE_COLS = edges.shape[2]
    BATCH = 16
    BATCHES = EDGE_COLS // BATCH
    RING = 4
    LOW = 1024
    BLOCKS, HIGH = LOW // P, TOKENS // LOW
    COLS = 3 * HIGH * F
    HEADROOM = 60.0
    assert COLS <= 512 and BLOCKS == 8
    row_statistics(core, core.x)
    with ExitStack() as own:
        def sb(name, shape, dt=F32):
            return own.enter_context(nc.sbuf_tensor(f"f0_{name}", shape, dt))

        def sem(name):
            return core.sem(f"f0_{name}")

        xT = sb("xT", [P, GRAPHS, NODES])
        normed_transposed(core, "f0n", core.x, xT)
        gates = sb("gates", [P, ALL_TILES, X])
        with ExitStack() as edge_part:
            def sbe(name, shape, dt=F32):
                return edge_part.enter_context(nc.sbuf_tensor(f"f0_{name}", shape, dt))

            wgat, att, post = sbe("wgat", [P, HX]), sbe("att", [P, 2, HX]), sbe("post", [P, 3, HX])
            source = sbe("source", [P, ALL_TILES, F])
            target = sbe("target", [P, ALL_TILES, 2 * HEADS])
            prod = sbe("prod", [P, ALL_TILES, HX])
            peak, peak_all = sbe("peak", [P, HEADS]), sbe("peak_all", [P, HEADS])
            hT = [sbe(f"hT{k}", [HX, NODES]) for k in range(2)]
            s_w, s_h, s_hc, s_t, s_tc = sem("w"), sem("h"), sem("h_copied"), sem("h_turned"), sem("h_turned_copied")
            s_tab, s_peak, s_store = sem("table_step"), sem("peak"), sem("tables_stored")
            src, dst = sbe("src", [P, EDGE_COLS + BATCH], I32), sbe("dst", [P, EDGE_COLS + BATCH], I32)
            s_edges = sem("edges")
            with core.block() as block:
                @block.sync
                def _(sp):
                    for to, of in ((wgat, wgat_in), (att, att_in), (post, post_in)):
                        sp.dma_start(to[:], of).then_inc(s_w, 16)
                    sp.dma_start(src[:, 0:EDGE_COLS], edges[0]).then_inc(s_edges, 16)
                    sp.dma_start(dst[:, 0:EDGE_COLS], edges[1]).then_inc(s_edges, 16)
                    sp.wait_ge(s_w, START + 48)
                    sp.wait_ge(s_tab, START + 9)
                    with nc.allow_non_contiguous_dma(reason="rows of a few floats"):
                        sp.dma_start(scratch[0].rearrange("(t p) f -> p t f", p=P), source[:, :, :]).then_inc(s_store, 16)
                        sp.dma_start(scratch[1].rearrange("(t p) f -> p t f", p=P), target[:, :, :]).then_inc(s_store, 16)
                    sp.wait_ge(s_store, START + 32)
                    sp.wait_ge(s_edges, START + 32)

                @block.tensor
                def _(pe):
                    pe.wait_ge(s_w, START + 48)
                    with pe.Fori(0, GRAPHS // 2) as i:
                        for k in range(2):
                            n = i * 2 + k
                            pe.wait_ge(s_hc, START + n)
                            pe.nop(nofuse=True)
                            pe.matmul(core.bank[k][0:HX, :], wgat[:, :],
                                      xT[:, bass.ds(n, 1), :].rearrange("p a m -> p (a m)"),
                                      start=True, stop=True).then_inc(s_h, 1)
                            pe.wait_ge(s_hc, START + n + 2)
                            pe.nop(nofuse=True)
                            pe.wait_ge(s_tc, START + n)
                            pe.nop(nofuse=True)
                            for t in range(TILES):
                                last = pe.transpose(core.bank[2 + k][:, t * HX:(t + 1) * HX],
                                                    hT[k][:, t * P:(t + 1) * P], core.ident[0:HX, 0:HX])
                            last.then_inc(s_t, 1)

                @block.scalar
                def _(act):
                    act.sem_inc(s_hc, 1)
                    with act.Fori(0, GRAPHS // 2) as i:
                        for k in range(2):
                            n = i * 2 + k
                            act.wait_ge(s_h, START + n + 1)
                            act.nop(nofuse=True)
                            act.wait_ge(s_t, START + i * 2 + max(k - 1, 0))
                            act.nop(nofuse=True)
                            act.activation(hT[k][:, :], core.bank[k][0:HX, :], ACT.Copy).then_inc(s_hc, 1)

                @block.vector
                def _(dve):
                    dve.sem_inc(s_tc, 1)
                    with dve.Fori(0, GRAPHS // 2) as i:
                        for k in range(2):
                            n = i * 2 + k
                            dve.wait_ge(s_t, START + n + 1)
                            dve.nop(nofuse=True)
                            dve.tensor_copy(source[:, bass.ds(n * TILES, TILES), HEADS:F],
                                            core.bank[2 + k][:, 0:TILES * HX].rearrange("p (t e) -> p t e", t=TILES)
                                            ).then_inc(s_tc, 1)
                    dve.wait_ge(s_tc, START + GRAPHS + 1)
                    dve.wait_ge(s_w, START + 48)
                    steps = 0

                    def then(ins):
                        nonlocal steps
                        steps += 1
                        ins.then_inc(s_tab, 1)
                        dve.wait_ge(s_tab, START + steps)

                    for side, into in ((0, source[:, :, 0:HEADS]), (1, target[:, :, 0:HEADS])):
                        then(dve.tensor_tensor(prod[:, :, :], source[:, :, HEADS:F],
                                               att[:, side, :].unsqueeze(1).to_broadcast([P, ALL_TILES, HX]), ALU.mult))
                        then(dve.tensor_reduce(into, prod[:, :, :].rearrange("p t (h e) -> p t h e", h=HEADS),
                                               AX_X, ALU.add))
                    then(dve.tensor_reduce(peak[:, :], source[:, :, 0:HEADS].rearrange("p t h -> p h t"), AX_X, ALU.max))
                    dve.wait_ge(s_peak, START + 1)
                    reference = target[:, :, HEADS:2 * HEADS]
                    then(dve.tensor_tensor(reference, target[:, :, 0:HEADS],
                                           peak_all[:, :].unsqueeze(1).to_broadcast([P, ALL_TILES, HEADS]), ALU.add))
                    then(dve.tensor_scalar(prod[:, :, 0:HEADS], reference, 0.2, None, ALU.mult))
                    then(dve.tensor_tensor(reference, prod[:, :, 0:HEADS], reference, ALU.max))
                    then(dve.tensor_scalar(reference, reference, -HEADROOM, None, ALU.add))

                @block.gpsimd
                def _(pool):
                    pool.wait_ge(s_tab, START + 5)
                    pool.partition_all_reduce(peak_all[:, :], peak[:, :], P, bass.bass_isa.ReduceOp.max).then_inc(s_peak, 1)

            agg = sbe("agg", [P, ALL_TILES, F])
            with ExitStack() as loop_part:
                def sbl(name, shape, dt=F32):
                    return loop_part.enter_context(nc.sbuf_tensor(f"f0_{name}", shape, dt))

                lanes_i, highs_i = sbl("lanes_i", [P, LOW], I32), sbl("highs_i", [P, HIGH], I32)
                lanes, highs = sbl("lanes", [P, LOW], mybir.dt.float16), sbl("highs", [P, HIGH])
                src_row = [sbl(f"src_row{k}", [P, BATCH], U32) for k in range(2)]
                dst_row = [sbl(f"dst_row{k}", [P, BATCH], U32) for k in range(2)]
                bits = [sbl(f"bits{k}", [P, 2, BATCH], I32) for k in range(2)]
                low = [sbl(f"low{k}", [P, 2, BATCH]) for k in range(2)]
                is_high = [sbl(f"is_high{k}", [P, BATCH, HIGH], BF16) for k in range(2)]
                from_src = [sbl(f"from_src{k}", [P, BATCH, F]) for k in range(2)]
                from_dst = [sbl(f"from_dst{k}", [P, BATCH, 2 * HEADS]) for k in range(2)]
                score, steep = sbl("score", [P, BATCH, HEADS]), sbl("steep", [P, BATCH, HEADS])
                feat = sbl("feat", [P, BATCH, F])
                parts = [sbl(f"parts{k}", [P, 3, BATCH, F], BF16) for k in range(2)]
                is_low = [sbl(f"is_low{r}", [P, LOW], BF16) for r in range(RING)]
                spread = [sbl(f"spread{r}", [P, 3, HIGH, F], BF16) for r in range(RING)]
                nothing = sbl("nothing", [P, 512], BF16)
                s_iota, s_idx, s_feat, s_exp = sem("iota"), sem("indices"), sem("features"), sem("exp")
                s_gs, s_gd = core.edges_gathered[0:2], core.edges_gathered[2:4]
                s_hot, s_sum, s_agg = sem("one_hots"), sem("summed"), sem("collected")
                IDX, FEAT = 7, 10
                sums = core.bank

                with core.block() as block:
                    @block.gpsimd
                    def _(pool):
                        pool.iota(lanes_i[:, :], pattern=[[1, LOW]], base=0, channel_multiplier=0).then_inc(s_iota, 1)
                        pool.iota(highs_i[:, :], pattern=[[1, HIGH]], base=0, channel_multiplier=0).then_inc(s_iota, 1)
                        with pool.Fori(0, BATCHES // 2) as i:
                            for k in range(2):
                                m = i * 2 + k
                                pool.wait_ge(s_idx, START + m * IDX + IDX + 2)
                                pool.nop(nofuse=True)
                                pool.wait_ge(s_feat, START + m * FEAT)
                                pool.nop(nofuse=True)
                                for c in range(BATCH):
                                    for rows, table, idx, s in ((from_src, 0, src_row, s_gs), (from_dst, 1, dst_row, s_gd)):
                                        pool.indirect_dma_start(
                                            out=rows[k][:, c, :], out_offset=None, in_=scratch[table][:, :],
                                            in_offset=bass.IndirectOffsetOnAxis(ap=idx[k][:, c:c + 1], axis=0)
                                            ).then_inc(s[k], 16)

                    @block.vector
                    def _(dve):
                        dve.memset(nothing[:, :], 0.0).then_inc(s_idx, 1)
                        dve.wait_ge(s_iota, START + 2)
                        dve.tensor_copy(lanes[:, :], lanes_i[:, :]).then_inc(s_iota, 1)
                        dve.tensor_copy(highs[:, :], highs_i[:, :]).then_inc(s_iota, 1)
                        dve.memset(src[:, EDGE_COLS:], 0).then_inc(s_iota, 1)
                        dve.memset(dst[:, EDGE_COLS:], 0).then_inc(s_iota, 1)
                        dve.sem_inc(s_feat, FEAT)
                        dve.wait_ge(s_iota, START + 6)
                        dve.sem_inc(s_idx, 1)
                        dve.wait_ge(s_idx, START + 2)

                        def indices(m, k):
                            cols = bass.ds(m * BATCH, BATCH)
                            base = m * IDX + 2
                            dve.tensor_scalar(src_row[k][:, :], src[:, cols], TOKENS - 1, None, ALU.min).then_inc(s_idx, 1)
                            dve.tensor_scalar(dst_row[k][:, :], dst[:, cols], TOKENS - 1, None, ALU.min).then_inc(s_idx, 1)
                            dve.tensor_scalar(bits[k][:, 0, :], dst[:, cols], LOW - 1, None, ALU.bitwise_and).then_inc(s_idx, 1)
                            dve.tensor_scalar(bits[k][:, 1, :], dst[:, cols], LOW.bit_length() - 1, None,
                                              ALU.logical_shift_right).then_inc(s_idx, 1)
                            dve.wait_ge(s_idx, START + base + 4)
                            dve.nop(nofuse=True)
                            dve.tensor_copy(low[k][:, :, :], bits[k][:, :, :]).then_inc(s_idx, 1)
                            dve.wait_ge(s_idx, START + base + 5)
                            dve.nop(nofuse=True)
                            dve.tensor_tensor(is_high[k][:, :, :],
                                              low[k][:, 1, :].unsqueeze(2).to_broadcast([P, BATCH, HIGH]),
                                              highs[:, :].unsqueeze(1).to_broadcast([P, BATCH, HIGH]),
                                              ALU.is_equal).then_inc(s_idx, 2)

                        indices(0, 0)
                        with dve.Fori(0, BATCHES // 2) as i:
                            for k in range(2):
                                m = i * 2 + k
                                dve.wait_ge(s_hot, START + m * (2 * BATCH))
                                dve.nop(nofuse=True)
                                indices(m + 1, (k + 1) % 2)
                                dve.wait_ge(s_gs[k], i * (BATCH * 16) + BATCH * 16)
                                dve.nop(nofuse=True)
                                dve.wait_ge(s_gd[k], i * (BATCH * 16) + BATCH * 16)
                                dve.nop(nofuse=True)
                                base = m * FEAT + FEAT
                                weights, messages = feat[:, :, 0:HEADS], feat[:, :, HEADS:F]
                                dve.tensor_tensor(score[:, :, :], from_src[k][:, :, 0:HEADS],
                                                  from_dst[k][:, :, 0:HEADS], ALU.add).then_inc(s_feat, 1)
                                dve.wait_ge(s_feat, START + base + 1)
                                dve.nop(nofuse=True)
                                dve.scalar_tensor_tensor(out=steep[:, :, :], in0=score[:, :, :], scalar=0.2,
                                                         in1=score[:, :, :], op0=ALU.mult, op1=ALU.max).then_inc(s_feat, 1)
                                dve.wait_ge(s_feat, START + base + 2)
                                dve.nop(nofuse=True)
                                dve.tensor_tensor(steep[:, :, :], steep[:, :, :], from_dst[k][:, :, HEADS:2 * HEADS],
                                                  ALU.subtract).then_inc(s_feat, 1)
                                dve.wait_ge(s_exp, START + m + 1)
                                dve.nop(nofuse=True)
                                dve.tensor_tensor(messages.rearrange("p c (h e) -> p c h e", h=HEADS),
                                                  from_src[k][:, :, HEADS:F].rearrange("p c (h e) -> p c h e", h=HEADS),
                                                  weights.unsqueeze(3).to_broadcast([P, BATCH, HEADS, X]), ALU.mult).then_inc(s_feat, 1)
                                dve.wait_ge(s_feat, START + base + 4)
                                dve.nop(nofuse=True)
                                dve.wait_ge(s_hot, START + m * (2 * BATCH))
                                dve.nop(nofuse=True)
                                dve.tensor_copy(parts[k][:, 0, :, :], feat[:, :, :]).then_inc(s_feat, 1)
                                dve.wait_ge(s_feat, START + base + 5)
                                dve.nop(nofuse=True)
                                dve.tensor_tensor(feat[:, :, :], feat[:, :, :], parts[k][:, 0, :, :],
                                                  ALU.subtract).then_inc(s_feat, 1)
                                dve.wait_ge(s_feat, START + base + 6)
                                dve.nop(nofuse=True)
                                dve.tensor_copy(parts[k][:, 1, :, :], feat[:, :, :]).then_inc(s_feat, 1)
                                dve.wait_ge(s_feat, START + base + 7)
                                dve.nop(nofuse=True)
                                dve.tensor_tensor(parts[k][:, 2, :, :], feat[:, :, :], parts[k][:, 1, :, :],
                                                  ALU.subtract).then_inc(s_feat, 3)
                                dve.wait_ge(s_feat, START + base + 10)
                                dve.nop(nofuse=True)
                                dve.wait_ge(s_idx, START + m * IDX + 2 + IDX)
                                dve.nop(nofuse=True)
                                for c in range(BATCH):
                                    dve.wait_ge(s_sum, START + m * BATCH + c + 1)
                                    dve.nop(nofuse=True)
                                    dve.tensor_scalar(is_low[c % RING][:, :], lanes[:, :], low[k][:, 0, c:c + 1], None,
                                                      ALU.is_equal).then_inc(s_hot, 1)
                                    dve.tensor_tensor(
                                        spread[c % RING][:, :, :, :],
                                        parts[k][:, :, c, :].unsqueeze(2).to_broadcast([P, 3, HIGH, F]),
                                        is_high[k][:, c, :].unsqueeze(1).unsqueeze(3).to_broadcast([P, 3, HIGH, F]),
                                        ALU.mult).then_inc(s_hot, 1)

                        dve.wait_ge(s_sum, START + EDGE_COLS + RING + 1)
                        by_block = agg[:, :, :].rearrange("p (h b) f -> p h b f", b=BLOCKS)
                        steps = 0
                        for q in range(3):
                            for b in range(BLOCKS):
                                piece = sums[b][:, q * HIGH * F:(q + 1) * HIGH * F].rearrange("p (h f) -> p h f", h=HIGH)
                                here = by_block[:, :, b, :]
                                if q == 0:
                                    dve.tensor_copy(here, piece).then_inc(s_agg, 1)
                                else:
                                    dve.tensor_tensor(here, here, piece, ALU.add).then_inc(s_agg, 1)
                                steps += 1
                            dve.wait_ge(s_agg, START + steps)

                    @block.scalar
                    def _(act):
                        with act.Fori(0, BATCHES) as m:
                            act.wait_ge(s_feat, START + m * FEAT + FEAT + 3)
                            act.nop(nofuse=True)
                            act.activation(feat[:, :, 0:HEADS], steep[:, :, :], ACT.Exp).then_inc(s_exp, 1)

                    @block.tensor
                    def _(pe):
                        pe.wait_ge(s_idx, START + 2)
                        pe.sem_inc(s_sum, RING)
                        for b in range(BLOCKS):
                            pe.matmul(sums[b][:, 0:COLS], nothing[:, 0:P], nothing[:, 0:COLS], start=True, stop=False)
                        with pe.Fori(0, EDGE_COLS // RING) as i:
                            for r in range(RING):
                                pe.wait_ge(s_hot, START + (i * RING + r) * 2 + 2)
                                pe.nop(nofuse=True)
                                for b in range(BLOCKS):
                                    last = pe.matmul(sums[b][:, 0:COLS], is_low[r][:, b * P:(b + 1) * P],
                                                     spread[r][:, :, :, :].rearrange("p q h f -> p (q h f)"),
                                                     start=False, stop=False)
                                last.then_inc(s_sum, 1)
                        for b in range(BLOCKS):
                            last = pe.matmul(sums[b][:, 0:COLS], nothing[:, 0:P], nothing[:, 0:COLS], start=False, stop=True)
                        last.then_inc(s_sum, 1)

            own_w = sbe("own_w", [P, ALL_TILES, HEADS])
            tmp_w = sbe("tmp_w", [P, ALL_TILES, HEADS])
            mean, var, std = sbe("mean", [P, ALL_TILES]), sbe("var", [P, ALL_TILES]), sbe("std", [P, ALL_TILES])
            scores = sbe("scores", [P, ALL_TILES, X])
            s_fin, s_root = sem("finish_step"), sem("finish_act")
            whole = [P, ALL_TILES, HX]
            marks = {}
            with core.block() as block:
                @block.vector
                def _(dve):
                    steps = 0

                    def then(ins):
                        nonlocal steps
                        steps += 1
                        ins.then_inc(s_fin, 1)
                        dve.wait_ge(s_fin, START + steps)

                    def heads_of(ap):
                        return ap.rearrange("p t (h e) -> p (t h) e", h=HEADS)

                    def spread_heads(ap):
                        return ap.rearrange("p t h -> p (t h)").unsqueeze(2).to_broadcast([P, ALL_TILES * HEADS, X])

                    sums_w, sums_m = agg[:, :, 0:HEADS], agg[:, :, HEADS:F]
                    then(dve.tensor_tensor(tmp_w[:, :, :], source[:, :, 0:HEADS], target[:, :, 0:HEADS], ALU.add))
                    then(dve.scalar_tensor_tensor(out=own_w[:, :, :], in0=tmp_w[:, :, :], scalar=0.2, in1=tmp_w[:, :, :],
                                                  op0=ALU.mult, op1=ALU.max))
                    then(dve.tensor_tensor(own_w[:, :, :], own_w[:, :, :], target[:, :, HEADS:2 * HEADS], ALU.subtract))
                    marks["own"] = steps
                    dve.wait_ge(s_root, START + 1)
                    then(dve.tensor_copy(prod[:, :, :], source[:, :, HEADS:F]))
                    then(dve.tensor_tensor(heads_of(prod[:, :, :]), heads_of(prod[:, :, :]), spread_heads(own_w[:, :, :]),
                                           ALU.mult))
                    then(dve.tensor_tensor(prod[:, :, :], prod[:, :, :], sums_m, ALU.add))
                    then(dve.tensor_tensor(own_w[:, :, :], own_w[:, :, :], sums_w, ALU.add))
                    then(dve.reciprocal(own_w[:, :, :], own_w[:, :, :]))
                    then(dve.tensor_tensor(heads_of(prod[:, :, :]), heads_of(prod[:, :, :]), spread_heads(own_w[:, :, :]),
                                           ALU.mult))

                    def rowwise(vec):
                        return vec.unsqueeze(1).to_broadcast(whole)

                    then(dve.tensor_tensor(prod[:, :, :], prod[:, :, :], rowwise(post[:, 0, :]), ALU.add))
                    then(dve.tensor_reduce(mean[:, :], prod[:, :, :], AX_X, ALU.add))
                    then(dve.tensor_scalar(mean[:, :], mean[:, :], 1.0 / HX, None, ALU.mult))
                    then(dve.tensor_tensor(prod[:, :, :], prod[:, :, :], mean[:, :].unsqueeze(2).to_broadcast(whole),
                                           ALU.subtract))
                    squares = agg[:, :, HEADS:F]
                    then(dve.tensor_tensor(squares, prod[:, :, :], prod[:, :, :], ALU.mult))
                    then(dve.tensor_reduce(var[:, :], squares, AX_X, ALU.add))
                    then(dve.tensor_scalar(var[:, :], var[:, :], 1.0 / HX, EPS, ALU.mult, ALU.add))
                    marks["var"] = steps
                    dve.wait_ge(s_root, START + 2)
                    then(dve.reciprocal(std[:, :], std[:, :]))
                    then(dve.tensor_tensor(prod[:, :, :], prod[:, :, :], std[:, :].unsqueeze(2).to_broadcast(whole), ALU.mult))
                    then(dve.tensor_tensor(prod[:, :, :], prod[:, :, :], rowwise(post[:, 1, :]), ALU.mult))
                    then(dve.tensor_tensor(prod[:, :, :], prod[:, :, :], rowwise(post[:, 2, :]), ALU.add))
                    then(dve.tensor_reduce(scores[:, :, :], prod[:, :, :].rearrange("p t (h e) -> p t e h", h=HEADS),
                                           AX_X, ALU.add))
                    then(dve.tensor_scalar(scores[:, :, :], scores[:, :, :], 1.0 / HEADS, None, ALU.mult))

                @block.scalar
                def _(act):
                    act.wait_ge(s_fin, START + marks["own"])
                    act.activation(own_w[:, :, :], own_w[:, :, :], ACT.Exp).then_inc(s_root, 1)
                    act.wait_ge(s_fin, START + marks["var"])
                    act.activation(std[:, :], var[:, :], ACT.Sqrt).then_inc(s_root, 1)
            top_two_gates(core, "f0", scores, gates, X, -MINUS_BIG)
        gelu_experts(core, "f0m", xT, w1_in, b1_in, w2_in, b2_in, gates, core.x)


def tropical_layer(core, wt_in, cols_in, sl_cvx_in, of_cvx_in, sl_ccv_in, of_ccv_in, wc_in, wg_in, wd_in, bd_in):
    nc = core.nc
    _, FC, _ = wt_in.shape
    PIECES = sl_cvx_in.shape[2]
    STEP = 4
    LOWEST = -3.0e38
    row_statistics(core, core.x)
    with ExitStack() as own:
        def sb(name, shape, dt=F32):
            return own.enter_context(nc.sbuf_tensor(f"f1_{name}", shape, dt))

        def sem(name):
            return core.sem(f"f1_{name}")

        xT = sb("xT", [P, GRAPHS, NODES])
        normed_transposed(core, "f1n", core.x, xT)
        part = [sb(f"part{q}", [P, GRAPHS, NODES], BF16) for q in range(3)]
        wt = sb("wt", [P, FC, D])
        cols = sb("cols", [P, 4, FC])
        sl_cvx, of_cvx, sl_ccv, of_ccv = (sb(s, [P, FC, PIECES]) for s in ("sl_cvx", "of_cvx", "sl_ccv", "of_ccv"))
        wc, wg, wd, bd = sb("wc", [P, FC, P]), sb("wg", [P, FC, P]), sb("wd", [P, FC, D]), sb("bd", [1, D])
        mix, one_less_mix = sb("mix", [P, FC]), sb("one_less_mix", [P, FC])
        s_w, s_split, s_mix = sem("w"), sem("split"), sem("mix")
        loads = ((wt, wt_in), (cols, cols_in), (sl_cvx, sl_cvx_in), (of_cvx, of_cvx_in), (sl_ccv, sl_ccv_in),
                 (of_ccv, of_ccv_in), (wc, wc_in), (wg, wg_in), (wd, wd_in), (bd, bd_in))

        with ExitStack() as early, core.block() as block:
            rest = early.enter_context(nc.sbuf_tensor("f1_rest", [P, GRAPHS // 4, NODES], F32))

            @block.sync
            def _(sp):
                for dst, src in loads:
                    sp.dma_start(dst[:], src).then_inc(s_w, 16)
                sp.wait_ge(s_w, START + 16 * len(loads))

            @block.scalar
            def _(act):
                act.wait_ge(s_w, START + 16 * len(loads))
                act.activation(mix[:, :], cols[:, 1, :], ACT.Sigmoid).then_inc(s_mix, 1)

            @block.vector
            def _(dve):
                dve.wait_ge(s_mix, START + 1)
                dve.tensor_scalar(one_less_mix[:, :], mix[:, :], -1.0, 1.0, ALU.mult, ALU.add).then_inc(s_mix, 1)
                steps = 0
                for g in range(0, GRAPHS, GRAPHS // 4):
                    block_of = slice(g, g + GRAPHS // 4)
                    whole, (high, mid, low) = xT[:, block_of, :], (p[:, block_of, :] for p in part)
                    for ins in (lambda: dve.tensor_copy(high, whole),
                                lambda: dve.tensor_tensor(rest[:, :, :], whole, high, ALU.subtract),
                                lambda: dve.tensor_copy(mid, rest[:, :, :]),
                                lambda: dve.tensor_tensor(low, rest[:, :, :], mid, ALU.subtract)):
                        ins().then_inc(s_split, 1)
                        steps += 1
                        dve.wait_ge(s_split, START + steps)

        acc, z = sb("acc", [P, FC, NODES]), sb("z", [P, FC, NODES])
        spread = [sb(f"spread{j}", [P, NODES]) for j in range(STEP)]
        piece = [sb(f"piece{r}", [P, NODES]) for r in range(2)]
        cvx, ccv = sb("cvx", [P, FC, NODES]), sb("ccv", [P, FC, NODES])
        classic, gate = sb("classic", [P, FC, NODES]), sb("gate", [P, FC, NODES])
        trop, fused = sb("trop", [P, NODES]), sb("fused", [P, FC, NODES])
        s_cast, s_spread, s_max, s_z, s_acc0 = sem("cast"), sem("spread"), sem("max_plus"), sem("z"), sem("acc_cleared")
        s_lin, s_linc, s_piece, s_take = sem("linear"), sem("linear_copied"), sem("piece"), sem("piece_taken")
        s_fuse, s_out, s_add = sem("fused"), sem("out"), sem("added")
        cast, lin, out_bank = core.bank[0:4], core.bank[4:6], core.bank[6]
        AHEAD = STEP * FC
        TURNS = D // STEP // FC
        assert TURNS == PIECES
        MADE = FC * PIECES * 2
        TAKEN = FC * (PIECES - 1) * 2
        FUSE = 7

        def turns_of(body):
            def with_loop(eng):
                body(0, True, False, False)
                body(1, True, True, False)
                with eng.Fori(2, GRAPHS) as n:
                    body(n, True, True, True)
                body(GRAPHS, False, True, True)
                body(GRAPHS + 1, False, False, True)
            return with_loop

        with core.block() as block:
            @block.tensor
            def _(pe):
                def body(n, now, last_one, before):
                    for c in range(FC):
                        if now:
                            with pe.Fori(c * TURNS, (c + 1) * TURNS) as turn:
                                for j in range(STEP):
                                    d = turn * STEP + j
                                    pe.wait_ge(s_spread, START + n * D + d + 1)
                                    pe.nop(nofuse=True)
                                    row = core.ident_bf[:, bass.ds(d, 1)].to_broadcast([P, P])
                                    for q in range(3):
                                        last = pe.matmul(cast[j][:, :], row,
                                                         part[q][:, bass.ds(n, 1), :].rearrange("p a m -> p (a m)"),
                                                         start=(q == 0), stop=(q == 2))
                                    last.then_inc(s_cast, 1)
                        if c == 0 and before:
                            m = n - 2
                            pe.wait_ge(s_fuse, START + m * (FC * FUSE) + 2 * FC * FUSE)
                            pe.nop(nofuse=True)
                            pe.wait_ge(s_add, START + m)
                            pe.nop(nofuse=True)
                            for t in range(TILES):
                                o = out_bank[:, t * P:(t + 1) * P]
                                for f in range(FC):
                                    pe.matmul(o, fused[:, f, t * P:(t + 1) * P], wd[:, f, :], start=(f == 0), stop=False)
                                last = pe.matmul(o, core.ones_row[:, :], bd[:, :], start=False, stop=True)
                            last.then_inc(s_out, 1)
                        if last_one:
                            m = n - 1
                            for r, w in ((0, wc), (1, wg)):
                                pe.wait_ge(s_linc, START + m * (2 * FC) + c * 2 + r + 1)
                                pe.nop(nofuse=True)
                                pe.matmul(lin[r][:, :], w[:, c, :],
                                          xT[:, bass.ds(m, 1), :].rearrange("p a m -> p (a m)"),
                                          start=True, stop=True).then_inc(s_lin, 1)

                turns_of(body)(pe)

            @block.vector
            def _(dve):
                dve.sem_inc(s_max, AHEAD)
                dve.sem_inc(s_take, 1)

                def maxima(n, turn):
                    for j in range(STEP):
                        d = turn * STEP + j
                        done = (n * D + d) * FC
                        dve.wait_ge(s_spread, START + n * D + d + STEP + 1)
                        dve.nop(nofuse=True)
                        for c in range(FC):
                            if c % 2 == 0:
                                dve.wait_ge(s_max, START + done + (AHEAD - FC) + c + 2)
                                dve.nop(nofuse=True)
                            dve.scalar_tensor_tensor(out=acc[:, c, :], in0=spread[j][:, :],
                                                     scalar=wt[:, c, bass.ds(d, 1)], in1=acc[:, c, :],
                                                     op0=ALU.add, op1=ALU.max).then_inc(s_max, 1)

                def take(m, c, p):
                    made = m * MADE + (c * PIECES + p) * 2
                    taken = m * TAKEN + (c * (PIECES - 1) + p - 1) * 2 + 1
                    for r, (env, op) in enumerate(((cvx, ALU.max), (ccv, ALU.min))):
                        dve.wait_ge(s_piece, START + made + r + 1)
                        dve.nop(nofuse=True)
                        if r == 0:
                            dve.wait_ge(s_take, START + taken)
                            dve.nop(nofuse=True)
                        here = env[:, bass.ds(c, 1), :].rearrange("p a m -> p (a m)")
                        dve.tensor_tensor(here, here, piece[r][:, :], op).then_inc(s_take, 1)

                def body(n, now, last_one, before):
                    if now:
                        dve.wait_ge(s_z, START + n * FC)
                        dve.nop(nofuse=True)
                        dve.memset(acc[:, :, :], LOWEST).then_inc(s_acc0, 1)
                        dve.wait_ge(s_acc0, START + n + 1)
                        dve.nop(nofuse=True)
                    if now or last_one:
                        with dve.Fori(0, FC) as c_now:
                            if now:
                                maxima(n, c_now * TURNS)
                            with dve.Fori(1, TURNS) as p_now:
                                if now:
                                    maxima(n, c_now * TURNS + p_now)
                                if last_one:
                                    take(n - 1, c_now, p_now)
                    if now:
                        dve.wait_ge(s_max, START + (n + 1) * (D * FC) + AHEAD)
                        dve.nop(nofuse=True)
                        dve.wait_ge(s_piece, START + n * MADE)
                        dve.nop(nofuse=True)
                        for c in range(FC):
                            dve.tensor_scalar(z[:, c, :], acc[:, c, :], cols[:, 0, c:c + 1], None,
                                              ALU.add).then_inc(s_z, 1)
                    if before:
                        m = n - 2
                        dve.wait_ge(s_out, START + m + 1)
                        dve.nop(nofuse=True)
                        xg = core.x[:, bass.ds(m * TILES, TILES), :]
                        dve.tensor_tensor(xg, out_bank[:, :].rearrange("p (t d) -> p t d", t=TILES), xg,
                                          ALU.add).then_inc(s_add, 1)

                turns_of(body)(dve)

            @block.scalar
            def _(act):
                act.sem_inc(s_linc, 2)
                act.sem_inc(s_spread, STEP)

                def copies(n, turn):
                    for j in range(STEP):
                        d = turn * STEP + j
                        act.wait_ge(s_cast, START + n * D + d + 1)
                        act.nop(nofuse=True)
                        act.wait_ge(s_max, START + (n * D + d) * FC + FC)
                        act.nop(nofuse=True)
                        act.activation(spread[j][:, :], cast[j][:, :], ACT.Copy).then_inc(s_spread, 1)

                def pieces(m, c, p, first):
                    for r, (sl, of, env) in enumerate(((sl_cvx, of_cvx, cvx), (sl_ccv, of_ccv, ccv))):
                        if first:
                            if r == 0:
                                act.wait_ge(s_fuse, START + m * (FC * FUSE) + c * FUSE + 3)
                                act.nop(nofuse=True)
                            to = env[:, c, :]
                        else:
                            act.wait_ge(s_take, START + m * TAKEN + (c * (PIECES - 1) + p - 1) * 2 + r)
                            act.nop(nofuse=True)
                            to = piece[r][:, :]
                        act.activation(to, z[:, c, :], ACT.Identity, bias=of[:, c, bass.ds(p, 1)],
                                       scale=sl[:, c, bass.ds(p, 1)]).then_inc(s_piece, 1)

                def body(n, now, last_one, before):
                    m = n - 1
                    for c in range(FC):
                        if now:
                            copies(n, c * TURNS)
                        if last_one:
                            if c == 0:
                                act.wait_ge(s_z, START + n * FC)
                                act.nop(nofuse=True)
                            pieces(m, c, 0, first=True)
                        if now or last_one:
                            with act.Fori(1, TURNS) as p:
                                if now:
                                    copies(n, p + c * TURNS)
                                if last_one:
                                    pieces(m, c, p, first=False)
                        if last_one:
                            act.wait_ge(s_fuse, START + m * (FC * FUSE) + (c + 1) * FUSE)
                            act.nop(nofuse=True)
                            for r, func, dst in ((0, ACT.Gelu, classic), (1, ACT.Sigmoid, gate)):
                                act.wait_ge(s_lin, START + m * (2 * FC) + c * 2 + r + 1)
                                act.nop(nofuse=True)
                                act.activation(dst[:, c, :], lin[r][:, :], func, bias=cols[:, 2 + r, c:c + 1],
                                               scale=1.0).then_inc(s_linc, 1)

                turns_of(body)(act)

            @block.gpsimd
            def _(pool):
                pool.sem_inc(s_fuse, FC * FUSE)

                def body(n, now, last_one, before):
                    if not last_one:
                        return
                    m = n - 1
                    for c in range(FC):
                        mark = (m + 1) * (FC * FUSE) + c * FUSE
                        pool.wait_ge(s_take, START + m * TAKEN + (c + 1) * (PIECES - 1) * 2 + 1)
                        pool.nop(nofuse=True)
                        pool.tensor_scalar(ccv[:, c, :], ccv[:, c, :], one_less_mix[:, c:c + 1], None,
                                           ALU.mult).then_inc(s_fuse, 1)
                        pool.wait_ge(s_fuse, START + mark)
                        pool.nop(nofuse=True)
                        pool.tensor_scalar(trop[:, :], cvx[:, c, :], mix[:, c:c + 1], None,
                                           ALU.mult).then_inc(s_fuse, 1)
                        pool.wait_ge(s_fuse, START + mark + 2)
                        pool.nop(nofuse=True)
                        pool.tensor_tensor(trop[:, :], trop[:, :], ccv[:, c, :], ALU.add).then_inc(s_fuse, 1)
                        pool.wait_ge(s_fuse, START + mark + 3)
                        pool.nop(nofuse=True)
                        pool.wait_ge(s_linc, START + m * (2 * FC) + c * 2 + 4)
                        pool.nop(nofuse=True)
                        if c == 0:
                            pool.wait_ge(s_out, START + m)
                            pool.nop(nofuse=True)
                        pool.tensor_tensor(fused[:, c, :], trop[:, :], gate[:, c, :], ALU.mult).then_inc(s_fuse, 1)
                        pool.wait_ge(s_fuse, START + mark + 4)
                        pool.nop(nofuse=True)
                        pool.tensor_scalar(gate[:, c, :], gate[:, c, :], -1.0, 1.0, ALU.mult,
                                           ALU.add).then_inc(s_fuse, 1)
                        pool.wait_ge(s_fuse, START + mark + 5)
                        pool.nop(nofuse=True)
                        pool.tensor_tensor(gate[:, c, :], gate[:, c, :], classic[:, c, :], ALU.mult).then_inc(s_fuse, 1)
                        pool.wait_ge(s_fuse, START + mark + 6)
                        pool.nop(nofuse=True)
                        pool.tensor_tensor(fused[:, c, :], fused[:, c, :], gate[:, c, :], ALU.add).then_inc(s_fuse, 1)

                turns_of(body)(pool)


def memory_attention(core, wpk_in, keys_in, wq_in, wo_in, tri_in, table, heads, top):
    nc = core.nc
    H, K = heads, top
    NK = keys_in.shape[0]
    DK = keys_in.shape[2] // H
    PAIRS = 2 * H // 2
    KV = 2 * D
    ROUNDS = K
    RING = 4
    LOWEST = -3.0e38
    QSCALE = float(D) ** -0.5
    STEPS = H * TILES
    ROWS = [(i, K // (i + 1)) for i in range(K)]
    FULL = [(i, c) for i, c in ROWS if c > 2]
    TWOS, ONES = [i for i, c in ROWS if c == 2], [i for i, c in ROWS if c == 1]
    CAND = sum(c for _, c in ROWS)
    FULL_END = sum(c for _, c in FULL)
    TWOS_END = FULL_END + 2 * len(TWOS)
    SUMS = len(FULL) + 2
    RANK, CANDS, FINAL, WEIGH = 10, 3 + 2 * SUMS, 9, 5
    assert K == ROUNDS == 16 and H == 8 and 2 * DK == P and NK == P
    row_statistics(core, core.x)
    with ExitStack() as own:
        def sb(name, shape, dt=F32):
            return own.enter_context(nc.sbuf_tensor(f"f3_{name}", shape, dt))

        def sem(name):
            return core.sem(f"f3_{name}")

        wpk, wq, wo = sb("wpk", [P, PAIRS, P]), sb("wq", [P, H, D]), sb("wo", [P, H, D])
        keysT = sb("keysT", [P, PAIRS, NK])
        tri = sb("tri", [P, P], BF16)
        tri_f = sb("tri_f", [P, P])
        places_i, places = sb("places_i", [P, CAND], I32), sb("places", [P, CAND])
        offset_i, offset = sb("offset_i", [P, H, K], I32), sb("offset", [P, H, K])
        s_w, s_const, s_kt, s_ktc = sem("w"), sem("constants"), sem("keys_turned"), sem("keys_copied")
        with ExitStack() as early, core.block() as block:
            keys = early.enter_context(nc.sbuf_tensor("f3_keys", [NK, 2, H * DK], F32))
            keys_p = keys[:, :, :].rearrange("k p (a c) -> k (p a) c", c=P)

            @block.sync
            def _(sp):
                for dst, src in ((wpk, wpk_in), (wq, wq_in), (wo, wo_in), (keys, keys_in), (tri_f, tri_in)):
                    sp.dma_start(dst[:], src).then_inc(s_w, 16)
                sp.wait_ge(s_w, START + 80)

            @block.gpsimd
            def _(pool):
                pool.iota(places_i[:, :], pattern=[[1, CAND]], base=0, channel_multiplier=0).then_inc(s_const, 1)
                pool.iota(offset_i[:, :, :], pattern=[[NK, H], [0, K]], base=0, channel_multiplier=0).then_inc(s_const, 1)

            @block.vector
            def _(dve):
                dve.wait_ge(s_const, START + 2)
                dve.wait_ge(s_w, START + 80)
                dve.tensor_copy(places[:, :], places_i[:, :]).then_inc(s_const, 1)
                dve.tensor_scalar(offset[:, :, :], offset_i[:, :, :], float(NK), None, ALU.mult).then_inc(s_const, 1)
                dve.tensor_copy(tri[:, :], tri_f[:, :]).then_inc(s_const, 1)

            @block.tensor
            def _(pe):
                pe.wait_ge(s_w, START + 80)
                for half in range(2):
                    for a in range(4):
                        last = pe.transpose(core.bank[half][:, a * P:(a + 1) * P], keys_p[:, half * 4 + a, :],
                                            core.ident[:, :])
                    last.then_inc(s_kt, 1)

            @block.scalar
            def _(act):
                for half in range(2):
                    act.wait_ge(s_kt, START + half + 1)
                    act.activation(keysT[:, half * 4:half * 4 + 4, :].rearrange("p a k -> p (a k)"),
                                   core.bank[half][:, :], ACT.Copy).then_inc(s_ktc, 1)

        xn, xnT = sb("xn", [P, D]), sb("xnT", [P, P])
        qT = sb("qT", [P, PAIRS, P])
        work = [sb(f"work{p}", [P, NK]) for p in range(2)]
        best = sb("best", [P, 2, H, K])
        place = sb("place", [P, 2, H, K], U32)
        place_f = sb("place_f", [P, 2, H, K])
        cand, cand_row = sb("cand", [P, H, CAND]), sb("cand_row", [P, H, CAND])
        work2 = sb("work2", [P, CAND])
        final = sb("final", [P, H, K])
        pos, pos_f = sb("pos", [P, K], U32), sb("pos_f", [P, K])
        same = sb("same", [P, K, CAND])
        row_f = sb("row_f", [P, H, K])
        total = sb("total", [P, H])
        weight = [sb(f"weight{k}", [P, H, K]) for k in range(2)]
        rows = [sb(f"rows{k}", [P, H, K], U32) for k in range(2)]
        ring = [sb(f"ring{r}", [P, H, KV]) for r in range(RING)]
        kv = [sb(f"kv{k}", [P, H, KV]) for k in range(2)]
        kT_new, kT = sb("kT_new", [P, H, NODES]), sb("kT", [P, H, NODES])
        v_new, v = sb("v_new", [P, TILES, H, D]), sb("v", [P, TILES, H, D])
        axn, axnT = sb("axn", [P, TILES, D]), sb("axnT", [P, NODES])
        qh = sb("qh", [P, NODES])
        ntop, den, rden = sb("ntop", [P, STEPS]), sb("den", [P, STEPS]), sb("rden", [P, STEPS])
        prob, probT = sb("prob", [P, NODES]), sb("probT", [P, NODES])
        o, oT = sb("o", [P, D]), sb("oT", [P, TILES, P])

        s_xn, s_q, s_qc = sem("xn"), sem("q_bank"), sem("q_bank_copied")
        s_sim, s_rank, s_cand, s_final = sem("sim"), sem("ranked"), sem("candidates"), sem("final")
        s_wt, s_wexp, s_rows, s_acc = sem("weigh"), sem("weigh_exp"), sem("rows_ready"), sem("accumulated")
        s_land = core.memory_gathered[0:RING]
        s_v, s_turnover = sem("v_copied"), sem("turnover")
        s_axn, s_m, s_mc = sem("axn"), sem("misc_bank"), sem("misc_bank_copied")
        s_s, s_top, s_p, s_pT, s_pTc = sem("scores"), sem("top"), sem("prob"), sem("probT"), sem("probT_copied")
        s_pv, s_rd, s_o, s_out, s_add = sem("pv"), sem("rden"), sem("o"), sem("out"), sem("added")
        sim, q_bank, s_bank, t_bank, o_bank, m_bank, out_bank = core.bank[0:2], *core.bank[2:8]
        Q_TILE = 5
        M_GRAPH = 1 + H + STEPS

        def use_q(h):
            return 1 + h + max(TILES * h - 1, 0)

        def use_o(g):
            return 1 + min((g + 1) // TILES + 1, H) + g

        def program(eng_body):
            def run(eng, prologue=None):
                if prologue:
                    prologue()
                eng_body(0, True, False, True)
                with eng.Fori(1, GRAPHS - 1) as n:
                    eng_body(n, True, True, True)
                eng_body(GRAPHS - 1, True, True, False)
                eng_body(GRAPHS, False, True, False)
            return run

        RANK_ROUND = {1: (0, 1), 2: (2, 3), 3: (4, 5), 4: (6, 7)}
        CANDIDATE_ROUND = 5
        FINAL_ROUND = {6 + h: (h,) for h in range(H)}
        WEIGH_ROUND = 14

        with core.block() as block:
            @block.gpsimd
            def _(pool):
                with pool.Fori(0, ALL_TILES // 2) as i:
                    for b in range(2):
                        tile = i * 2 + b
                        pool.wait_ge(s_rows, START + tile + 1)
                        pool.nop(nofuse=True)
                        for k in range(ROUNDS):
                            pool.wait_ge(s_acc, START + (tile * ROUNDS + k + 1) * H)
                            pool.nop(nofuse=True)
                            for h in range(H):
                                pool.indirect_dma_start(
                                    out=ring[k % RING][:, h, :], out_offset=None, in_=table[:, :],
                                    in_offset=bass.IndirectOffsetOnAxis(ap=rows[b][:, h, k:k + 1], axis=0)
                                    ).then_inc(s_land[k % RING], 16)

            @block.vector
            def _(dve):
                def prepare(T, first=False):
                    if not first:
                        dve.wait_ge(s_q, START + T * Q_TILE - 2)
                        dve.nop(nofuse=True)
                    dve.tensor_scalar(xn[:, :], core.x[:, bass.ds(T, 1), :].rearrange("p a d -> p (a d)"),
                                      core.mean[:, bass.ds(T, 1)], core.rstd[:, bass.ds(T, 1)],
                                      ALU.subtract, ALU.mult).then_inc(s_xn, 1)

                def rank(T, h):
                    base = (T * H + h) * RANK + RANK
                    dve.wait_ge(s_sim, START + T * H + h + 1)
                    dve.nop(nofuse=True)
                    if h == 0:
                        dve.wait_ge(s_cand, START + T * CANDS)
                        dve.nop(nofuse=True)
                    sims = [sim[h % 2][:, p * NK:(p + 1) * NK] for p in range(2)]
                    for p in range(2):
                        dve.max(best[:, p, h, 0:8], sims[p]).then_inc(s_rank, 1)
                    dve.wait_ge(s_rank, START + base + 2)
                    dve.nop(nofuse=True)
                    for p in range(2):
                        dve.max_index(place[:, p, h, 0:8], best[:, p, h, 0:8], sims[p]).then_inc(s_rank, 1)
                    for p in range(2):
                        dve.match_replace(work[p][:, :], best[:, p, h, 0:8], sims[p], LOWEST).then_inc(s_rank, 1)
                    dve.wait_ge(s_rank, START + base + 6)
                    dve.nop(nofuse=True)
                    for p in range(2):
                        dve.max(best[:, p, h, 8:16], work[p][:, :]).then_inc(s_rank, 1)
                    dve.wait_ge(s_rank, START + base + 8)
                    dve.nop(nofuse=True)
                    for p in range(2):
                        dve.max_index(place[:, p, h, 8:16], best[:, p, h, 8:16], work[p][:, :]).then_inc(s_rank, 1)
                    dve.wait_ge(s_rank, START + base + 10)
                    dve.nop(nofuse=True)

                def candidates(T):
                    base = T * CANDS
                    dve.wait_ge(s_final, START + T * (H * FINAL))
                    dve.nop(nofuse=True)
                    dve.tensor_copy(place_f[:, :, :, :], place[:, :, :, :]).then_inc(s_cand, 1)
                    dve.wait_ge(s_cand, START + base + 1)
                    dve.nop(nofuse=True)
                    dve.tensor_scalar(place_f[:, 1, :, :], place_f[:, 1, :, :], float(NK), None, ALU.mult).then_inc(s_cand, 1)
                    dve.tensor_tensor(place_f[:, 0, :, :], place_f[:, 0, :, :], offset[:, :, :], ALU.add).then_inc(s_cand, 1)
                    dve.wait_ge(s_cand, START + base + 3)
                    dve.nop(nofuse=True)
                    for out, of in ((cand, best), (cand_row, place_f)):
                        first, second = of[:, 0, :, :], of[:, 1, :, :]
                        at = 0
                        for i, c in FULL:
                            dve.tensor_tensor(out[:, :, at:at + c], first[:, :, i:i + 1].to_broadcast([P, H, c]),
                                              second[:, :, 0:c], ALU.add).then_inc(s_cand, 1)
                            at += c
                        n2 = len(TWOS)
                        dve.tensor_tensor(
                            out[:, :, FULL_END:TWOS_END].rearrange("p h (i j) -> p h i j", j=2),
                            first[:, :, TWOS[0]:TWOS[0] + n2].unsqueeze(3).to_broadcast([P, H, n2, 2]),
                            second[:, :, 0:2].unsqueeze(2).to_broadcast([P, H, n2, 2]), ALU.add).then_inc(s_cand, 1)
                        dve.tensor_tensor(out[:, :, TWOS_END:CAND], first[:, :, ONES[0]:K],
                                          second[:, :, 0:1].to_broadcast([P, H, len(ONES)]), ALU.add).then_inc(s_cand, 1)
                    dve.wait_ge(s_cand, START + base + CANDS)
                    dve.nop(nofuse=True)

                def finals(T, h):
                    base = (T * H + h) * FINAL
                    if h == 0:
                        dve.wait_ge(s_wt, START + T * WEIGH)
                        dve.nop(nofuse=True)
                    dve.wait_ge(s_final, START + base)
                    dve.nop(nofuse=True)
                    dve.max(final[:, h, 0:8], cand[:, h, :]).then_inc(s_final, 1)
                    dve.wait_ge(s_final, START + base + 1)
                    dve.nop(nofuse=True)
                    dve.max_index(pos[:, 0:8], final[:, h, 0:8], cand[:, h, :]).then_inc(s_final, 1)
                    dve.match_replace(work2[:, :], final[:, h, 0:8], cand[:, h, :], LOWEST).then_inc(s_final, 1)
                    dve.wait_ge(s_final, START + base + 3)
                    dve.nop(nofuse=True)
                    dve.max(final[:, h, 8:16], work2[:, :]).then_inc(s_final, 1)
                    dve.wait_ge(s_final, START + base + 4)
                    dve.nop(nofuse=True)
                    dve.max_index(pos[:, 8:16], final[:, h, 8:16], work2[:, :]).then_inc(s_final, 1)
                    dve.wait_ge(s_final, START + base + 5)
                    dve.nop(nofuse=True)
                    dve.tensor_copy(pos_f[:, :], pos[:, :]).then_inc(s_final, 1)
                    dve.wait_ge(s_final, START + base + 6)
                    dve.nop(nofuse=True)
                    dve.tensor_tensor(same[:, :, :], places[:, :].unsqueeze(1).to_broadcast([P, K, CAND]),
                                      pos_f[:, :].unsqueeze(2).to_broadcast([P, K, CAND]), ALU.is_equal).then_inc(s_final, 1)
                    dve.wait_ge(s_final, START + base + 7)
                    dve.nop(nofuse=True)
                    dve.tensor_tensor(same[:, :, :], same[:, :, :],
                                      cand_row[:, h, :].unsqueeze(1).to_broadcast([P, K, CAND]), ALU.mult).then_inc(s_final, 1)
                    dve.wait_ge(s_final, START + base + 8)
                    dve.nop(nofuse=True)
                    dve.tensor_reduce(row_f[:, h, :], same[:, :, :], AX_X, ALU.add).then_inc(s_final, 1)

                def weigh(T, b):
                    base = T * WEIGH
                    dve.wait_ge(s_final, START + (T + 1) * (H * FINAL))
                    dve.nop(nofuse=True)
                    dve.tensor_copy(rows[b][:, :, :], row_f[:, :, :]).then_inc(s_rows, 1)
                    dve.tensor_tensor(weight[b][:, :, :], final[:, :, :], final[:, :, 0:1].to_broadcast([P, H, K]),
                                      ALU.subtract).then_inc(s_wt, 1)
                    dve.wait_ge(s_wexp, START + T + 1)
                    dve.nop(nofuse=True)
                    dve.tensor_reduce(total[:, :], weight[b][:, :, :], AX_X, ALU.add).then_inc(s_wt, 1)
                    dve.wait_ge(s_wt, START + base + 2)
                    dve.nop(nofuse=True)
                    dve.reciprocal(total[:, :], total[:, :]).then_inc(s_wt, 1)
                    dve.wait_ge(s_wt, START + base + 3)
                    dve.nop(nofuse=True)
                    dve.tensor_tensor(weight[b][:, :, :], weight[b][:, :, :],
                                      total[:, :].unsqueeze(2).to_broadcast([P, H, K]), ALU.mult).then_inc(s_wt, 2)
                    dve.wait_ge(s_wt, START + base + 5)
                    dve.nop(nofuse=True)
                    dve.wait_ge(s_rows, START + T + 1)
                    dve.nop(nofuse=True)

                def add_rows(T, b, k):
                    dve.wait_ge(s_land[k % RING], T * (ROUNDS // RING * H * 16) + (k // RING + 1) * (H * 16))
                    dve.nop(nofuse=True)
                    dve.wait_ge(s_acc, START + (T * ROUNDS + k + RING) * H)
                    dve.nop(nofuse=True)
                    if k == 0:
                        dve.wait_ge(s_v, START + T)
                        dve.nop(nofuse=True)
                    for h in range(H):
                        row, w = ring[k % RING][:, h, :], weight[b][:, h, k:k + 1]
                        if k == 0:
                            dve.tensor_scalar(kv[b][:, h, :], row, w, None, ALU.mult).then_inc(s_acc, 1)
                        else:
                            dve.scalar_tensor_tensor(out=kv[b][:, h, :], in0=row, scalar=w, in1=kv[b][:, h, :],
                                                     op0=ALU.mult, op1=ALU.add).then_inc(s_acc, 1)

                def scale_out(m, g):
                    dve.wait_ge(s_p, START + m * STEPS + g + 1)
                    dve.nop(nofuse=True)
                    dve.reciprocal(rden[:, g:g + 1], den[:, g:g + 1]).then_inc(s_rd, 1)
                    dve.wait_ge(s_rd, START + m * STEPS + g + 1)
                    dve.nop(nofuse=True)
                    dve.wait_ge(s_pv, START + m * STEPS + g + 1)
                    dve.nop(nofuse=True)
                    dve.wait_ge(s_m, START + (m * M_GRAPH + (use_o(g - 1) + 1 if g else 0)))
                    dve.nop(nofuse=True)
                    dve.tensor_scalar(o[:, :], o_bank[:, 0:D], rden[:, g:g + 1], None, ALU.mult).then_inc(s_o, 1)

                def add_out(m, h):
                    dve.wait_ge(s_out, START + m * H + h + 1)
                    dve.nop(nofuse=True)
                    dve.wait_ge(s_add, START + m * H + h)
                    dve.nop(nofuse=True)
                    xg = core.x[:, bass.ds(m * TILES, TILES), :]
                    dve.tensor_tensor(xg, out_bank[:, :].rearrange("p (t d) -> p t d", t=TILES), xg,
                                      ALU.add).then_inc(s_add, 1)

                def attend(m, t, k):
                    g = t * (STEPS // TILES) + k // 2
                    h, i = divmod(g, TILES)
                    n_cols = (i + 1) * P
                    if k % 2 == 0:
                        dve.wait_ge(s_s, START + m * STEPS + g + 1)
                        dve.nop(nofuse=True)
                        dve.tensor_reduce(ntop[:, g:g + 1], s_bank[:, 0:n_cols], AX_X, ALU.max, negate=True).then_inc(s_top, 1)
                        if g >= 1:
                            scale_out(m, g - 1)
                    else:
                        dve.wait_ge(s_pT, START + m * STEPS + g + 1)
                        dve.nop(nofuse=True)
                        dve.wait_ge(s_pv, START + m * STEPS + g)
                        dve.nop(nofuse=True)
                        dve.tensor_copy(probT[:, 0:n_cols], t_bank[:, 0:n_cols]).then_inc(s_pTc, 1)
                        if i == 1 and h >= 1:
                            add_out(m, h - 1)

                def body(n, now, attention, ahead):
                    m = n - 1
                    if attention:
                        dve.wait_ge(s_m, START + m * M_GRAPH)
                        dve.nop(nofuse=True)
                        for t in range(TILES):
                            tile = m * TILES + t
                            dve.tensor_scalar(axn[:, t, :], core.x[:, bass.ds(tile, 1), :].rearrange("p a d -> p (a d)"),
                                              core.mean[:, bass.ds(tile, 1)], core.rstd[:, bass.ds(tile, 1)],
                                              ALU.subtract, ALU.mult).then_inc(s_axn, 1)
                    for t in range(TILES):
                        T, b = n * TILES + t, t % 2
                        more = now and (ahead or t < TILES - 1)
                        for k in range(ROUNDS):
                            if more:
                                if k == 0:
                                    prepare(T + 1)
                                for h in RANK_ROUND.get(k, ()):
                                    rank(T + 1, h)
                                if k == CANDIDATE_ROUND:
                                    candidates(T + 1)
                                for h in FINAL_ROUND.get(k, ()):
                                    finals(T + 1, h)
                                if k == WEIGH_ROUND:
                                    weigh(T + 1, 1 - b)
                            if attention:
                                attend(m, t, k)
                            if now:
                                add_rows(T, b, k)
                    if attention:
                        scale_out(m, STEPS - 1)
                        add_out(m, H - 1)

                def prologue():
                    dve.sem_inc(s_acc, RING * H)
                    dve.sem_inc(s_rank, RANK)
                    prepare(0, first=True)
                    for h in range(H):
                        rank(0, h)
                    candidates(0)
                    for h in range(H):
                        finals(0, h)
                    weigh(0, 0)

                program(body)(dve, prologue)

            @block.scalar
            def _(act):
                def q_copies(use):
                    act.wait_ge(s_q, START + use + 1)
                    act.nop(nofuse=True)
                    act.activation(xnT[:, :], q_bank[:, 0:P], ACT.Copy).then_inc(s_qc, 1)
                    for half in range(2):
                        act.wait_ge(s_q, START + use + 2 + half)
                        act.nop(nofuse=True)
                        act.activation(qT[:, half * 4:half * 4 + 4, :].rearrange("p a k -> p (a k)"), q_bank[:, :],
                                       ACT.Copy).then_inc(s_qc, 1)

                def weigh_exp(T, b):
                    act.wait_ge(s_wt, START + T * WEIGH + 1)
                    act.nop(nofuse=True)
                    act.activation(weight[b][:, :, :], weight[b][:, :, :], ACT.Exp).then_inc(s_wexp, 1)

                def copy_o(m, g):
                    h, i = divmod(g, TILES)
                    act.wait_ge(s_m, START + m * M_GRAPH + use_o(g) + 1)
                    act.nop(nofuse=True)
                    if i == 0:
                        act.wait_ge(s_out, START + m * H + h)
                        act.nop(nofuse=True)
                    act.activation(oT[:, i, :], m_bank[:, 0:P], ACT.Copy).then_inc(s_mc, 1)

                def attend(m, t, k):
                    g = t * (STEPS // TILES) + k // 2
                    h, i = divmod(g, TILES)
                    n_cols = (i + 1) * P
                    if k % 2 == 0:
                        if i == 0:
                            act.wait_ge(s_m, START + m * M_GRAPH + use_q(h) + 1)
                            act.nop(nofuse=True)
                            act.wait_ge(s_s, START + m * STEPS + g)
                            act.nop(nofuse=True)
                            act.activation(qh[:, :], m_bank[:, :], ACT.Copy, scale=QSCALE).then_inc(s_mc, 1)
                        act.wait_ge(s_top, START + m * STEPS + g + 1)
                        act.nop(nofuse=True)
                        act.wait_ge(s_pT, START + m * STEPS + g)
                        act.nop(nofuse=True)
                        act.activation(prob[:, 0:n_cols], s_bank[:, 0:n_cols], ACT.Exp, bias=ntop[:, g:g + 1], scale=1.0,
                                       accum_out=den[:, g:g + 1]).then_inc(s_p, 1)
                    elif g >= 1:
                        copy_o(m, g - 1)

                def body(n, now, attention, ahead):
                    m = n - 1
                    if attention:
                        act.wait_ge(s_m, START + m * M_GRAPH + 1)
                        act.nop(nofuse=True)
                        act.activation(axnT[:, :], m_bank[:, :], ACT.Copy).then_inc(s_mc, 1)
                    for t in range(TILES):
                        T, b = n * TILES + t, t % 2
                        more = now and (ahead or t < TILES - 1)
                        for k in range(ROUNDS):
                            if more and k == 0:
                                q_copies(T * Q_TILE + 3)
                            if more and k == WEIGH_ROUND:
                                weigh_exp(T + 1, 1 - b)
                            if attention:
                                attend(m, t, k)
                        if now:
                            after = T * Q_TILE + 6
                            if t == 0:
                                act.wait_ge(s_turnover, START + n * 2)
                                act.nop(nofuse=True)
                            for half in range(2):
                                act.wait_ge(s_q, START + (after + half + 1 if more else T * Q_TILE + 3 + half + 1))
                                act.nop(nofuse=True)
                                act.activation(kT_new[:, half * 4:half * 4 + 4, t * P:(t + 1) * P],
                                               q_bank[:, :].rearrange("p (a k) -> p a k", a=4), ACT.Copy).then_inc(s_qc, 1)
                            act.wait_ge(s_acc, START + (T + 1) * (ROUNDS * H) + RING * H)
                            act.nop(nofuse=True)
                            act.activation(v_new[:, t, :, :], kv[b][:, :, D:KV], ACT.Copy).then_inc(s_v, 1)
                    if attention:
                        copy_o(m, STEPS - 1)
                    if now:
                        act.wait_ge(s_pv, START + n * STEPS)
                        act.nop(nofuse=True)
                        act.wait_ge(s_qc, START + ((n + 1) * (TILES * Q_TILE) + 3 if ahead else (n + 1) * (TILES * Q_TILE)))
                        act.nop(nofuse=True)
                        act.wait_ge(s_v, START + (n + 1) * TILES + 1)
                        act.nop(nofuse=True)
                        act.activation(kT[:, :, :], kT_new[:, :, :], ACT.Copy).then_inc(s_turnover, 1)
                        act.activation(v[:, :, :, :], v_new[:, :, :, :], ACT.Copy).then_inc(s_turnover, 1)

                def prologue():
                    act.sem_inc(s_v, 1)
                    q_copies(0)
                    weigh_exp(0, 0)

                program(body)(act, prologue)

            @block.tensor
            def _(pe):
                def q_of(T, use):
                    pe.wait_ge(s_xn, START + T + 1)
                    pe.nop(nofuse=True)
                    pe.wait_ge(s_qc, START + use)
                    pe.nop(nofuse=True)
                    pe.transpose(q_bank[:, 0:P], xn[:, :], core.ident[:, :]).then_inc(s_q, 1)
                    pe.wait_ge(s_sim, START + T * H)
                    pe.nop(nofuse=True)
                    for half in range(2):
                        pe.wait_ge(s_qc, START + use + 1 + half)
                        pe.nop(nofuse=True)
                        for a in range(4):
                            last = pe.matmul(q_bank[:, a * P:(a + 1) * P], wpk[:, half * 4 + a, :], xnT[:, :],
                                             start=True, stop=True)
                        last.then_inc(s_q, 1)

                def sims_of(T, h, use):
                    if h == 0:
                        pe.wait_ge(s_qc, START + use + 3)
                        pe.nop(nofuse=True)
                    pe.wait_ge(s_rank, START + (T * H + h) * RANK)
                    pe.nop(nofuse=True)
                    at = (h % 2) * DK
                    for p in range(2):
                        pair = p * (H // 2) + h // 2
                        last = pe.matmul(sim[h % 2][:, p * NK:(p + 1) * NK], qT[at:at + DK, pair, :],
                                         keysT[at:at + DK, pair, :], start=True, stop=True)
                    last.then_inc(s_sim, 1)

                def pv(m, g):
                    h, i = divmod(g, TILES)
                    pe.wait_ge(s_pTc, START + m * STEPS + g + 1)
                    pe.nop(nofuse=True)
                    pe.wait_ge(s_o, START + m * STEPS + g)
                    pe.nop(nofuse=True)
                    for j in range(i + 1):
                        last = pe.matmul(o_bank[:, 0:D], probT[:, j * P:(j + 1) * P], v[:, j, h, :],
                                         start=(j == 0), stop=(j == i))
                    last.then_inc(s_pv, 1)

                def turn_o(m, g):
                    pe.wait_ge(s_o, START + m * STEPS + g + 1)
                    pe.nop(nofuse=True)
                    pe.wait_ge(s_mc, START + m * M_GRAPH + use_o(g))
                    pe.nop(nofuse=True)
                    pe.transpose(m_bank[:, 0:P], o[:, :], core.ident[:, :]).then_inc(s_m, 1)

                def out_of(m, h):
                    pe.wait_ge(s_mc, START + m * M_GRAPH + use_o(TILES * h + TILES - 1) + 1)
                    pe.nop(nofuse=True)
                    pe.wait_ge(s_add, START + m * H + h)
                    pe.nop(nofuse=True)
                    for i in range(TILES):
                        last = pe.matmul(out_bank[:, i * P:(i + 1) * P], oT[:, i, :], wo[:, h, :], start=True, stop=True)
                    last.then_inc(s_out, 1)

                def attend(m, t, k):
                    g = t * (STEPS // TILES) + k // 2
                    h, i = divmod(g, TILES)
                    if k % 2 == 0:
                        if i == 0:
                            pe.wait_ge(s_mc, START + m * M_GRAPH + use_q(h))
                            pe.nop(nofuse=True)
                            pe.matmul(m_bank[:, :], wq[:, h, :], axnT[:, :], start=True, stop=True).then_inc(s_m, 1)
                            pe.wait_ge(s_mc, START + m * M_GRAPH + use_q(h) + 1)
                            pe.nop(nofuse=True)
                        if i == 1 and h >= 1:
                            out_of(m, h - 1)
                        pe.wait_ge(s_p, START + m * STEPS + g)
                        pe.nop(nofuse=True)
                        q = qh[:, i * P:(i + 1) * P]
                        if i:
                            pe.matmul(s_bank[:, 0:i * P], q, kT[:, h, 0:i * P], start=True, stop=True)
                        here = s_bank[:, i * P:(i + 1) * P]
                        pe.matmul(here, q, kT[:, h, i * P:(i + 1) * P], start=True, stop=False)
                        pe.matmul(here, core.ident_bf[:, :], tri[:, :], start=False, stop=True).then_inc(s_s, 1)
                        if g >= 1:
                            pv(m, g - 1)
                    else:
                        pe.wait_ge(s_p, START + m * STEPS + g + 1)
                        pe.nop(nofuse=True)
                        pe.wait_ge(s_pTc, START + m * STEPS + g)
                        pe.nop(nofuse=True)
                        for j in range(i + 1):
                            last = pe.transpose(t_bank[:, j * P:(j + 1) * P], prob[:, j * P:(j + 1) * P], core.ident[:, :])
                        last.then_inc(s_pT, 1)
                        if g >= 1:
                            turn_o(m, g - 1)

                def body(n, now, attention, ahead):
                    m = n - 1
                    if attention:
                        pe.wait_ge(s_axn, START + (m + 1) * TILES)
                        pe.nop(nofuse=True)
                        pe.wait_ge(s_mc, START + m * M_GRAPH)
                        pe.nop(nofuse=True)
                        for t in range(TILES):
                            last = pe.transpose(m_bank[:, t * P:(t + 1) * P], axn[:, t, :], core.ident[:, :])
                        last.then_inc(s_m, 1)
                        pe.wait_ge(s_turnover, START + n * 2)
                        pe.nop(nofuse=True)
                    for t in range(TILES):
                        T, b = n * TILES + t, t % 2
                        more = now and (ahead or t < TILES - 1)
                        use = T * Q_TILE + 3
                        for k in range(ROUNDS):
                            if more:
                                if k == 0:
                                    q_of(T + 1, use)
                                for h in RANK_ROUND.get(k, ()):
                                    sims_of(T + 1, h, use)
                            if attention:
                                attend(m, t, k)
                        if now:
                            after = T * Q_TILE + 6 if more else use
                            pe.wait_ge(s_acc, START + (T + 1) * (ROUNDS * H) + RING * H)
                            pe.nop(nofuse=True)
                            for half in range(2):
                                pe.wait_ge(s_qc, START + after + half)
                                pe.nop(nofuse=True)
                                for a in range(4):
                                    last = pe.transpose(q_bank[:, a * P:(a + 1) * P], kv[b][:, half * 4 + a, 0:D],
                                                        core.ident[:, :])
                                last.then_inc(s_q, 1)
                    if attention:
                        pv(m, STEPS - 1)
                        turn_o(m, STEPS - 1)
                        out_of(m, H - 1)

                def prologue():
                    q_of(0, 0)
                    for h in range(H):
                        sims_of(0, h, 0)

                program(body)(pe, prologue)


def build_program(nc, io):
    with ExitStack() as ctx:
        core = Core(nc, ctx)
        with core.stage():
            load_and_constants(core, io["x"])
        with core.stage():
            attention_layer(core, io["adj"], io["head_scale"], io["gain1"], io["shift1"], io["gain2"], io["shift2"],
                            io["mlp_w1"], io["mlp_b1"], io["mlp_w2"], io["mlp_b2"], heads=8)
        with core.stage():
            edge_routed_experts(core, io["edges"], io["w_gat"], io["att"], io["post"], io["moe_w1"], io["moe_b1"],
                                io["moe_w2"], io["moe_b2"], 4, (io["source_table"], io["target_table"]))
        with core.stage():
            row_statistics(core, core.x)
            graph_layer(core, "g1", io["adj"], io["g1_w"], io["g1_row"], io["g1_col"], slope=0.2, over_rows=True,
                        elu=True, keep_neg=True)
        with core.stage():
            tropical_layer(core, io["wt"], io["trop_cols"], io["sl_cvx"], io["of_cvx"], io["sl_ccv"], io["of_ccv"],
                           io["wc"], io["wg"], io["wd"], io["bd"])
        with core.stage():
            row_statistics(core, core.x)
            graph_layer(core, "g2", io["adj"], io["g2_w"], io["g2_row"], io["g2_col"], slope=0.0, over_rows=False,
                        elu=True, keep_neg=True)
        with core.stage():
            routed_experts(core, io["router_w1"], io["router_b1"], io["router_w2"], io["router_b2"], io["experts_w"],
                           io["experts_b12"], io["experts_b3"], 6)
        with core.stage():
            row_statistics(core, core.x)
            graph_layer(core, "g3", io["adj"], io["g3_w"], io["g3_row"], io["g3_col"], slope=0.2, over_rows=False,
                        elu=False, keep_neg=False)
        with core.stage():
            memory_attention(core, io["wpk"], io["pk_keys"], io["wq"], io["wo"], io["causal"], io["table"],
                             heads=8, top=16)
        with core.stage():
            store_result(core, io["out"])


def lay_out(i):
    import numpy as np

    heads, head_dim, chunks = 8, 16, 4

    def repeated(a):
        return np.broadcast_to(a, (P,) + a.shape)

    def chunked(a):
        return a.reshape(chunks, P, -1).transpose(1, 0, 2)

    def columns(a):
        return np.repeat(a.reshape(P, 1), P, 1)

    head_scale = np.zeros((P, heads), np.float32)
    head_scale[np.arange(P), np.arange(P) // head_dim] = head_dim ** -0.5
    causal = np.where(np.arange(P)[None, :] > np.arange(P)[:, None], MINUS_BIG, 0.0).astype(np.float32)
    a1, a2 = i["L1_gnn_a"], i["L2_gnn_a"]
    return {
        "x": i["x"], "adj": i["adj"], "head_scale": head_scale,
        "gain1": repeated(i["L0_gnn_gamma1"]), "shift1": repeated(i["L0_gnn_beta1"]),
        "gain2": i["L0_gnn_gamma2"][:, None], "shift2": i["L0_gnn_beta2"][:, None],
        "mlp_w1": i["L0_gnn_W1"].reshape(P, 1, chunks, P), "mlp_b1": i["L0_gnn_b1"].reshape(1, chunks, P).transpose(2, 0, 1),
        "mlp_w2": i["L0_gnn_W2"].reshape(1, chunks, P, D).transpose(2, 0, 1, 3), "mlp_b2": i["L0_gnn_b2"].reshape(1, 1, D),
        "edges": i["L0_ffn_edge_index"].reshape(2, P, -1), "w_gat": i["L0_ffn_W_gat"],
        "att": repeated(np.stack([i["L0_ffn_att_src"].ravel(), i["L0_ffn_att_dst"].ravel()])),
        "post": repeated(np.stack([i["L0_ffn_b_gat"], i["L0_ffn_ln_gamma"], i["L0_ffn_ln_beta"]])),
        "moe_w1": i["L0_ffn_W1"].reshape(4, P, 2, P).transpose(1, 0, 2, 3),
        "moe_b1": i["L0_ffn_b1"].reshape(4, 2, P).transpose(2, 0, 1),
        "moe_w2": i["L0_ffn_W2"].reshape(4, 2, P, D).transpose(2, 0, 1, 3), "moe_b2": i["L0_ffn_b2"][None],
        "g1_w": i["L1_gnn_W"], "g1_row": columns(a1[:P]), "g1_col": a1[P:],
        "g2_w": i["L2_gnn_W"], "g2_row": columns(a2[P:]), "g2_col": a2[:P],
        "g3_w": i["L3_gnn_W"], "g3_row": columns(i["L3_gnn_a_dst"]), "g3_col": i["L3_gnn_a_src"][:, None],
        "wt": chunked(i["L1_ffn_Wt"]),
        "trop_cols": np.stack([i["L1_ffn_" + k] for k in ("bt", "alpha", "bc", "bg")]).reshape(4, chunks, P).transpose(2, 0, 1),
        "sl_cvx": chunked(i["L1_ffn_sl_cvx"]), "of_cvx": chunked(i["L1_ffn_of_cvx"]),
        "sl_ccv": chunked(i["L1_ffn_sl_ccv"]), "of_ccv": chunked(i["L1_ffn_of_ccv"]),
        "wc": i["L1_ffn_Wc"].reshape(P, chunks, P), "wg": i["L1_ffn_Wg"].reshape(P, chunks, P),
        "wd": chunked(i["L1_ffn_Wd"]), "bd": i["L1_ffn_bd"][None],
        "router_w1": i["L2_ffn_router_w1"], "router_b1": i["L2_ffn_router_b1"][:, None],
        "router_w2": i["L2_ffn_router_w2"], "router_b2": i["L2_ffn_router_b2"][None],
        "experts_w": np.stack([i["L2_ffn_expert_w1"], i["L2_ffn_expert_w2"], i["L2_ffn_expert_w3"]]).transpose(2, 0, 1, 3),
        "experts_b12": np.stack([i["L2_ffn_expert_b1"], i["L2_ffn_expert_b2"]]).transpose(2, 0, 1),
        "experts_b3": i["L2_ffn_expert_b3"][None],
        "wpk": i["L3_ffn_Wq_pk"].reshape(P, heads, P),
        "pk_keys": i["L3_ffn_pk_keys"].transpose(1, 0, 2, 3).reshape(P, 2, -1),
        "wq": i["L3_ffn_Wq"].reshape(P, heads, D), "wo": i["L3_ffn_Wo"].reshape(heads, D, D).transpose(1, 0, 2),
        "causal": causal, "table": np.concatenate([i["L3_ffn_keys_table"], i["L3_ffn_values_table"]], 1),
    }


def kernel(**inputs):
    import numpy as np
    import concourse.bacc as bacc
    from concourse.bass_utils import run_bass_kernel_spmd

    nc = bacc.Bacc("TRN2", target_bir_lowering=False, num_devices=1)
    arrays, io = {}, {}
    for name, a in lay_out({k: np.asarray(v) for k, v in inputs.items()}).items():
        a = np.ascontiguousarray(a)
        arrays[f"in_{name}"] = a
        io[name] = nc.dram_tensor(f"in_{name}", a.shape, mybir.dt.from_np(a.dtype), kind="ExternalInput").ap()
    io["source_table"] = nc.dram_tensor("source_table", (TOKENS, 20), F32, kind="Internal").ap()
    io["target_table"] = nc.dram_tensor("target_table", (TOKENS, 8), F32, kind="Internal").ap()
    io["out"] = nc.dram_tensor("out", (GRAPHS, NODES, D), F32, kind="ExternalOutput").ap()
    build_program(nc, io)
    return run_bass_kernel_spmd(nc, [arrays], core_ids=[0]).results[0]["out"]
```
